# Optimizing a Trainium2 kernel written in Bass

```python
import numpy as np
import jax
import jax.numpy as jnp

def _softmax(x, axis=-1):
    return jax.nn.softmax(x, axis=axis)

def _gelu(x):
    return jax.nn.gelu(x, approximate=True)

def _silu(x):
    return jax.nn.silu(x)

def _sigmoid(x):
    return jax.nn.sigmoid(x)

def _layernorm(x, axis=-1, eps=1e-05):
    m = jnp.mean(x, axis=axis, keepdims=True)
    v = jnp.var(x, axis=axis, keepdims=True)
    return (x - m) / jnp.sqrt(v + eps)

def _scatter_add(tgt, idx, src, axis=0):
    return tgt.at[idx].add(src)

def _segment_sum(src, seg, n):
    return jax.ops.segment_sum(src, seg, n)
kernel_name = 'mk_xattn_seq_d4_seqx_r8_eaa814'

def setup_inputs(seed: int=0):
    np.random.seed(seed)
    _w = jnp.asarray

    def _rec_inputs():
        import jax
        import jax.numpy as jnp
        _rk = jax.random.key(seed)
        x = -0.0002928 + 1 * jax.random.normal(jax.random.fold_in(_rk, 1), (16, 64, 128), jnp.float32)
        _lenS = 64 - jax.random.randint(jax.random.fold_in(_rk, 7), (16,), 0, max(1, 64 // 4) + 1, jnp.int32)
        _lenS2 = 64 - jax.random.randint(jax.random.fold_in(_rk, 8), (16,), 0, max(1, 64 // 4) + 1, jnp.int32)
        _ctx_1024P = jax.random.normal(jax.random.fold_in(_rk, 11), (16, 16, 128), jnp.float32)
        _ctx_1024c = jax.random.dirichlet(jax.random.fold_in(_rk, 511), 0.3 * jnp.ones((16,), jnp.float32), (16, 64))
        _ctx_1024t = jnp.einsum('bsk,bkd->bsd', _ctx_1024c, _ctx_1024P)
        _ctx_1024t = _ctx_1024t * jax.lax.rsqrt(jnp.mean(jnp.square(_ctx_1024t)) + 1e-12) * 0.953939
        ctx_1024 = -1.39393e-06 + 0.999914 * (_ctx_1024t + 0.3 * jax.random.normal(jax.random.fold_in(_rk, 611), (16, 64, 128), jnp.float32))
        return (x, ctx_1024)
    x, ctx_1024 = _rec_inputs()

    def _L0_xattn_setup():
        import jax, jax.numpy as jnp
        import numpy as np
        B, LX, LY = (2, 256, 256)
        E, H = (128, 16)
        HD = E // H
        FF = 512
        EPS = 1e-05

        def _rope_tables(L, d):
            inv = 1.0 / 10000.0 ** (jnp.arange(0, d, 2, dtype=jnp.float32) / d)
            t = jnp.arange(L, dtype=jnp.float32)
            f = jnp.outer(t, inv)
            return (jnp.cos(f), jnp.sin(f))

        def _apply_rope(x, cos, sin):
            d2 = x.shape[-1] // 2
            x1, x2 = (x[..., :d2], x[..., d2:])
            c = cos[None, :, None, :]
            s = sin[None, :, None, :]
            return jnp.concatenate([x1 * c - x2 * s, x2 * c + x1 * s], axis=-1)

        def _ln(x, g, b):
            m = jnp.mean(x, axis=-1, keepdims=True)
            v = jnp.var(x, axis=-1, keepdims=True)
            return (x - m) / jnp.sqrt(v + EPS) * g + b

        def _attn(q, k, v, causal):
            s = jnp.einsum('blhd,bmhd->bhlm', q, k)
            if causal:
                Lq, Lk = (s.shape[2], s.shape[3])
                mask = jnp.tril(jnp.ones((Lq, Lk), dtype=bool))
                s = jnp.where(mask, s, -jnp.inf)
            p = jax.nn.softmax(s, axis=-1)
            return jnp.einsum('bhlm,bmhd->blhd', p, v)

        def _forward(x, y, ln1_g, ln1_b, sa_wq, sa_bq, sa_wk, sa_bk, sa_wv, sa_bv, sa_wo, sa_bo, ln2_g, ln2_b, ca_wq, ca_bq, ca_wk, ca_bk, ca_wv, ca_bv, ca_wo, ca_bo, ln3_g, ln3_b, fc1_w, fc1_b, fc2_w, fc2_b):
            Bx, Lx, _ = x.shape
            Ly = y.shape[1]
            cos, sin = _rope_tables(max(Lx, Ly), HD)
            scale = HD ** (-0.5)
            h = _ln(x, ln1_g, ln1_b)
            q = (h @ sa_wq + sa_bq).reshape(Bx, Lx, H, HD) * scale
            k = (h @ sa_wk + sa_bk).reshape(Bx, Lx, H, HD)
            v = (h @ sa_wv + sa_bv).reshape(Bx, Lx, H, HD)
            q = _apply_rope(q, cos[:Lx], sin[:Lx])
            k = _apply_rope(k, cos[:Lx], sin[:Lx])
            a = _attn(q, k, v, causal=True).reshape(Bx, Lx, E)
            x = x + (a @ sa_wo + sa_bo)
            h = _ln(x, ln2_g, ln2_b)
            q = (h @ ca_wq + ca_bq).reshape(Bx, Lx, H, HD) * scale
            k = (y @ ca_wk + ca_bk).reshape(Bx, Ly, H, HD)
            v = (y @ ca_wv + ca_bv).reshape(Bx, Ly, H, HD)
            q = _apply_rope(q, cos[:Lx], sin[:Lx])
            k = _apply_rope(k, cos[:Ly], sin[:Ly])
            a = _attn(q, k, v, causal=False).reshape(Bx, Lx, E)
            x = x + (a @ ca_wo + ca_bo)
            h = _ln(x, ln3_g, ln3_b)
            return x + (jax.nn.gelu(h @ fc1_w + fc1_b) @ fc2_w + fc2_b)
        key = jax.random.key(seed)
        ks = jax.random.split(key, 16)

        def w(k, *s):
            return jax.random.normal(k, s, jnp.float32) * 0.02
        z = lambda *s: jnp.zeros(s, jnp.float32)
        o = lambda *s: jnp.ones(s, jnp.float32)
        return {'x': jax.random.normal(ks[0], (B, LX, E), jnp.float32), 'y': jax.random.normal(ks[1], (B, LY, E), jnp.float32), 'ln1_g': o(E), 'ln1_b': z(E), 'sa_wq': w(ks[2], E, E), 'sa_bq': z(E), 'sa_wk': w(ks[3], E, E), 'sa_bk': z(E), 'sa_wv': w(ks[4], E, E), 'sa_bv': z(E), 'sa_wo': w(ks[5], E, E), 'sa_bo': z(E), 'ln2_g': o(E), 'ln2_b': z(E), 'ca_wq': w(ks[6], E, E), 'ca_bq': z(E), 'ca_wk': w(ks[7], E, E), 'ca_bk': z(E), 'ca_wv': w(ks[8], E, E), 'ca_bv': z(E), 'ca_wo': w(ks[9], E, E), 'ca_bo': z(E), 'ln3_g': o(E), 'ln3_b': z(E), 'fc1_w': w(ks[10], E, FF), 'fc1_b': z(FF), 'fc2_w': w(ks[11], FF, E), 'fc2_b': z(E)}
    _L0_xattn_all = _L0_xattn_setup()
    _L0_xattn_in = {k: v for k, v in _L0_xattn_all.items() if k in ('ln1_g', 'ln1_b', 'sa_wq', 'sa_bq', 'sa_wk', 'sa_bk', 'sa_wv', 'sa_bv', 'sa_wo', 'sa_bo', 'ln2_g', 'ln2_b', 'ca_wq', 'ca_bq', 'ca_wk', 'ca_bk', 'ca_wv', 'ca_bv', 'ca_wo', 'ca_bo', 'ln3_g', 'ln3_b', 'fc1_w', 'fc1_b', 'fc2_w', 'fc2_b')}
    del _L0_xattn_all

    def _L1_xattn_setup():
        import jax, jax.numpy as jnp
        import numpy as np
        D = 128
        H = 16
        HD = D // H
        DFF = 4 * D
        LN_EPS = 1e-05

        def layernorm(x, gamma, beta):
            mu = jnp.mean(x, axis=-1, keepdims=True)
            var = jnp.mean(jnp.square(x - mu), axis=-1, keepdims=True)
            return (x - mu) * jax.lax.rsqrt(var + LN_EPS) * gamma + beta
        key = jax.random.key(seed)
        ks = jax.random.split(key, 10)
        B, Nq, Nk = (2, 256, 256)
        s = 0.02
        return {'q_x': jax.random.normal(ks[0], (B, Nq, D), jnp.float32), 'kv_x': jax.random.normal(ks[1], (B, Nk, D), jnp.float32), 'Wq': jax.random.normal(ks[2], (D, D), jnp.float32) * s, 'Wkv': jax.random.normal(ks[3], (2 * D, D), jnp.float32) * s, 'Wo': jax.random.normal(ks[4], (D, D), jnp.float32) * s, 'bo': jnp.zeros((D,), jnp.float32), 'ln_q_g': jnp.ones((D,), jnp.float32), 'ln_q_b': jnp.zeros((D,), jnp.float32), 'ln_kv_g': jnp.ones((D,), jnp.float32), 'ln_kv_b': jnp.zeros((D,), jnp.float32), 'W1': jax.random.normal(ks[5], (DFF, D), jnp.float32) * s, 'b1': jnp.zeros((DFF,), jnp.float32), 'W2': jax.random.normal(ks[6], (D, DFF), jnp.float32) * s, 'b2': jnp.zeros((D,), jnp.float32)}
    _L1_xattn_all = _L1_xattn_setup()
    _L1_xattn_in = {k: v for k, v in _L1_xattn_all.items() if k in ('Wq', 'Wkv', 'Wo', 'bo', 'ln_q_g', 'ln_q_b', 'ln_kv_g', 'ln_kv_b', 'W1', 'b1', 'W2', 'b2')}
    del _L1_xattn_all

    def _L2_xattn_setup():
        import jax, jax.numpy as jnp
        import numpy as np
        TOPK = 10
        NUM_HEADS = 16
        key = jax.random.key(seed)
        ks = jax.random.split(key, 8)
        B, N, S, D = (32, 256, 256, 128)
        sc = 1.0 / np.sqrt(D)
        return {'base_hidden': jax.random.normal(ks[0], (B, N, D), jnp.float32), 'scaffold_hidden': jax.random.normal(ks[1], (B, S, D), jnp.float32), 'in_proj_w': jax.random.normal(ks[2], (3 * D, D), jnp.float32) * sc, 'in_proj_b': jax.random.normal(ks[3], (3 * D,), jnp.float32) * 0.02, 'out_w': jax.random.normal(ks[4], (D, D), jnp.float32) * sc, 'out_b': jax.random.normal(ks[5], (D,), jnp.float32) * 0.02, 'score_w': jax.random.normal(ks[6], (1, D), jnp.float32) * sc, 'score_b': jax.random.normal(ks[7], (1,), jnp.float32) * 0.02}
    _L2_xattn_all = _L2_xattn_setup()
    _L2_xattn_in = {k: v for k, v in _L2_xattn_all.items() if k in ('in_proj_w', 'in_proj_b', 'out_w', 'out_b', 'score_w', 'score_b')}
    del _L2_xattn_all

    def _L3_xattn_setup():
        import jax, jax.numpy as jnp
        import numpy as np
        D, H, E, K, DFF = (128, 16, 8, 2, 512)
        B, L, T = (4, 64, 256)
        EPS = 1e-05

        def _xavier(key, shape):
            fan_in, fan_out = (shape[-1], shape[-2])
            a = jnp.sqrt(6.0 / (fan_in + fan_out))
            return jax.random.uniform(key, shape, jnp.float32, -a, a)

        def _ln(x, g, b):
            m = x.mean(-1, keepdims=True)
            v = ((x - m) ** 2).mean(-1, keepdims=True)
            return (x - m) / jnp.sqrt(v + EPS) * g + b

        def _mha(q_in, kv_in, in_w, in_b, out_w, out_b):
            wq, wk, wv = jnp.split(in_w, 3, axis=0)
            bq, bk, bv = jnp.split(in_b, 3, axis=0)
            dh = D // H

            def heads(x, w, b):
                y = x @ w.T + b
                return y.reshape(x.shape[0], x.shape[1], H, dh).transpose(0, 2, 1, 3)
            q = heads(q_in, wq, bq)
            k = heads(kv_in, wk, bk)
            v = heads(kv_in, wv, bv)
            scores = jnp.einsum('bhqd,bhkd->bhqk', q, k) / jnp.sqrt(jnp.float32(dh))
            attn = jax.nn.softmax(scores, axis=-1)
            out = jnp.einsum('bhqk,bhkd->bhqd', attn, v)
            out = out.transpose(0, 2, 1, 3).reshape(q_in.shape[0], q_in.shape[1], D)
            return out @ out_w.T + out_b

        def _fuse_moe(x, ln_g, ln_b, rw, rb, fc1_w, fc1_b, fc2_w, fc2_b):
            h = _ln(x, ln_g, ln_b)
            logits = h @ rw.T + rb
            vals, idx = jax.lax.top_k(logits, K)
            gates = jax.nn.softmax(vals, axis=-1)
            N = x.shape[0] * x.shape[1]
            hf = h.reshape(N, D)
            h1 = jax.nn.gelu(jnp.einsum('nd,efd->enf', hf, fc1_w) + fc1_b[:, None, :], approximate=False)
            eo = jnp.einsum('enf,edf->end', h1, fc2_w) + fc2_b[:, None, :]
            idx_f = idx.reshape(N, K)
            gates_f = gates.reshape(N, K)
            gathered = eo[idx_f, jnp.arange(N)[:, None], :]
            mixed = (gathered * gates_f[..., None]).sum(axis=1).reshape(x.shape)
            return x + mixed
        key = jax.random.key(seed)
        ks = jax.random.split(key, 16)
        inp = {'latents': jax.random.normal(ks[0], (B, L, D), jnp.float32), 'tokens': jax.random.normal(ks[1], (B, T, D), jnp.float32), 'sa_ln_g': jnp.ones((D,)), 'sa_ln_b': jnp.zeros((D,)), 'sa_in_w': _xavier(ks[2], (3 * D, D)), 'sa_in_b': jnp.zeros((3 * D,)), 'sa_out_w': _xavier(ks[3], (D, D)), 'sa_out_b': jnp.zeros((D,)), 'ca_q_ln_g': jnp.ones((D,)), 'ca_q_ln_b': jnp.zeros((D,)), 'ca_kv_ln_g': jnp.ones((D,)), 'ca_kv_ln_b': jnp.zeros((D,)), 'ca_in_w': _xavier(ks[4], (3 * D, D)), 'ca_in_b': jnp.zeros((3 * D,)), 'ca_out_w': _xavier(ks[5], (D, D)), 'ca_out_b': jnp.zeros((D,)), 'moe_ln_g': jnp.ones((D,)), 'moe_ln_b': jnp.zeros((D,)), 'router_w': _xavier(ks[6], (E, D)), 'router_b': jnp.zeros((E,)), 'e_fc1_w': jax.vmap(lambda k: _xavier(k, (DFF, D)))(jax.random.split(ks[7], E)), 'e_fc1_b': jnp.zeros((E, DFF)), 'e_fc2_w': jax.vmap(lambda k: _xavier(k, (D, DFF)))(jax.random.split(ks[8], E)), 'e_fc2_b': jnp.zeros((E, D))}
        return inp
    _L3_xattn_all = _L3_xattn_setup()
    _L3_xattn_in = {k: v for k, v in _L3_xattn_all.items() if k in ('sa_ln_g', 'sa_ln_b', 'sa_in_w', 'sa_in_b', 'sa_out_w', 'sa_out_b', 'ca_q_ln_g', 'ca_q_ln_b', 'ca_kv_ln_g', 'ca_kv_ln_b', 'ca_in_w', 'ca_in_b', 'ca_out_w', 'ca_out_b', 'moe_ln_g', 'moe_ln_b', 'router_w', 'router_b', 'e_fc1_w', 'e_fc1_b', 'e_fc2_w', 'e_fc2_b')}
    del _L3_xattn_all
    return {'x': x, 'ctx_1024': ctx_1024, 'L0_xattn_ln1_g': _L0_xattn_in['ln1_g'], 'L0_xattn_ln1_b': _L0_xattn_in['ln1_b'], 'L0_xattn_sa_wq': _L0_xattn_in['sa_wq'], 'L0_xattn_sa_bq': _L0_xattn_in['sa_bq'], 'L0_xattn_sa_wk': _L0_xattn_in['sa_wk'], 'L0_xattn_sa_bk': _L0_xattn_in['sa_bk'], 'L0_xattn_sa_wv': _L0_xattn_in['sa_wv'], 'L0_xattn_sa_bv': _L0_xattn_in['sa_bv'], 'L0_xattn_sa_wo': _L0_xattn_in['sa_wo'], 'L0_xattn_sa_bo': _L0_xattn_in['sa_bo'], 'L0_xattn_ln2_g': _L0_xattn_in['ln2_g'], 'L0_xattn_ln2_b': _L0_xattn_in['ln2_b'], 'L0_xattn_ca_wq': _L0_xattn_in['ca_wq'], 'L0_xattn_ca_bq': _L0_xattn_in['ca_bq'], 'L0_xattn_ca_wk': _L0_xattn_in['ca_wk'], 'L0_xattn_ca_bk': _L0_xattn_in['ca_bk'], 'L0_xattn_ca_wv': _L0_xattn_in['ca_wv'], 'L0_xattn_ca_bv': _L0_xattn_in['ca_bv'], 'L0_xattn_ca_wo': _L0_xattn_in['ca_wo'], 'L0_xattn_ca_bo': _L0_xattn_in['ca_bo'], 'L0_xattn_ln3_g': _L0_xattn_in['ln3_g'], 'L0_xattn_ln3_b': _L0_xattn_in['ln3_b'], 'L0_xattn_fc1_w': _L0_xattn_in['fc1_w'], 'L0_xattn_fc1_b': _L0_xattn_in['fc1_b'], 'L0_xattn_fc2_w': _L0_xattn_in['fc2_w'], 'L0_xattn_fc2_b': _L0_xattn_in['fc2_b'], 'L1_xattn_Wq': _L1_xattn_in['Wq'], 'L1_xattn_Wkv': _L1_xattn_in['Wkv'], 'L1_xattn_Wo': _L1_xattn_in['Wo'], 'L1_xattn_bo': _L1_xattn_in['bo'], 'L1_xattn_ln_q_g': _L1_xattn_in['ln_q_g'], 'L1_xattn_ln_q_b': _L1_xattn_in['ln_q_b'], 'L1_xattn_ln_kv_g': _L1_xattn_in['ln_kv_g'], 'L1_xattn_ln_kv_b': _L1_xattn_in['ln_kv_b'], 'L1_xattn_W1': _L1_xattn_in['W1'], 'L1_xattn_b1': _L1_xattn_in['b1'], 'L1_xattn_W2': _L1_xattn_in['W2'], 'L1_xattn_b2': _L1_xattn_in['b2'], 'L2_xattn_in_proj_w': _L2_xattn_in['in_proj_w'], 'L2_xattn_in_proj_b': _L2_xattn_in['in_proj_b'], 'L2_xattn_out_w': _L2_xattn_in['out_w'], 'L2_xattn_out_b': _L2_xattn_in['out_b'], 'L2_xattn_score_w': _L2_xattn_in['score_w'], 'L2_xattn_score_b': _L2_xattn_in['score_b'], 'L3_xattn_sa_ln_g': _L3_xattn_in['sa_ln_g'], 'L3_xattn_sa_ln_b': _L3_xattn_in['sa_ln_b'], 'L3_xattn_sa_in_w': _L3_xattn_in['sa_in_w'], 'L3_xattn_sa_in_b': _L3_xattn_in['sa_in_b'], 'L3_xattn_sa_out_w': _L3_xattn_in['sa_out_w'], 'L3_xattn_sa_out_b': _L3_xattn_in['sa_out_b'], 'L3_xattn_ca_q_ln_g': _L3_xattn_in['ca_q_ln_g'], 'L3_xattn_ca_q_ln_b': _L3_xattn_in['ca_q_ln_b'], 'L3_xattn_ca_kv_ln_g': _L3_xattn_in['ca_kv_ln_g'], 'L3_xattn_ca_kv_ln_b': _L3_xattn_in['ca_kv_ln_b'], 'L3_xattn_ca_in_w': _L3_xattn_in['ca_in_w'], 'L3_xattn_ca_in_b': _L3_xattn_in['ca_in_b'], 'L3_xattn_ca_out_w': _L3_xattn_in['ca_out_w'], 'L3_xattn_ca_out_b': _L3_xattn_in['ca_out_b'], 'L3_xattn_moe_ln_g': _L3_xattn_in['moe_ln_g'], 'L3_xattn_moe_ln_b': _L3_xattn_in['moe_ln_b'], 'L3_xattn_router_w': _L3_xattn_in['router_w'], 'L3_xattn_router_b': _L3_xattn_in['router_b'], 'L3_xattn_e_fc1_w': _L3_xattn_in['e_fc1_w'], 'L3_xattn_e_fc1_b': _L3_xattn_in['e_fc1_b'], 'L3_xattn_e_fc2_w': _L3_xattn_in['e_fc2_w'], 'L3_xattn_e_fc2_b': _L3_xattn_in['e_fc2_b']}

def reference(x, ctx_1024, L0_xattn_ln1_g, L0_xattn_ln1_b, L0_xattn_sa_wq, L0_xattn_sa_bq, L0_xattn_sa_wk, L0_xattn_sa_bk, L0_xattn_sa_wv, L0_xattn_sa_bv, L0_xattn_sa_wo, L0_xattn_sa_bo, L0_xattn_ln2_g, L0_xattn_ln2_b, L0_xattn_ca_wq, L0_xattn_ca_bq, L0_xattn_ca_wk, L0_xattn_ca_bk, L0_xattn_ca_wv, L0_xattn_ca_bv, L0_xattn_ca_wo, L0_xattn_ca_bo, L0_xattn_ln3_g, L0_xattn_ln3_b, L0_xattn_fc1_w, L0_xattn_fc1_b, L0_xattn_fc2_w, L0_xattn_fc2_b, L1_xattn_Wq, L1_xattn_Wkv, L1_xattn_Wo, L1_xattn_bo, L1_xattn_ln_q_g, L1_xattn_ln_q_b, L1_xattn_ln_kv_g, L1_xattn_ln_kv_b, L1_xattn_W1, L1_xattn_b1, L1_xattn_W2, L1_xattn_b2, L2_xattn_in_proj_w, L2_xattn_in_proj_b, L2_xattn_out_w, L2_xattn_out_b, L2_xattn_score_w, L2_xattn_score_b, L3_xattn_sa_ln_g, L3_xattn_sa_ln_b, L3_xattn_sa_in_w, L3_xattn_sa_in_b, L3_xattn_sa_out_w, L3_xattn_sa_out_b, L3_xattn_ca_q_ln_g, L3_xattn_ca_q_ln_b, L3_xattn_ca_kv_ln_g, L3_xattn_ca_kv_ln_b, L3_xattn_ca_in_w, L3_xattn_ca_in_b, L3_xattn_ca_out_w, L3_xattn_ca_out_b, L3_xattn_moe_ln_g, L3_xattn_moe_ln_b, L3_xattn_router_w, L3_xattn_router_b, L3_xattn_e_fc1_w, L3_xattn_e_fc1_b, L3_xattn_e_fc2_w, L3_xattn_e_fc2_b):
    import jax
    import jax.numpy as jnp

    def _L0_xattn_ref(x, y, ln1_g, ln1_b, sa_wq, sa_bq, sa_wk, sa_bk, sa_wv, sa_bv, sa_wo, sa_bo, ln2_g, ln2_b, ca_wq, ca_bq, ca_wk, ca_bk, ca_wv, ca_bv, ca_wo, ca_bo, ln3_g, ln3_b, fc1_w, fc1_b, fc2_w, fc2_b):
        import jax, jax.numpy as jnp
        import numpy as np
        B, LX, LY = (2, 256, 256)
        E, H = (128, 16)
        HD = E // H
        FF = 512
        EPS = 1e-05

        def _rope_tables(L, d):
            inv = 1.0 / 10000.0 ** (jnp.arange(0, d, 2, dtype=jnp.float32) / d)
            t = jnp.arange(L, dtype=jnp.float32)
            f = jnp.outer(t, inv)
            return (jnp.cos(f), jnp.sin(f))

        def _apply_rope(x, cos, sin):
            d2 = x.shape[-1] // 2
            x1, x2 = (x[..., :d2], x[..., d2:])
            c = cos[None, :, None, :]
            s = sin[None, :, None, :]
            return jnp.concatenate([x1 * c - x2 * s, x2 * c + x1 * s], axis=-1)

        def _ln(x, g, b):
            m = jnp.mean(x, axis=-1, keepdims=True)
            v = jnp.var(x, axis=-1, keepdims=True)
            return (x - m) / jnp.sqrt(v + EPS) * g + b

        def _attn(q, k, v, causal):
            s = jnp.einsum('blhd,bmhd->bhlm', q, k)
            if causal:
                Lq, Lk = (s.shape[2], s.shape[3])
                mask = jnp.tril(jnp.ones((Lq, Lk), dtype=bool))
                s = jnp.where(mask, s, -jnp.inf)
            p = jax.nn.softmax(s, axis=-1)
            return jnp.einsum('bhlm,bmhd->blhd', p, v)

        def _forward(x, y, ln1_g, ln1_b, sa_wq, sa_bq, sa_wk, sa_bk, sa_wv, sa_bv, sa_wo, sa_bo, ln2_g, ln2_b, ca_wq, ca_bq, ca_wk, ca_bk, ca_wv, ca_bv, ca_wo, ca_bo, ln3_g, ln3_b, fc1_w, fc1_b, fc2_w, fc2_b):
            Bx, Lx, _ = x.shape
            Ly = y.shape[1]
            cos, sin = _rope_tables(max(Lx, Ly), HD)
            scale = HD ** (-0.5)
            h = _ln(x, ln1_g, ln1_b)
            q = (h @ sa_wq + sa_bq).reshape(Bx, Lx, H, HD) * scale
            k = (h @ sa_wk + sa_bk).reshape(Bx, Lx, H, HD)
            v = (h @ sa_wv + sa_bv).reshape(Bx, Lx, H, HD)
            q = _apply_rope(q, cos[:Lx], sin[:Lx])
            k = _apply_rope(k, cos[:Lx], sin[:Lx])
            a = _attn(q, k, v, causal=True).reshape(Bx, Lx, E)
            x = x + (a @ sa_wo + sa_bo)
            h = _ln(x, ln2_g, ln2_b)
            q = (h @ ca_wq + ca_bq).reshape(Bx, Lx, H, HD) * scale
            k = (y @ ca_wk + ca_bk).reshape(Bx, Ly, H, HD)
            v = (y @ ca_wv + ca_bv).reshape(Bx, Ly, H, HD)
            q = _apply_rope(q, cos[:Lx], sin[:Lx])
            k = _apply_rope(k, cos[:Ly], sin[:Ly])
            a = _attn(q, k, v, causal=False).reshape(Bx, Lx, E)
            x = x + (a @ ca_wo + ca_bo)
            h = _ln(x, ln3_g, ln3_b)
            return x + (jax.nn.gelu(h @ fc1_w + fc1_b) @ fc2_w + fc2_b)
        return _forward(x, y, ln1_g, ln1_b, sa_wq, sa_bq, sa_wk, sa_bk, sa_wv, sa_bv, sa_wo, sa_bo, ln2_g, ln2_b, ca_wq, ca_bq, ca_wk, ca_bk, ca_wv, ca_bv, ca_wo, ca_bo, ln3_g, ln3_b, fc1_w, fc1_b, fc2_w, fc2_b)

    def _L1_xattn_ref(q_x, kv_x, Wq, Wkv, Wo, bo, ln_q_g, ln_q_b, ln_kv_g, ln_kv_b, W1, b1, W2, b2):
        import jax, jax.numpy as jnp
        import numpy as np
        D = 128
        H = 16
        HD = D // H
        DFF = 4 * D
        LN_EPS = 1e-05

        def layernorm(x, gamma, beta):
            mu = jnp.mean(x, axis=-1, keepdims=True)
            var = jnp.mean(jnp.square(x - mu), axis=-1, keepdims=True)
            return (x - mu) * jax.lax.rsqrt(var + LN_EPS) * gamma + beta
        B, Nq, _ = q_x.shape
        Nk = kv_x.shape[1]
        scale = HD ** (-0.5)
        q = layernorm(q_x, ln_q_g, ln_q_b) @ Wq.T
        kv = layernorm(kv_x, ln_kv_g, ln_kv_b) @ Wkv.T
        q = q.reshape(B, Nq, H, HD).transpose(0, 2, 1, 3)
        kv = kv.reshape(B, Nk, 2, H, HD).transpose(2, 0, 3, 1, 4)
        k, v = (kv[0], kv[1])
        attn = jnp.einsum('bhqd,bhkd->bhqk', q, k) * scale
        attn = jax.nn.softmax(attn, axis=-1)
        out = jnp.einsum('bhqk,bhkd->bhqd', attn, v)
        out = out.transpose(0, 2, 1, 3).reshape(B, Nq, D)
        x = q_x + out @ Wo.T + bo
        h = jax.nn.silu(x @ W1.T + b1)
        x = x + h @ W2.T + b2
        return x

    def _L2_xattn_ref(base_hidden, scaffold_hidden, in_proj_w, in_proj_b, out_w, out_b, score_w, score_b):
        import jax, jax.numpy as jnp
        import numpy as np
        TOPK = 10
        NUM_HEADS = 16
        B, N, D = base_hidden.shape
        H = NUM_HEADS
        dh = D // H
        scores = jnp.einsum('bnd,d->bn', base_hidden, score_w[0]) + score_b[0]
        _, topk_idx = jax.lax.top_k(scores, TOPK)
        sparse_hidden = jnp.take_along_axis(base_hidden, topk_idx[:, :, None], axis=1)
        Wq, Wk, Wv = jnp.split(in_proj_w, 3, axis=0)
        bq, bk, bv = jnp.split(in_proj_b, 3)
        q = (sparse_hidden @ Wq.T + bq).reshape(B, TOPK, H, dh).transpose(0, 2, 1, 3)
        k = (scaffold_hidden @ Wk.T + bk).reshape(B, -1, H, dh).transpose(0, 2, 1, 3)
        v = (scaffold_hidden @ Wv.T + bv).reshape(B, -1, H, dh).transpose(0, 2, 1, 3)
        scale = 1.0 / np.sqrt(dh).astype(np.float32)
        logits = jnp.einsum('bhqd,bhkd->bhqk', q, k) * scale
        attn = jax.nn.softmax(logits, axis=-1)
        o = jnp.einsum('bhqk,bhkd->bhqd', attn, v).transpose(0, 2, 1, 3).reshape(B, TOPK, D)
        attn_out = o @ out_w.T + out_b
        return base_hidden.at[jnp.arange(B)[:, None], topk_idx].set(attn_out)

    def _L3_xattn_ref(latents, tokens, sa_ln_g, sa_ln_b, sa_in_w, sa_in_b, sa_out_w, sa_out_b, ca_q_ln_g, ca_q_ln_b, ca_kv_ln_g, ca_kv_ln_b, ca_in_w, ca_in_b, ca_out_w, ca_out_b, moe_ln_g, moe_ln_b, router_w, router_b, e_fc1_w, e_fc1_b, e_fc2_w, e_fc2_b):
        import jax, jax.numpy as jnp
        import numpy as np
        D, H, E, K, DFF = (128, 16, 8, 2, 512)
        B, L, T = (4, 64, 256)
        EPS = 1e-05

        def _xavier(key, shape):
            fan_in, fan_out = (shape[-1], shape[-2])
            a = jnp.sqrt(6.0 / (fan_in + fan_out))
            return jax.random.uniform(key, shape, jnp.float32, -a, a)

        def _ln(x, g, b):
            m = x.mean(-1, keepdims=True)
            v = ((x - m) ** 2).mean(-1, keepdims=True)
            return (x - m) / jnp.sqrt(v + EPS) * g + b

        def _mha(q_in, kv_in, in_w, in_b, out_w, out_b):
            wq, wk, wv = jnp.split(in_w, 3, axis=0)
            bq, bk, bv = jnp.split(in_b, 3, axis=0)
            dh = D // H

            def heads(x, w, b):
                y = x @ w.T + b
                return y.reshape(x.shape[0], x.shape[1], H, dh).transpose(0, 2, 1, 3)
            q = heads(q_in, wq, bq)
            k = heads(kv_in, wk, bk)
            v = heads(kv_in, wv, bv)
            scores = jnp.einsum('bhqd,bhkd->bhqk', q, k) / jnp.sqrt(jnp.float32(dh))
            attn = jax.nn.softmax(scores, axis=-1)
            out = jnp.einsum('bhqk,bhkd->bhqd', attn, v)
            out = out.transpose(0, 2, 1, 3).reshape(q_in.shape[0], q_in.shape[1], D)
            return out @ out_w.T + out_b

        def _fuse_moe(x, ln_g, ln_b, rw, rb, fc1_w, fc1_b, fc2_w, fc2_b):
            h = _ln(x, ln_g, ln_b)
            logits = h @ rw.T + rb
            vals, idx = jax.lax.top_k(logits, K)
            gates = jax.nn.softmax(vals, axis=-1)
            N = x.shape[0] * x.shape[1]
            hf = h.reshape(N, D)
            h1 = jax.nn.gelu(jnp.einsum('nd,efd->enf', hf, fc1_w) + fc1_b[:, None, :], approximate=False)
            eo = jnp.einsum('enf,edf->end', h1, fc2_w) + fc2_b[:, None, :]
            idx_f = idx.reshape(N, K)
            gates_f = gates.reshape(N, K)
            gathered = eo[idx_f, jnp.arange(N)[:, None], :]
            mixed = (gathered * gates_f[..., None]).sum(axis=1).reshape(x.shape)
            return x + mixed
        q = _ln(latents, sa_ln_g, sa_ln_b)
        x = latents + _mha(q, q, sa_in_w, sa_in_b, sa_out_w, sa_out_b)
        qc = _ln(x, ca_q_ln_g, ca_q_ln_b)
        kv = _ln(tokens, ca_kv_ln_g, ca_kv_ln_b)
        x = x + _mha(qc, kv, ca_in_w, ca_in_b, ca_out_w, ca_out_b)
        return _fuse_moe(x, moe_ln_g, moe_ln_b, router_w, router_b, e_fc1_w, e_fc1_b, e_fc2_w, e_fc2_b)
    x = _L0_xattn_ref(x, ctx_1024, L0_xattn_ln1_g, L0_xattn_ln1_b, L0_xattn_sa_wq, L0_xattn_sa_bq, L0_xattn_sa_wk, L0_xattn_sa_bk, L0_xattn_sa_wv, L0_xattn_sa_bv, L0_xattn_sa_wo, L0_xattn_sa_bo, L0_xattn_ln2_g, L0_xattn_ln2_b, L0_xattn_ca_wq, L0_xattn_ca_bq, L0_xattn_ca_wk, L0_xattn_ca_bk, L0_xattn_ca_wv, L0_xattn_ca_bv, L0_xattn_ca_wo, L0_xattn_ca_bo, L0_xattn_ln3_g, L0_xattn_ln3_b, L0_xattn_fc1_w, L0_xattn_fc1_b, L0_xattn_fc2_w, L0_xattn_fc2_b)
    x = _L1_xattn_ref(x, ctx_1024, L1_xattn_Wq, L1_xattn_Wkv, L1_xattn_Wo, L1_xattn_bo, L1_xattn_ln_q_g, L1_xattn_ln_q_b, L1_xattn_ln_kv_g, L1_xattn_ln_kv_b, L1_xattn_W1, L1_xattn_b1, L1_xattn_W2, L1_xattn_b2)
    x = _L2_xattn_ref(x, ctx_1024, L2_xattn_in_proj_w, L2_xattn_in_proj_b, L2_xattn_out_w, L2_xattn_out_b, L2_xattn_score_w, L2_xattn_score_b)
    x = _L3_xattn_ref(x, ctx_1024, L3_xattn_sa_ln_g, L3_xattn_sa_ln_b, L3_xattn_sa_in_w, L3_xattn_sa_in_b, L3_xattn_sa_out_w, L3_xattn_sa_out_b, L3_xattn_ca_q_ln_g, L3_xattn_ca_q_ln_b, L3_xattn_ca_kv_ln_g, L3_xattn_ca_kv_ln_b, L3_xattn_ca_in_w, L3_xattn_ca_in_b, L3_xattn_ca_out_w, L3_xattn_ca_out_b, L3_xattn_moe_ln_g, L3_xattn_moe_ln_b, L3_xattn_router_w, L3_xattn_router_b, L3_xattn_e_fc1_w, L3_xattn_e_fc1_b, L3_xattn_e_fc2_w, L3_xattn_e_fc2_b)
    return x

_drawn_inputs = setup_inputs


def setup_inputs(seed=0):
    import zlib

    import numpy as np

    out = dict(_drawn_inputs(seed))
    spreads = {'L0_xattn_ln1_g': (1.0, 0.6),
     'L0_xattn_ln1_b': (0.0, 0.328),
     'L0_xattn_sa_bq': (0.0, 0.782),
     'L0_xattn_sa_bk': (0.0, 0.8),
     'L0_xattn_sa_bv': (0.0, 0.1),
     'L0_xattn_sa_bo': (0.0, 0.1),
     'L0_xattn_ln2_g': (1.0, 0.6),
     'L0_xattn_ln2_b': (0.0, 0.8),
     'L0_xattn_ca_bq': (0.0, 0.8),
     'L0_xattn_ca_bk': (0.0, 0.8),
     'L0_xattn_ca_bv': (0.0, 0.1),
     'L0_xattn_ca_bo': (0.0, 0.1),
     'L0_xattn_ln3_g': (1.0, 0.6),
     'L0_xattn_ln3_b': (0.0, 0.394),
     'L0_xattn_fc1_b': (0.0, 0.1),
     'L0_xattn_fc2_b': (0.0, 0.1),
     'L1_xattn_bo': (0.0, 0.1),
     'L1_xattn_ln_q_g': (1.0, 0.6),
     'L1_xattn_ln_q_b': (0.0, 2.0),
     'L1_xattn_ln_kv_g': (1.0, 0.586),
     'L1_xattn_ln_kv_b': (0.0, 0.457),
     'L1_xattn_b1': (0.0, 0.1),
     'L1_xattn_b2': (0.0, 0.1),
     'L3_xattn_sa_ln_g': (1.0, 0.2),
     'L3_xattn_sa_ln_b': (0.0, 0.1),
     'L3_xattn_sa_in_b': (0.0, 0.1),
     'L3_xattn_sa_out_b': (0.0, 0.1),
     'L3_xattn_ca_q_ln_g': (1.0, 0.2),
     'L3_xattn_ca_q_ln_b': (0.0, 0.333),
     'L3_xattn_ca_kv_ln_g': (1.0, 0.2),
     'L3_xattn_ca_kv_ln_b': (0.0, 0.1),
     'L3_xattn_ca_in_b': (0.0, 0.1),
     'L3_xattn_ca_out_b': (0.0, 0.1),
     'L3_xattn_moe_ln_g': (1.0, 0.2),
     'L3_xattn_moe_ln_b': (0.0, 0.1),
     'L3_xattn_router_b': (0.0, 0.1),
     'L3_xattn_e_fc1_b': (0.0, 0.1),
     'L3_xattn_e_fc2_b': (0.0, 0.1)}
    factors = {'L0_xattn_sa_wq': 5.81,
     'L0_xattn_sa_wk': 7.168,
     'L0_xattn_ca_wq': 8.0,
     'L0_xattn_ca_wk': 8.0,
     'L1_xattn_Wq': 6.795,
     'L2_xattn_in_proj_b': 2.715}
    for name, (base, spread) in spreads.items():
        noise = np.random.default_rng([zlib.crc32(name.encode()), seed]).standard_normal(out[name].shape)
        drawn = base * np.exp(spread * noise) if base else spread * noise
        out[name] = jnp.asarray(drawn.astype(out[name].dtype))
    for name, factor in factors.items():
        out[name] = (out[name] * factor).astype(out[name].dtype)
    return out
```

```python
from contextlib import ExitStack

import concourse.bass as bass
from concourse import mybir

ALU = mybir.AluOpType
ACT = mybir.ActivationFunctionType
AX_X = mybir.AxisListType.X
F32 = mybir.dt.float32
BF16 = mybir.dt.bfloat16

P = 128
D = 128
SEQS, SEQ = 16, 64
TILES = SEQS * SEQ // P
HEADS, HD = 16, 8
PAIRS = HEADS // 2
SLOTS = HEADS // 2
SP = SLOTS // 2
VW = HD + 1
FF = 512
CH = FF // P
EXPERTS = 8
TOPK = 10
LN_EPS = 1e-5
SCALE = HD ** -0.5
GELU_C = 0.7978845608028654
GELU_A = 0.044715

BLOCKS = [
    dict(name="sa0", kind="attn", ln=True, rope=True, kv="self", causal=True),
    dict(name="ca0", kind="attn", ln=True, rope=True, kv="ctx"),
    dict(name="ff0", kind="mlp", ln=True, act="gelu"),
    dict(name="ca1", kind="attn", ln=True, kv="ctx1", nobias=True),
    dict(name="ff1", kind="mlp", ln=False, act="silu"),
    dict(name="ca2", kind="attn", ln=False, kv="ctx", topk=True),
    dict(name="sa3", kind="attn", ln=True, kv="self"),
    dict(name="ca3", kind="attn", ln=True, kv="ctx3"),
    dict(name="moe", kind="moe", ln=True),
]
NB = len(BLOCKS)
LNS = [n for n, b in enumerate(BLOCKS) if b["ln"]]

WEIGHTS = []
for _b in BLOCKS:
    if _b["kind"] == "attn":
        WEIGHTS += [(_b["name"], w) for w in (("q", "qr", "k", "kr", "v", "o0", "o1") if _b.get("rope") else ("q", "k", "v", "o0", "o1"))]
COLS = []
for _b in BLOCKS:
    if _b["ln"]:
        COLS += [(_b["name"], "g"), (_b["name"], "b")]
    if _b["kind"] == "attn" and not _b.get("nobias"):
        COLS += [(_b["name"], c) for c in (("bq", "bqr", "bk", "bkr", "bv0", "bv1") if _b.get("rope") else ("bq", "bk", "bv0", "bv1"))]
    if _b["kind"] == "mlp":
        COLS += [(_b["name"], f"f{c}") for c in range(CH)]
COLS += [("ctx1", "g"), ("ctx1", "b"), ("ctx3", "g"), ("ctx3", "b")]
COLS += [("moe", f"f{e}_{c}") for e in range(EXPERTS) for c in range(CH)]
ROWS = [(b["name"], "bo") for b in BLOCKS if b["kind"] != "moe"] + [("ca2", "score")]
ROW_ROUTER = len(ROWS) * D
ROW_SCORE_B = ROW_ROUTER + EXPERTS
ROW_N = ROW_SCORE_B + 1
CONSTS, _at = {}, 0
for _n, _w in (("ident", P), ("same_seq", P), ("fold", SEQ), ("before", SEQ), ("causal", SEQ), ("slot", SLOTS),
               ("cos", 2 * SEQ), ("sin", 2 * SEQ), ("before8", EXPERTS * EXPERTS)):
    CONSTS[_n] = (_at, _w)
    _at += _w
CONST_N = _at

OFFSET = {"attn": 5, "mlp": 3, "moe": 0}
ORDER = {
    "attn": {"ln": 0, "topk": 0, "scores": 2, "turn_h": 0, "turn_o": 4, "turn_p": 3, "qk": 0, "update": 4, "values": 0, "pv": 3},
    "mlp": {"ln": 0, "turn_h": 0, "hidden": 1, "tanh": 1, "gate": 2, "fc2": 2},
    "moe": {"ln": 0, "turn_h": 0, "route": 1, "mixture_bias": 2},
}
FIRST = ["ctx_ln", "topk", "ln", "gate"]
PER_BLOCK = ["turn_p", "scores"]
LAST = ["ctx_turn", "turn_h", "turn_o", "hidden", "pv", "fc2", "qk", "update", "tanh", "values", "route", "mixture_bias"]


def make_schedule():
    start, at = [], 1
    for b in BLOCKS:
        start.append(at)
        at += OFFSET[b["kind"]]
    out = []

    def add(stage, n, slot):
        b = BLOCKS[n]
        lag = ORDER[b["kind"]].get(stage)
        if stage in ("ctx_ln", "ctx_turn"):
            if n:
                return
            lag = (stage == "ctx_turn") - start[0]
        if lag is None or stage == "topk" and not b.get("topk") or stage == "ln" and not b["ln"]:
            return
        t = slot - start[n] - lag
        if 0 <= t < TILES:
            out.append((stage, n, t))

    for slot in range(at + TILES + 8):
        for stage in FIRST:
            for n in range(NB):
                add(stage, n, slot)
        for n in range(NB):
            for stage in PER_BLOCK:
                add(stage, n, slot)
        for stage in LAST:
            for n in range(NB):
                add(stage, n, slot)
    return out


SCHEDULE = make_schedule()
_runs, NTH = {}, {}
for _s, _b, _t in SCHEDULE:
    _runs[_s] = _runs.get(_s, 0) + 1
    NTH[_s, _b, _t] = _runs[_s]
USES = {"ctx_turn": 2, "topk": 1, "turn_h": 1, "turn_o": 1, "qk": 1, "update": 1, "values": 1, "pv": 1,
        "hidden": 1, "fc2": 1, "route": 1, "mixture_bias": 2}
_n, BANK = 0, {}
for _s, _b, _t in SCHEDULE:
    for _u in range(USES.get(_s, 0)):
        BANK[_s, _b, _t, _u] = (_n % 2, _n // 2)
        _n += 1
ATTNS = [n for n, b in enumerate(BLOCKS) if b["kind"] == "attn"]
MOE = NB - 1
BIASED = [n for n in ATTNS if not BLOCKS[n].get("nobias")]
BIAS_FREE = next(n for n in ATTNS if BLOCKS[n].get("nobias"))
GROUPS = 2
GT = TILES // GROUPS
EXPERT_RUNS = [(g, e) for g in range(GROUPS) for e in range(EXPERTS)]


def bank_use(stage, block, tile, use=0):
    return BANK[stage, block, tile, use]


def previous_attention(n):
    before = [a for a in ATTNS if a < n]
    return before[-1] if before else None


def residual_ready(eng, sems, n, t):
    if n == 0:
        eng.wait_ge(sems["x_in"], 16)
        return
    b, count = bank_use("update" if BLOCKS[n - 1]["kind"] == "attn" else "fc2", n - 1, t)
    eng.wait_ge(sems["bank_empty"][b], count + 1)


def build(nc, x_in, ctx_in, weights, mlp_w, moe_w1, moe_w2, moe_b2, router_w, cols, rows, consts, out):
    with ExitStack() as ctx:
        def sb(name, shape, dt=F32):
            return ctx.enter_context(nc.sbuf_tensor(name, shape, dt))

        def sem(name):
            return ctx.enter_context(nc.semaphore(name))

        w_sb = sb("w_sb", [P, len(WEIGHTS), D])
        mlp_sb = sb("mlp_sb", [P, 2, 2, FF])
        moe1_sb = sb("moe1_sb", [P, EXPERTS, FF])
        moe2_sb = sb("moe2_sb", [P, EXPERTS, CH, D])
        moe_b2_sb = sb("moe_b2_sb", [EXPERTS, D])
        router_sb = sb("router_sb", [P, EXPERTS])
        cols_sb = sb("cols_sb", [P, len(COLS)])
        rows_sb = sb("rows_sb", [P, ROW_N])
        const_sb = sb("const_sb", [P, CONST_N])
        ident16 = sb("ident16", [P, P], BF16)
        causal16 = sb("causal16", [P, SEQ], BF16)
        bv_wide = sb("bv_wide", [P, 2, P])
        out_bias = sb("out_bias", [P, len(ATTNS), D])
        minus_half = sb("minus_half", [P, 1])
        x_sb = sb("x_sb", [P, TILES, D])
        ctx_sb = sb("ctx_sb", [P, TILES, D])
        ctx_hat = sb("ctx_hat", [P, TILES, D])
        feat = {k: sb(f"feat_{k}", [P, TILES, P]) for k in ("self", "ctx", "ctx1", "ctx3")}
        xhat = sb("xhat", [P, TILES, D])
        xbias = xhat
        stats = sb("stats", [P, TILES, 6])
        moments = sb("moments", [P, TILES, 2])
        varp = sb("varp", [P, TILES, 1])
        rstd = sb("rstd", [P, TILES, 1])
        cstats = sb("cstats", [P, TILES, 6])
        cmoments = sb("cmoments", [P, TILES, 2])
        cvarp = sb("cvarp", [P, TILES, 1])
        crstd = sb("crstd", [P, TILES, 1])
        k_feat = sb("k_feat", [P, TILES, P])
        q_blocks = sb("q_blocks", [P, TILES, 2, 2, SEQ])
        rope_a = sb("rope_a", [P, 2, 2, P])
        rope_b = sb("rope_b", [P, 2, 2, P])
        key_blocks = sb("key_blocks", [P, TILES, 2, SLOTS, SEQ])
        value_blocks = sb("value_blocks", [P, TILES, 2, 2, SP, 2, VW])
        row_max = sb("row_max", [P, 2, HEADS])
        probs = sb("probs", [P, 2, HEADS, SEQ])
        probs_t = sb("probs_t", [P, 2, PAIRS, P])
        rden = sb("rden", [P, TILES, HEADS])
        onorm = ctx_hat
        o_blocks = sb("o_blocks", [P, TILES, 2, 2, SEQ])
        score_junk = sb("score_junk", [P, D])
        score = sb("score", [P, TILES, 2])
        score_diag = sb("score_diag", [P, 2, SEQ])
        rank_junk = sb("rank_junk", [P, 3, SEQ])
        rank = sb("rank", [P, TILES, 4])
        chosen = sb("chosen", [P, TILES, 2])
        hid = moe2_sb[:, 0:2]
        hid_act = moe2_sb[:, 2:4]
        logits = sb("logits", [P, TILES, EXPERTS])
        cmp_gt = sb("cmp_gt", [P, 2, EXPERTS, EXPERTS])
        cmp_eq = sb("cmp_eq", [P, 2, EXPERTS, EXPERTS])
        rank8 = sb("rank8", [P, TILES, EXPERTS])
        top = sb("top", [P, TILES, 1])
        gate_e = sb("gate_e", [P, TILES, EXPERTS])
        gate_s = sb("gate_s", [P, TILES, 2])
        gates = sb("gates", [P, TILES, EXPERTS])
        gates_t = feat["ctx1"][0:EXPERTS]
        hidden_e = key_blocks[:, 0:4].rearrange("p t s h k -> p (t s h k)").rearrange("p (r c q) -> p r c q", r=2, c=CH)
        mix = feat["ctx"]

        ps_scores = ctx.enter_context(nc.psum_tensor("ps_scores", [P, 4, 512], F32))
        ps_turn = ctx.enter_context(nc.psum_tensor("ps_turn", [P, 2, 512], F32))
        ps_work = ctx.enter_context(nc.psum_tensor("ps_work", [P, 2, 512], F32))

        x_loaded, ctx_loaded, small_loaded = sem("x_loaded"), sem("ctx_loaded"), sem("small_loaded")
        w_loaded = {b["name"]: sem(f"w_loaded_{b['name']}") for b in BLOCKS}
        setup_done = sem("setup_done")
        pool_setup = sem("pool_setup")
        dve_chain = sem("dve_chain")
        pool_chain = sem("pool_chain")
        moments_ready, rstd_ready, xhat_ready = sem("moments_ready"), sem("rstd_ready"), sem("xhat_ready")
        cmoments_ready, crstd_ready, chat_ready = sem("cmoments_ready"), sem("crstd_ready"), sem("chat_ready")
        xbias_ready = sem("xbias_ready")
        bank_full = [sem("bank_full0"), sem("bank_full1")]
        bank_empty = [sem("bank_empty0"), sem("bank_empty1")]
        q_roped, k_roped = sem("q_roped"), sem("k_roped")
        keys_ready = sem("keys_ready")
        bv_ready, bias_full, bias_ready = sem("bv_ready"), sem("bias_full"), sem("bias_ready")
        scores_ready, shifted, probs_ready = sem("scores_ready"), sem("shifted"), sem("probs_ready")
        turned, turned_out = sem("turned"), sem("turned_out")
        diag_ready = sem("diag_ready")
        chosen_ready = sem("chosen_ready")
        sq_ready, cubic_ready, tanh_ready, gated_ready = (
            sem("sq_ready"), sem("cubic_ready"), sem("tanh_ready"), sem("gated_ready"))
        logits_shifted, gate_exp, gates_ready = sem("logits_shifted"), sem("gate_exp"), sem("gates_ready")
        fc1_full = [sem(f"fc1_full{i}") for i in range(4)]
        fc1_empty = [sem(f"fc1_empty{i}") for i in range(4)]
        fc2_full = [sem(f"fc2_full{i}") for i in range(2)]
        fc2_empty = [sem(f"fc2_empty{i}") for i in range(2)]
        mixed = sem("mixed")
        out_done = sem("out_done")
        sems = {"x_in": x_loaded, "bank_empty": bank_empty}

        def weight(n, which):
            return w_sb[:, WEIGHTS.index((BLOCKS[n]["name"], which)), :]

        def col(name, which):
            i = COLS.index((name, which))
            return cols_sb[:, i:i + 1]

        def row(name, which):
            i = ROWS.index((name, which)) * D
            return rows_sb[:, i:i + D]

        def const(name):
            at, width = CONSTS[name]
            return const_sb[:, at:at + width]

        ident = const("ident")
        def qkv_order(n):
            b = BLOCKS[n]
            if b.get("rope"):
                return ["q", "k", "qr", "kr"]
            return ["q", "k"]

        block = ctx.enter_context(nc.Block())

        @block.sync
        def _(sp):
            sp.dma_start(cols_sb[:, :], cols).then_inc(small_loaded, 16)
            sp.dma_start(const_sb[:, :], consts).then_inc(small_loaded, 16)
            sp.dma_start(x_sb[:, :, :], x_in.rearrange("(t p) d -> p t d", p=P)).then_inc(x_loaded, 16)
            sp.dma_start(ctx_sb[:, :, :], ctx_in.rearrange("(t p) d -> p t d", p=P)).then_inc(ctx_loaded, 16)
            at = 0
            m = 0
            for b in BLOCKS:
                if b["kind"] == "attn":
                    k = sum(w[0] == b["name"] for w in WEIGHTS)
                    sp.dma_start(w_sb[:, at:at + k, :], weights[:, at:at + k, :]).then_inc(w_loaded[b["name"]], 16)
                    at += k
                elif b["kind"] == "mlp":
                    sp.dma_start(mlp_sb[:, m], mlp_w[:, m]).then_inc(w_loaded[b["name"]], 16)
                    m += 1
                if b["name"] == "sa0":
                    sp.dma_start(rows_sb[:, :], rows.broadcast_to([P, ROW_N])).then_inc(small_loaded, 16)
                    sp.dma_start(router_sb[:, :], router_w).then_inc(small_loaded, 16)
                    sp.dma_start(moe_b2_sb[:, :], moe_b2).then_inc(small_loaded, 16)
            sp.dma_start(moe1_sb[:, :, :], moe_w1).then_inc(w_loaded["moe"], 16)

            for stage, n, t in SCHEDULE:
                if (stage, BLOCKS[n]["name"], t) == ("fc2", "ff1", TILES - 1):
                    j, count = bank_use(stage, n, t)
                    sp.wait_ge(bank_empty[j], count + 1)
                    sp.dma_start(moe2_sb[:, :, :, :], moe_w2).then_inc(w_loaded["moe"], 16)
            for g in range(GROUPS):
                for t in range(g * GT, (g + 1) * GT):
                    sp.wait_ge(mixed, (g * EXPERTS + EXPERTS - 1) * GT + t - g * GT + 1)
                    sp.dma_start(out[t * P:(t + 1) * P, :], mix[:, t, :]).then_inc(out_done, 16)
            sp.wait_ge(out_done, 16 * TILES)

        @block.gpsimd
        def _(pool):
            chain = [0]

            def link(ins):
                chain[0] += 1
                ins.then_inc(pool_chain, 1)
                pool.wait_ge(pool_chain, chain[0])

            pool.memset(minus_half[:, :], -0.5).then_inc(pool_setup, 1)
            for buffer in (q_blocks, o_blocks):
                pool.memset(buffer[:, :, :, :, :].rearrange("p t a b q -> p (t a b q)"), 0.0).then_inc(pool_setup, 1)
            pool.wait_ge(pool_setup, 3)

            def root(moment, var_eps, inverse_root, ready, count, done):
                pool.wait_ge(ready, count)
                link(pool.tensor_scalar(var_eps, moment[:, 1:2], LN_EPS, None, ALU.add))
                pool.tensor_tensor(inverse_root, var_eps, minus_half[:, :], ALU.pow).then_inc(done, 1)

            for stage, n, t in SCHEDULE:
                b = BLOCKS[n]
                if stage == "ctx_ln":
                    root(cmoments[:, t, :], cvarp[:, t, :], crstd[:, t, :], cmoments_ready, t + 1, crstd_ready)
                elif stage == "ln":
                    root(moments[:, t, :], varp[:, t, :], rstd[:, t, :], moments_ready, NTH["ln", n, t], rstd_ready)
                elif stage == "turn_h" and b["kind"] != "moe" and not b.get("topk"):
                    residual_ready(pool, sems, n, t)
                    j, count = bank_use(stage, n, t)
                    pool.wait_ge(bank_full[j], count + 1)
                    pool.wait_ge(bias_ready, len(BIASED) + 1)
                    bias = out_bias[:, ATTNS.index(n), :] if n in BIASED else row(b["name"], "bo")
                    pool.tensor_tensor(xbias[:, t, :], x_sb[:, t, :], bias, ALU.add).then_inc(xbias_ready, 1)
                elif stage == "turn_h" and b.get("topk"):
                    pool.wait_ge(chosen_ready, t + 1)
                    pool.wait_ge(small_loaded, 80)
                    keep = chosen[:, t, 1:2].broadcast_to([P, D])
                    take = chosen[:, t, 0:1].broadcast_to([P, D])
                    link(pool.tensor_tensor(xbias[:, t, :], x_sb[:, t, :], keep, ALU.mult))
                    link(pool.tensor_tensor(onorm[:, t, :], out_bias[:, ATTNS.index(n), :], take, ALU.mult))
                    pool.tensor_tensor(xbias[:, t, :], xbias[:, t, :], onorm[:, t, :], ALU.add).then_inc(xbias_ready, 1)
                elif stage == "qk":
                    j, count = bank_use("qk", n, t)
                    pool.wait_ge(bank_empty[j], count + 1)
                    if b.get("rope"):
                        i = NTH_ROPE[n, t]
                        pool.tensor_tensor(k_feat[:, t, :], rope_a[:, i % 2, 1], rope_b[:, i % 2, 1], ALU.add).then_inc(k_roped, 1)
                        pool.wait_ge(k_roped, i)
                    spread = k_feat[:, t, :].rearrange("p (b o k) -> p b o k", b=2, o=1).broadcast_to([P, 2, SLOTS, SEQ])
                    mask = const("slot").rearrange("p (b s o) -> p b s o", b=1, o=1).broadcast_to([P, 2, SLOTS, SEQ])
                    pool.tensor_tensor(key_blocks[:, t], spread, mask, ALU.mult).then_inc(keys_ready, 1)
                elif stage == "hidden" and b["act"] == "gelu":
                    i = NTH["hidden", n, t] - 1
                    pool.wait_ge(sq_ready, t + 1)
                    link(pool.tensor_tensor(hid_act[:, i % 2], hid_act[:, i % 2], hid[:, i % 2], ALU.mult))
                    pool.tensor_tensor(hid_act[:, i % 2], hid_act[:, i % 2], hid[:, i % 2], ALU.add).then_inc(cubic_ready, 1)

        @block.scalar
        def _(act):
            act.wait_ge(small_loaded, 80)

            def drain(stage, n, t, use, emit):
                j, count = bank_use(stage, n, t, use)
                act.wait_ge(bank_full[j], count + 1)
                emit(ps_work[:, j]).then_inc(bank_empty[j], 1)

            def affine(out, in_, g, b):
                return nc.scalar.activation(out, in_, ACT.Identity, bias=b, scale=g)

            for stage, n, t in SCHEDULE:
                b = BLOCKS[n]
                name = b["name"]
                if stage == "ctx_turn":
                    drain(stage, n, t, 0, lambda ps: nc.scalar.copy(feat["ctx"][:, t, :], ps[:, 0:P]))

                    def both(ps):
                        affine(feat["ctx1"][:, t, :], ps[:, 0:P], col("ctx1", "g"), col("ctx1", "b"))
                        return affine(feat["ctx3"][:, t, :], ps[:, 0:P], col("ctx3", "g"), col("ctx3", "b"))
                    drain(stage, n, t, 1, both)
                elif stage == "turn_h":
                    if b["ln"]:
                        drain(stage, n, t, 0, lambda ps: affine(feat["self"][:, t, :], ps[:, 0:P], col(name, "g"), col(name, "b")))
                    else:
                        drain(stage, n, t, 0, lambda ps: nc.scalar.copy(feat["self"][:, t, :], ps[:, 0:P]))
                elif stage == "turn_o":
                    def onto_blocks(ps):
                        for s in range(2):
                            r = slice(s * SEQ, (s + 1) * SEQ)
                            last = nc.scalar.copy(o_blocks[r, t, :, s, :], ps[r, 0:P].rearrange("p (h q) -> p h q", h=2))
                        return last
                    if n == 0:
                        act.wait_ge(pool_setup, 3)
                    drain(stage, n, t, 0, onto_blocks)
                elif stage == "values":
                    def both_halves(ps):
                        for e in range(2):
                            r = slice(e * SEQ, (e + 1) * SEQ)
                            dst = value_blocks[r, t, :, :, :, e, 0:HD].rearrange("p s h j d -> p (s h j) d")
                            last = nc.scalar.copy(dst, ps[r, 0:D].rearrange("p (g d) -> p g d", d=HD))
                        return last
                    if n == 0:
                        act.wait_ge(setup_done, 1)
                    drain(stage, n, t, 0, both_halves)
                elif stage == "scores":
                    i = NTH[stage, n, t]
                    act.wait_ge(shifted, i)
                    flat = probs[:, i % 2].rearrange("p h k -> p (h k)")
                    nc.scalar.activation(flat, flat, ACT.Exp).then_inc(probs_ready, 1)
                elif stage == "turn_p":
                    i = NTH[stage, n, t]
                    for half in range(2):
                        act.wait_ge(turned, 2 * (i - 1) + half + 1)
                        nc.scalar.copy(probs_t[:, i % 2, 4 * half:4 * half + 4, :].rearrange("p g q -> p (g q)"),
                                       ps_turn[:, half, :]).then_inc(turned_out, 1)
                elif stage == "hidden" and b["act"] == "gelu":
                    i = NTH[stage, n, t]
                    k, count = bank_use(stage, n, t)
                    act.wait_ge(bank_empty[k], count + 1)
                    nc.scalar.activation(hid_act[:, (i - 1) % 2], hid[:, (i - 1) % 2], ACT.Square, scale=GELU_A ** 0.5).then_inc(sq_ready, 1)
                elif stage == "tanh":
                    i = NTH[stage, n, t]
                    j = (i - 1) % 2
                    if b["act"] == "gelu":
                        act.wait_ge(cubic_ready, t + 1)
                        src, scale = hid_act[:, j], GELU_C
                    else:
                        k, count = bank_use("hidden", n, t)
                        act.wait_ge(bank_empty[k], count + 1)
                        src, scale = hid[:, j], 0.5
                    if i > 2:
                        act.wait_ge(gated_ready, i - 2)
                    nc.scalar.activation(hid_act[:, j], src, ACT.Tanh, scale=scale).then_inc(tanh_ready, 1)
                elif stage == "route":
                    act.wait_ge(logits_shifted, t + 1)
                    nc.scalar.activation(gate_e[:, t, :], gate_e[:, t, :], ACT.Exp).then_inc(gate_exp, 1)
                elif stage == "mixture_bias":
                    j, count = bank_use(stage, n, t, 0)
                    act.wait_ge(bank_full[j], count + 1)
                    nc.scalar.copy(gates_t[:, t, :], ps_work[0:EXPERTS, j, 0:P]).then_inc(bank_empty[j], 1)

            for r, (g, e) in enumerate(EXPERT_RUNS):
                for c in range(CH):
                    act.wait_ge(fc1_full[c], r + 1)
                    if c == 0 and r >= 2:
                        act.wait_ge(fc2_full[r % 2], (r - 2) // 2 + 1)
                    nc.scalar.activation(hidden_e[:, r % 2, c, :], ps_scores[:, c, :], ACT.Gelu,
                                         bias=col("moe", f"f{e}_{c}")).then_inc(fc1_empty[c], 1)

        @block.vector
        def _(dve):
            v = nc.vector
            chain = [0]

            def link(ins):
                chain[0] += 1
                ins.then_inc(dve_chain, 1)
                dve.wait_ge(dve_chain, chain[0])

            def full(stage, n, t, use=0):
                j, count = bank_use(stage, n, t, use)
                dve.wait_ge(bank_full[j], count + 1)
                return ps_work[:, j], bank_empty[j]

            link(v.memset(value_blocks[:, :, :, :, :, :, :].rearrange("p t s h j e v -> p (t s h j e v)"), 0.0))
            for e in range(2):
                r = slice(e * SEQ, (e + 1) * SEQ)
                ones = value_blocks[r, :, :, :, :, e, HD].rearrange("p t s h j -> p (t s h j)")
                if e == 0:
                    link(v.memset(ones, 1.0))
                else:
                    v.memset(ones, 1.0).then_inc(setup_done, 1)
            dve.wait_ge(small_loaded, 80)
            link(v.tensor_copy(ident16[:, :], ident))
            v.tensor_copy(causal16[:, :], const("causal")).then_inc(setup_done, 1)
            for i, n in enumerate(BIASED):
                if i:
                    dve.wait_ge(bias_full, i)
                name = BLOCKS[n]["name"]
                for h in range(2):
                    ins = v.tensor_scalar(bv_wide[0:SEQ, h, :], const("same_seq")[0:SEQ], 0.0, col(name, f"bv{h}")[0:SEQ], ALU.mult, ALU.add)
                ins.then_inc(bv_ready, 1)
                dve.wait_ge(bias_full, i + 1)
                v.tensor_tensor(out_bias[:, ATTNS.index(n), :], ps_turn[:, i % 2, 0:D], row(name, "bo"), ALU.add).then_inc(bias_ready, 1)
            n = BIAS_FREE
            v.tensor_copy(out_bias[:, ATTNS.index(n), :], row(BLOCKS[n]["name"], "bo")).then_inc(bias_ready, 1)

            def normalize(src, st, mo, rs, dst, moments_done, rstd_done, count, done):
                link(v.bn_stats(st, src))
                v.bn_aggr(mo, st).then_inc(moments_done, 1)
                dve.wait_ge(moments_done, count)
                dve.wait_ge(rstd_done, count)
                v.tensor_scalar(dst, src, mo[:, 0:1], rs, ALU.subtract, ALU.mult).then_inc(done, 1)

            for stage, n, t in SCHEDULE:
                b = BLOCKS[n]
                name = b["name"]
                if stage == "ctx_ln":
                    if t == 0:
                        dve.wait_ge(ctx_loaded, 16)
                    normalize(ctx_sb[:, t, :], cstats[:, t, :], cmoments[:, t, :], crstd[:, t, :], ctx_hat[:, t, :],
                              cmoments_ready, crstd_ready, t + 1, chat_ready)
                elif stage == "ln":
                    residual_ready(dve, sems, n, t)
                    normalize(x_sb[:, t, :], stats[:, t, :], moments[:, t, :], rstd[:, t, :], xhat[:, t, :],
                              moments_ready, rstd_ready, NTH["ln", n, t], xhat_ready)
                elif stage == "topk":
                    residual_ready(dve, sems, n, t)
                    link(v.scalar_tensor_tensor(score_junk[:, :], x_sb[:, t, :], 1.0, row("ca2", "score"), ALU.mult, ALU.mult,
                                                accum_out=score[:, t, 0:1]))
                    link(v.tensor_scalar(score[:, t, 1:2], score[:, t, 0:1], rows_sb[:, ROW_SCORE_B:ROW_SCORE_B + 1], None, ALU.add))
                    v.tensor_scalar(score_diag[:, t % 2], const("fold"), score[:, t, 1:2], None, ALU.mult).then_inc(diag_ready, 1)
                    ps, empty = full(stage, n, t)
                    ps = ps[:, 0:SEQ]
                    own, above, ties, total = (rank[:, t, i:i + 1] for i in range(4))
                    link(v.scalar_tensor_tensor(rank_junk[:, 0], ps, 1.0, const("fold"), ALU.mult, ALU.mult, accum_out=own))
                    link(v.tensor_scalar(rank_junk[:, 1], ps, own, 0.0, ALU.is_gt, ALU.add, accum_out=above))
                    v.scalar_tensor_tensor(rank_junk[:, 2], ps, own, const("before"), ALU.is_equal, ALU.mult,
                                           accum_out=ties).then_inc(empty, 1)
                    dve.wait_ge(empty, bank_use(stage, n, t)[1] + 1)
                    link(v.tensor_tensor(total, above, ties, ALU.add))
                    link(v.tensor_scalar(chosen[:, t, 0:1], total, TOPK - 0.5, None, ALU.is_lt))
                    v.tensor_scalar(chosen[:, t, 1:2], chosen[:, t, 0:1], -1.0, 1.0, ALU.mult, ALU.add).then_inc(chosen_ready, 1)
                elif stage == "qk":
                    ps, empty = full(stage, n, t)
                    if b.get("rope"):
                        i = NTH_ROPE[n, t]
                        if i > 2:
                            dve.wait_ge(k_roped, i - 2)
                        v4 = ps.rearrange("p (k b s) -> p k b s", k=4, b=2)
                        for table, first, dst, suffix in (("cos", 0, rope_a, ""), ("sin", 2, rope_b, "r")):
                            for k in range(2):
                                tab = const(table)[:, k * SEQ:(k + 1) * SEQ].rearrange("p (o s) -> p o s", o=1).broadcast_to([P, 2, SEQ])
                                ins = v.scalar_tensor_tensor(dst[:, i % 2, k].rearrange("p (b s) -> p b s", b=2), v4[:, first + k],
                                                             col(name, "b" + "qk"[k] + suffix), tab, ALU.add, ALU.mult)
                        ins.then_inc(empty, 1)
                        dve.wait_ge(empty, bank_use(stage, n, t)[1] + 1)
                        if (n, t) == (0, 0):
                            dve.wait_ge(pool_setup, 3)
                        for h in range(2):
                            r = slice(h * SEQ, (h + 1) * SEQ)
                            ins = v.tensor_tensor(q_blocks[r, t, :, h, :], rope_a[r, i % 2, 0].rearrange("p (b s) -> p b s", b=2),
                                                  rope_b[r, i % 2, 0].rearrange("p (b s) -> p b s", b=2), ALU.add)
                        ins.then_inc(q_roped, 1)
                    else:
                        for h in range(2):
                            r = slice(h * SEQ, (h + 1) * SEQ)
                            src = ps[r, 0:P].rearrange("p (b s) -> p b s", b=2)
                            if b.get("nobias"):
                                v.tensor_scalar(q_blocks[r, t, :, h, :], src, SCALE, None, ALU.mult)
                            else:
                                v.tensor_scalar(q_blocks[r, t, :, h, :], src, col(name, "bq")[r], SCALE, ALU.add, ALU.mult)
                        if b.get("nobias"):
                            v.tensor_copy(k_feat[:, t, :], ps[:, P:2 * P]).then_inc(empty, 1)
                        else:
                            v.tensor_scalar(k_feat[:, t, :], ps[:, P:2 * P], col(name, "bk"), None, ALU.add).then_inc(empty, 1)
                elif stage == "scores":
                    i = NTH[stage, n, t]
                    j = i % 2
                    s3 = ps_scores[:, 2 * j:2 * j + 2, :].rearrange("p g (h k) -> p (g h) k", k=SEQ)
                    dve.wait_ge(scores_ready, i)
                    link(v.tensor_reduce(row_max[:, j], s3, AX_X, ALU.max))
                    if i > 2:
                        dve.wait_ge(turned, 2 * (i - 2))
                    mx = row_max[:, j].rearrange("p (h o) -> p h o", o=1).broadcast_to([P, HEADS, SEQ])
                    v.tensor_tensor(probs[:, j], s3, mx, ALU.subtract).then_inc(shifted, 1)
                elif stage == "pv":
                    ps, empty = full(stage, n, t)
                    o5 = ps[:, 0:PAIRS * 4 * VW].rearrange("p (g h e v) -> p g h e v", g=PAIRS, h=2, e=2)
                    for h in range(2):
                        r = slice(h * SEQ, (h + 1) * SEQ)
                        rd = rden[r, t, :].rearrange("p (g e) -> p g e", e=2)
                        ins = v.reciprocal(rd, o5[r, :, h, :, HD])
                        ins.then_inc(dve_chain, 1)
                        chain[0] += 1
                    dve.wait_ge(dve_chain, chain[0])
                    for h in range(2):
                        r = slice(h * SEQ, (h + 1) * SEQ)
                        rd = rden[r, t, :].rearrange("p (g e o) -> p g e o", e=2, o=1).broadcast_to([SEQ, PAIRS, 2, HD])
                        dst = onorm[r, t, :].rearrange("p (g e d) -> p g e d", e=2, d=HD)
                        last = v.tensor_tensor(dst, o5[r, :, h, :, 0:HD], rd, ALU.mult)
                    last.then_inc(empty, 1)
                elif stage == "update":
                    ps, empty = full(stage, n, t)
                    dve.wait_ge(xbias_ready, NTH_XB[n, t])
                    if b.get("topk"):
                        v.scalar_tensor_tensor(x_sb[:, t, :], ps[:, 0:D], chosen[:, t, 0:1], xbias[:, t, :], ALU.mult, ALU.add).then_inc(empty, 1)
                    else:
                        v.tensor_tensor(x_sb[:, t, :], ps[:, 0:D], xbias[:, t, :], ALU.add).then_inc(empty, 1)
                elif stage == "hidden":
                    i = NTH[stage, n, t]
                    ps, empty = full(stage, n, t)
                    c0 = COLS.index((name, "f0"))
                    bias = cols_sb[:, c0:c0 + CH].rearrange("p (c o) -> p c o", o=1).broadcast_to([P, CH, P])
                    if i > 2:
                        dve.wait_ge(gated_ready, i - 2)
                    v.tensor_tensor(hid[:, (i - 1) % 2], ps.rearrange("p (c q) -> p c q", c=CH), bias, ALU.add).then_inc(empty, 1)
                elif stage == "gate":
                    i = NTH[stage, n, t]
                    j = (i - 1) % 2
                    dve.wait_ge(tanh_ready, i)
                    v.scalar_tensor_tensor(hid_act[:, j], hid_act[:, j], 1.0, hid[:, j], ALU.add, ALU.mult).then_inc(gated_ready, 1)
                elif stage == "fc2":
                    ps, empty = full(stage, n, t)
                    dve.wait_ge(xbias_ready, NTH_XB[n, t])
                    v.scalar_tensor_tensor(x_sb[:, t, :], ps[:, 0:D], 0.5, xbias[:, t, :], ALU.mult, ALU.add).then_inc(empty, 1)
                elif stage == "route":
                    ps, empty = full(stage, n, t)
                    j = t % 2
                    lg = logits[:, t, :]
                    v.tensor_tensor(lg, ps[:, 0:EXPERTS], rows_sb[:, ROW_ROUTER:ROW_ROUTER + EXPERTS], ALU.add).then_inc(empty, 1)
                    dve.wait_ge(empty, bank_use(stage, n, t)[1] + 1)
                    mine = lg.rearrange("p (e o) -> p e o", o=1).broadcast_to([P, EXPERTS, EXPERTS])
                    other = lg.rearrange("p (o f) -> p o f", o=1).broadcast_to([P, EXPERTS, EXPERTS])
                    link(v.tensor_tensor(cmp_eq[:, j], other, mine, ALU.is_equal))
                    link(v.tensor_tensor(cmp_gt[:, j], other, mine, ALU.is_gt))
                    link(v.tensor_tensor(cmp_eq[:, j], cmp_eq[:, j], const("before8").rearrange("p (e f) -> p e f", e=EXPERTS), ALU.mult))
                    link(v.tensor_tensor(cmp_gt[:, j], cmp_gt[:, j], cmp_eq[:, j], ALU.add))
                    link(v.tensor_reduce(rank8[:, t, :], cmp_gt[:, j], AX_X, ALU.add))
                    link(v.tensor_reduce(top[:, t, :], lg, AX_X, ALU.max))
                    v.tensor_scalar(gate_e[:, t, :], lg, top[:, t, :], None, ALU.subtract).then_inc(logits_shifted, 1)
                    dve.wait_ge(gate_exp, t + 1)
                    link(v.scalar_tensor_tensor(gates[:, t, :], rank8[:, t, :], 1.5, gate_e[:, t, :], ALU.is_lt, ALU.mult,
                                                accum_out=gate_s[:, t, 0:1]))
                    link(v.reciprocal(gate_s[:, t, 1:2], gate_s[:, t, 0:1]))
                    v.tensor_scalar(gates[:, t, :], gates[:, t, :], gate_s[:, t, 1:2], None, ALU.mult).then_inc(gates_ready, 1)
                elif stage == "mixture_bias":
                    ps, empty = full(stage, n, t, 1)
                    v.tensor_tensor(mix[:, t, :], ps[:, 0:D], x_sb[:, t, :], ALU.add).then_inc(empty, 1)

            for r, (g, e) in enumerate(EXPERT_RUNS):
                dve.wait_ge(fc2_full[r % 2], r // 2 + 1)
                for k in range(GT):
                    t = g * GT + k
                    if e == 0:
                        j, count = bank_use("mixture_bias", MOE, t, 1)
                        dve.wait_ge(bank_empty[j], count + 1)
                    else:
                        dve.wait_ge(mixed, (r - 1) * GT + k + 1)
                    ins = v.scalar_tensor_tensor(mix[:, t, :], ps_turn[:, r % 2, k * P:(k + 1) * P], gates[:, t, e:e + 1],
                                                 mix[:, t, :], ALU.mult, ALU.add).then_inc(mixed, 1)

        @block.tensor
        def _(pe):
            def claim(stage, n, t, use=0):
                j, count = bank_use(stage, n, t, use)
                if count:
                    pe.wait_ge(bank_empty[j], count)
                return ps_work[:, j], bank_full[j]

            def emptied(stage, n, t, use=0):
                j, count = bank_use(stage, n, t, use)
                pe.wait_ge(bank_empty[j], count + 1)

            def source(n, t):
                kv = BLOCKS[n]["kv"]
                if kv != "self":
                    emptied("ctx_turn", 0, t, 0 if kv == "ctx" else 1)
                return feat[kv][:, t, :]

            pe.wait_ge(small_loaded, 80)
            for i, n in enumerate(BIASED):
                pe.wait_ge(bv_ready, i + 1)
                pe.wait_ge(w_loaded[BLOCKS[n]["name"]], 16)
                if i >= 2:
                    pe.wait_ge(bias_ready, i - 1)
                for h in range(2):
                    ins = nc.tensor.matmul(ps_turn[:, i % 2, 0:D], bv_wide[0:SEQ, h, :], weight(n, f"o{h}")[0:SEQ],
                                           start=(h == 0), stop=(h == 1))
                ins.then_inc(bias_full, 1)
            pe.wait_ge(bias_ready, len(BIASED))
            for stage, n, t in SCHEDULE:
                b = BLOCKS[n]
                if stage == "ctx_turn":
                    if t == 0:
                        pe.wait_ge(ctx_loaded, 16)
                    ps, ready = claim(stage, n, t, 0)
                    nc.tensor.transpose(ps[:, 0:P], ctx_sb[:, t, :], ident).then_inc(ready, 1)
                    pe.wait_ge(chat_ready, t + 1)
                    ps, ready = claim(stage, n, t, 1)
                    nc.tensor.transpose(ps[:, 0:P], ctx_hat[:, t, :], ident).then_inc(ready, 1)
                elif stage == "turn_h":
                    if b["ln"]:
                        pe.wait_ge(xhat_ready, NTH["ln", n, t])
                        src = xhat[:, t, :]
                    else:
                        residual_ready(pe, sems, n, t)
                        src = x_sb[:, t, :]
                    ps, ready = claim(stage, n, t)
                    nc.tensor.transpose(ps[:, 0:P], src, ident).then_inc(ready, 1)
                elif stage == "topk":
                    pe.wait_ge(diag_ready, t + 1)
                    ps, ready = claim(stage, n, t)
                    nc.tensor.matmul(ps[:, 0:SEQ], const("same_seq"), score_diag[:, t % 2], start=True, stop=True).then_inc(ready, 1)
                elif stage == "qk":
                    emptied("turn_h", n, t)
                    src_kv = source(n, t)
                    pe.wait_ge(w_loaded[b["name"]], 16)
                    ps, ready = claim(stage, n, t)
                    for i, w in enumerate(qkv_order(n)):
                        src = src_kv if w[0] == "k" else feat["self"][:, t, :]
                        ins = nc.tensor.matmul(ps[:, i * P:(i + 1) * P], weight(n, w), src, start=True, stop=True)
                    ins.then_inc(ready, 1)
                elif stage == "values":
                    src_kv = source(n, t)
                    ps, ready = claim(stage, n, t)
                    for s in range(2):
                        for e in range(2):
                            ins = nc.tensor.matmul(ps[e * SEQ:(e + 1) * SEQ, s * SEQ:(s + 1) * SEQ], src_kv[:, s * SEQ:(s + 1) * SEQ],
                                                   weight(n, "v")[:, e * SEQ:(e + 1) * SEQ], start=True, stop=True)
                    ins.then_inc(ready, 1)
                elif stage == "scores":
                    i = NTH[stage, n, t]
                    j = i % 2
                    pe.wait_ge(keys_ready, NTH["qk", n, t])
                    if b.get("rope"):
                        pe.wait_ge(q_roped, NTH_ROPE[n, t])
                    else:
                        emptied("qk", n, t)
                    if i > 2:
                        pe.wait_ge(shifted, i - 2)
                    if b.get("causal"):
                        pe.wait_ge(setup_done, 2)
                    for s in range(2):
                        dst = ps_scores[:, 2 * j + s, :]
                        if b.get("causal"):
                            mask = causal16[:, :].rearrange("p (o k) -> p o k", o=1).broadcast_to([P, SLOTS, SEQ])
                            nc.tensor.matmul(dst, ident16[:, :], mask, start=True, stop=False)
                        ins = nc.tensor.matmul(dst, q_blocks[:, t, s].rearrange("p h q -> p (h q)"),
                                               key_blocks[:, t, s].rearrange("p h k -> p (h k)"),
                                               start=not b.get("causal"), stop=True)
                    ins.then_inc(scores_ready, 1)
                elif stage == "turn_p":
                    i = NTH[stage, n, t]
                    pe.wait_ge(probs_ready, i)
                    for half in range(2):
                        if i > 1:
                            pe.wait_ge(turned_out, 2 * (i - 2) + half + 1)
                        for g in range(4):
                            pair = probs[:, i % 2, 8 * half + 2 * g:8 * half + 2 * g + 2, :].rearrange("p h k -> p (h k)")
                            ins = nc.tensor.transpose(ps_turn[:, half, g * P:(g + 1) * P], pair, ident)
                        ins.then_inc(turned, 1)
                elif stage == "pv":
                    i = NTH[stage, n, t]
                    emptied("values", n, t)
                    pe.wait_ge(turned_out, 2 * i)
                    ps, ready = claim(stage, n, t)
                    for g in range(PAIRS):
                        ins = nc.tensor.matmul(ps[:, g * 4 * VW:(g + 1) * 4 * VW], probs_t[:, i % 2, g, :],
                                               value_blocks[:, t, g // SP, :, g % SP].rearrange("p h e v -> p h (e v)"), start=True, stop=True)
                    ins.then_inc(ready, 1)
                elif stage == "turn_o":
                    emptied("pv", n, t)
                    ps, ready = claim(stage, n, t)
                    nc.tensor.transpose(ps[:, 0:P], onorm[:, t, :], ident).then_inc(ready, 1)
                elif stage == "update":
                    emptied("turn_o", n, t)
                    ps, ready = claim(stage, n, t)
                    for h in range(2):
                        ins = nc.tensor.matmul(ps[:, 0:D], o_blocks[:, t, h].rearrange("p s q -> p (s q)"), weight(n, f"o{h}"),
                                               start=(h == 0), stop=(h == 1))
                    ins.then_inc(ready, 1)
                elif stage == "hidden":
                    emptied("turn_h", n, t)
                    pe.wait_ge(w_loaded[b["name"]], 16)
                    m = 0 if b["name"] == "ff0" else 1
                    ps, ready = claim(stage, n, t)
                    for c in range(CH):
                        ins = nc.tensor.matmul(ps[:, c * P:(c + 1) * P], mlp_sb[:, m, 0, c * P:(c + 1) * P], feat["self"][:, t, :],
                                               start=True, stop=True)
                    ins.then_inc(ready, 1)
                elif stage == "fc2":
                    m = 0 if b["name"] == "ff0" else 1
                    pe.wait_ge(gated_ready, NTH["gate", n, t])
                    ps, ready = claim(stage, n, t)
                    for c in range(CH):
                        ins = nc.tensor.matmul(ps[:, 0:D], hid_act[:, (NTH["gate", n, t] - 1) % 2, c, :],
                                               mlp_sb[:, m, 1, c * D:(c + 1) * D], start=(c == 0), stop=(c == CH - 1))
                    ins.then_inc(ready, 1)
                elif stage == "route":
                    emptied("turn_h", n, t)
                    ps, ready = claim(stage, n, t)
                    nc.tensor.matmul(ps[:, 0:EXPERTS], feat["self"][:, t, :], router_sb[:, :], start=True, stop=True).then_inc(ready, 1)
                elif stage == "mixture_bias":
                    pe.wait_ge(gates_ready, t + 1)
                    ps, ready = claim(stage, n, t, 0)
                    nc.tensor.transpose(ps[0:EXPERTS, 0:P], gates[:, t, :], ident).then_inc(ready, 1)
                    emptied(stage, n, t, 0)
                    ps, ready = claim(stage, n, t, 1)
                    nc.tensor.matmul(ps[:, 0:D], gates_t[:, t, :], moe_b2_sb[:, :], start=True, stop=True).then_inc(ready, 1)

            pe.wait_ge(w_loaded["moe"], 32)
            pe.wait_ge(shifted, NTH["scores", ATTNS[-1], TILES - 1])
            pe.wait_ge(turned_out, 2 * len(ATTNS) * TILES)
            for r in range(len(EXPERT_RUNS) + 1):
                if r < len(EXPERT_RUNS):
                    g, e = EXPERT_RUNS[r]
                    for c in range(CH):
                        if r:
                            pe.wait_ge(fc1_empty[c], r)
                        nc.tensor.matmul(ps_scores[:, c, :], moe1_sb[:, e, c * P:(c + 1) * P],
                                         feat["self"][:, g * GT:(g + 1) * GT, :], start=True, stop=True).then_inc(fc1_full[c], 1)
                if r:
                    q = r - 1
                    g, e = EXPERT_RUNS[q]
                    pe.wait_ge(fc1_empty[CH - 1], q + 1)
                    if q >= 2:
                        pe.wait_ge(mixed, (q - 1) * GT)
                    for k in range(GT):
                        for c in range(CH):
                            ins = nc.tensor.matmul(ps_turn[:, q % 2, k * P:(k + 1) * P], hidden_e[:, q % 2, c, k * P:(k + 1) * P],
                                                   moe2_sb[:, e, c, :], start=(c == 0), stop=(c == CH - 1))
                    ins.then_inc(fc2_full[q % 2], 1)


NTH_ROPE = {}
NTH_XB = {}
for _s, _b, _t in SCHEDULE:
    if _s == "qk" and BLOCKS[_b].get("rope"):
        NTH_ROPE[_b, _t] = len(NTH_ROPE) + 1
    if _s == "turn_h" and BLOCKS[_b]["kind"] != "moe":
        NTH_XB[_b, _t] = len(NTH_XB) + 1


def shape_constants():
    import numpy as np

    c = np.zeros((P, CONST_N), np.float32)

    def put(name, a):
        at, width = CONSTS[name]
        c[:, at:at + width] = a

    p = np.arange(P)
    put("ident", np.eye(P))
    put("same_seq", (p[:, None] // SEQ) == (p[None, :] // SEQ))
    k = np.arange(SEQ)
    put("fold", (p[:, None] % SEQ) == k)
    put("before", k < (p[:, None] % SEQ))
    put("slot", (p[:, None] // HD % SLOTS) == np.arange(SLOTS))
    put("causal", np.where(k > (p[:, None] % SEQ), -1e30, 0.0))
    half = HD // 2
    inv = (1.0 / 10000.0 ** (np.arange(0, HD, 2, dtype=np.float32) / HD)).astype(np.float32)
    angle = np.outer(inv[p % half], np.arange(SEQ, dtype=np.float32)).astype(np.float32)
    cos, sin = np.cos(angle), np.sin(angle) * np.where(p % HD < half, -1.0, 1.0)[:, None]
    put("cos", np.concatenate([cos * SCALE, cos], 1))
    put("sin", np.concatenate([sin * SCALE, sin], 1))
    e = np.arange(EXPERTS)
    put("before8", np.broadcast_to((e[None, :] < e[:, None]).reshape(-1), (P, EXPERTS * EXPERTS)))
    return c


def kernel(**inputs):
    import numpy as np
    import concourse.bacc as bacc
    from concourse.bass_utils import run_bass_kernel_spmd

    a = {k: np.asarray(v) for k, v in inputs.items()}
    p = np.arange(D)
    partner = p // HD * HD + (p % HD + HD // 2) % HD

    by_parity = p.reshape(PAIRS, 2, HD).transpose(1, 0, 2).reshape(-1)

    def split3(w):
        return w[0:D], w[D:2 * D], w[2 * D:3 * D]

    w, c, r = {}, {}, {}
    for name, pre in (("sa0", "L0_xattn_sa_"), ("ca0", "L0_xattn_ca_")):
        for x in "qkvo":
            w[name, x] = a[pre + "w" + x]
            if x in "qk":
                w[name, x + "r"] = a[pre + "w" + x][:, partner]
                c[name, "b" + x], c[name, "b" + x + "r"] = a[pre + "b" + x], a[pre + "b" + x][partner]
        c[name, "bv"], r[name, "bo"] = a[pre + "bv"], a[pre + "bo"]
    kv1 = a["L1_xattn_Wkv"]
    w["ca1", "q"], w["ca1", "k"], w["ca1", "v"], w["ca1", "o"] = (
        a["L1_xattn_Wq"].T, kv1[0:D].T, kv1[D:2 * D].T, a["L1_xattn_Wo"].T)
    r["ca1", "bo"] = a["L1_xattn_bo"]
    for name, win, bin_, wout, bout in (("ca2", "L2_xattn_in_proj_w", "L2_xattn_in_proj_b", "L2_xattn_out_w", "L2_xattn_out_b"),
                                        ("sa3", "L3_xattn_sa_in_w", "L3_xattn_sa_in_b", "L3_xattn_sa_out_w", "L3_xattn_sa_out_b"),
                                        ("ca3", "L3_xattn_ca_in_w", "L3_xattn_ca_in_b", "L3_xattn_ca_out_w", "L3_xattn_ca_out_b")):
        for x, part, bias in zip("qkv", split3(a[win]), split3(a[bin_])):
            w[name, x], c[name, "b" + x] = part.T, bias
        w[name, "o"], r[name, "bo"] = a[wout].T, a[bout]
    for name, pre in (("sa0", "L0_xattn_ln1_"), ("ca0", "L0_xattn_ln2_"), ("ff0", "L0_xattn_ln3_"), ("ca1", "L1_xattn_ln_q_"),
                      ("ctx1", "L1_xattn_ln_kv_"), ("sa3", "L3_xattn_sa_ln_"), ("ca3", "L3_xattn_ca_q_ln_"),
                      ("ctx3", "L3_xattn_ca_kv_ln_"), ("moe", "L3_xattn_moe_ln_")):
        c[name, "g"], c[name, "b"] = a[pre + "g"], a[pre + "b"]
    for name, b1, b2 in (("ff0", "L0_xattn_fc1_b", "L0_xattn_fc2_b"), ("ff1", "L1_xattn_b1", "L1_xattn_b2")):
        for i in range(CH):
            c[name, f"f{i}"] = a[b1][i * P:(i + 1) * P]
        r[name, "bo"] = a[b2]
    for e in range(EXPERTS):
        for i in range(CH):
            c["moe", f"f{e}_{i}"] = a["L3_xattn_e_fc1_b"][e, i * P:(i + 1) * P]
    r["ca2", "score"] = a["L2_xattn_score_w"][0]

    for name in {k[0] for k in w}:
        wo = w.pop((name, "o"))
        for h in range(2):
            half = slice(h * D // 2, (h + 1) * D // 2)
            w[name, f"o{h}"] = np.concatenate([wo[half], wo[half]], 0)
            if (name, "bv") in c:
                c[name, f"bv{h}"] = np.concatenate([c[name, "bv"][half]] * 2)

    def hidden_major(w2):
        return w2.reshape(CH, P, D).transpose(1, 0, 2).reshape(P, CH * D)

    mlp = np.stack([np.stack([a["L0_xattn_fc1_w"], hidden_major(a["L0_xattn_fc2_w"])], 1),
                    np.stack([a["L1_xattn_W1"].T, hidden_major(a["L1_xattn_W2"].T)], 1)], 1)
    arrays = {
        "x": a["x"].reshape(SEQS * SEQ, D),
        "ctx": a["ctx_1024"].reshape(SEQS * SEQ, D),
        "weights": np.stack([w[k][:, by_parity] if k[1] == "v" else w[k] for k in WEIGHTS], 1),
        "mlp_w": mlp,
        "moe_w1": a["L3_xattn_e_fc1_w"].transpose(2, 0, 1),
        "moe_w2": a["L3_xattn_e_fc2_w"].transpose(2, 0, 1).reshape(CH, P, EXPERTS, D).transpose(1, 2, 0, 3),
        "moe_b2": a["L3_xattn_e_fc2_b"],
        "router_w": a["L3_xattn_router_w"].T,
        "cols": np.stack([c[k] for k in COLS], 1),
        "rows": np.concatenate([r[k] for k in ROWS] + [a["L3_xattn_router_b"], a["L2_xattn_score_b"]])[None, :],
        "consts": shape_constants(),
    }
    nc = bacc.Bacc("TRN2", target_bir_lowering=False, num_devices=1)
    args = []
    feed = {}
    for name, array in arrays.items():
        feed[f"in_{name}"] = np.ascontiguousarray(array)
        args.append(nc.dram_tensor(f"in_{name}", array.shape, F32, kind="ExternalInput").ap())
    args.append(nc.dram_tensor("out", [SEQS * SEQ, D], F32, kind="ExternalOutput").ap())
    build(nc, *args)
    got = run_bass_kernel_spmd(nc, [feed], core_ids=[0])
    return got.results[0]["out"].reshape(SEQS, SEQ, D)
```

```python
from contextlib import ExitStack

import concourse.bass as bass
from concourse import mybir

ALU = mybir.AluOpType
ACT = mybir.ActivationFunctionType
AX_X = mybir.AxisListType.X
F32 = mybir.dt.float32
BF16 = mybir.dt.bfloat16

P = 128
D = 128
SEQS, SEQ = 16, 64
TILES = SEQS * SEQ // P
HEADS, HD = 16, 8
PAIRS = HEADS // 2
SLOTS = HEADS // 2
SP = SLOTS // 2
VW = HD + 1
FF = 512
CH = FF // P
EXPERTS = 8
TOPK = 10
LN_EPS = 1e-5
SCALE = HD ** -0.5
GELU_C = 0.7978845608028654
GELU_A = 0.044715

BLOCKS = [
    dict(name="sa0", kind="attn", ln=True, rope=True, kv="self", causal=True),
    dict(name="ca0", kind="attn", ln=True, rope=True, kv="ctx"),
    dict(name="ff0", kind="mlp", ln=True, act="gelu"),
    dict(name="ca1", kind="attn", ln=True, kv="ctx1", nobias=True),
    dict(name="ff1", kind="mlp", ln=False, act="silu"),
    dict(name="ca2", kind="attn", ln=False, kv="ctx", topk=True),
    dict(name="sa3", kind="attn", ln=True, kv="self"),
    dict(name="ca3", kind="attn", ln=True, kv="ctx3"),
    dict(name="moe", kind="moe", ln=True),
]
NB = len(BLOCKS)
LNS = [n for n, b in enumerate(BLOCKS) if b["ln"]]

WEIGHTS = []
for _b in BLOCKS:
    if _b["kind"] == "attn":
        WEIGHTS += [(_b["name"], w) for w in (("q", "qr", "k", "kr", "v", "o0", "o1") if _b.get("rope") else ("q", "k", "v", "o0", "o1"))]
COLS = []
for _b in BLOCKS:
    if _b["ln"]:
        COLS += [(_b["name"], "g"), (_b["name"], "b")]
    if _b["kind"] == "attn" and not _b.get("nobias"):
        COLS += [(_b["name"], c) for c in (("bq", "bqr", "bk", "bkr", "bv0", "bv1") if _b.get("rope") else ("bq", "bk", "bv0", "bv1"))]
    if _b["kind"] == "mlp":
        COLS += [(_b["name"], f"f{c}") for c in range(CH)]
COLS += [("ctx1", "g"), ("ctx1", "b"), ("ctx3", "g"), ("ctx3", "b")]
COLS += [("moe", f"f{e}_{c}") for e in range(EXPERTS) for c in range(CH)]
ROWS = [(b["name"], "bo") for b in BLOCKS if b["kind"] != "moe"] + [("ca2", "score")]
ROW_ROUTER = len(ROWS) * D
ROW_SCORE_B = ROW_ROUTER + EXPERTS
ROW_N = ROW_SCORE_B + 1
CONSTS, _at = {}, 0
for _n, _w in (("ident", P), ("same_seq", P), ("fold", SEQ), ("before", SEQ), ("causal", SEQ), ("slot", SLOTS),
               ("cos", 2 * SEQ), ("sin", 2 * SEQ), ("before8", EXPERTS * EXPERTS)):
    CONSTS[_n] = (_at, _w)
    _at += _w
CONST_N = _at

STEPS = {
    "ctx_stats": ("dve", 330, (), ()),
    "ctx_root": ("pool", 650, (), ()),
    "ctx_apply": ("dve", 180, (), ()),
    "ctx_turn": ("pe", 150, ("bank",), ()),
    "ctx_copy": ("act", 350, (), ("bank",)),
    "hat_turn": ("pe", 150, ("bank",), ()),
    "hat_copy": ("act", 600, (), ("bank",)),
    "wide_bias": ("dve", 300, ("wide",), ()),
    "bias_out": ("pe", 500, ("bank",), ("wide",)),
    "add_bias": ("dve", 220, (), ("bank",)),
    "stats": ("dve", 330, (), ()),
    "root": ("pool", 650, (), ()),
    "apply": ("dve", 180, (), ()),
    "turn_h": ("pe", 150, ("bank",), ()),
    "copy_h": ("act", 350, (), ("bank",)),
    "xbias": ("pool", 420, (), ()),
    "score": ("dve", 500, (), ()),
    "rank_spread": ("pe", 250, ("bank",), ()),
    "rank": ("dve", 900, (), ("bank",)),
    "qk": ("pe", 440, ("bank",), ()),
    "copy_qk": ("dve", 750, (), ("bank",)),
    "qk_rope": ("pe", 880, ("bank", "rope"), ()),
    "copy_rope": ("dve", 1050, (), ("bank",)),
    "rope_q": ("dve", 420, (), ()),
    "rope_k": ("pool", 420, (), ("rope",)),
    "keys": ("pool", 1850, (), ()),
    "values": ("pe", 450, ("bank",), ()),
    "copy_v": ("act", 320, (), ("bank",)),
    "scores": ("pe", 1720, ("scores",), ()),
    "shift": ("dve", 2300, ("probs",), ("scores",)),
    "exp": ("act", 950, (), ()),
    "turn_p0": ("pe", 570, ("bank",), ()),
    "turn_p1": ("pe", 570, ("bank",), ("probs",)),
    "copy_p0": ("act", 480, ("probs_t",), ("bank",)),
    "copy_p1": ("act", 480, (), ("bank",)),
    "pv": ("pe", 470, ("bank",), ("probs_t",)),
    "norm": ("dve", 850, (), ("bank",)),
    "turn_o": ("pe", 150, ("bank", "o"), ()),
    "copy_o": ("act", 320, (), ("bank",)),
    "project": ("pe", 430, ("bank",), ("o",)),
    "add_o": ("dve", 220, (), ("bank",)),
    "hidden": ("pe", 870, ("bank", "hid"), ()),
    "add_b": ("dve", 600, (), ("bank",)),
    "square": ("act", 450, (), ()),
    "cubic": ("pool", 2500, (), ()),
    "tanh": ("act", 520, (), ()),
    "gate": ("dve", 600, (), ()),
    "fc2": ("pe", 870, ("bank",), ("hid",)),
    "add_f": ("dve", 220, (), ("bank",)),
    "route": ("pe", 220, ("bank",), ()),
    "rank_e": ("dve", 900, (), ("bank",)),
    "exp_e": ("act", 120, (), ()),
    "gates": ("dve", 330, (), ()),
    "turn_g": ("pe", 150, ("bank",), ()),
    "copy_g": ("act", 200, (), ("bank",)),
    "mix_bias": ("pe", 220, ("bank",), ()),
    "add_m": ("dve", 220, (), ("bank",)),
    "expert_in0": ("pe", 1720, ("scores", "hidden_e"), ()),
    "expert_in1": ("pe", 1720, ("scores",), ()),
    "gelu0": ("act", 1140, (), ("scores",)),
    "gelu1": ("act", 1140, (), ("scores",)),
    "expert_out": ("pe", 3450, ("bank",), ("hidden_e",)),
    "mix_in": ("dve", 1050, (), ("bank",)),
}
BUFFERS = {"wide": 2, "bank": 4, "scores": 2, "probs": 2, "probs_t": 2, "hid": 2, "rope": 2, "o": 4, "hidden_e": 2}
TAKER = {("bias_out", "wide"): "wide_bias", ("add_bias", "bank"): "bias_out",
         ("ctx_copy", "bank"): "ctx_turn", ("hat_copy", "bank"): "hat_turn", ("copy_h", "bank"): "turn_h",
         ("rank", "bank"): "rank_spread", ("copy_qk", "bank"): "qk", ("copy_rope", "bank"): "qk_rope",
         ("rope_k", "rope"): "qk_rope", ("copy_v", "bank"): "values", ("shift", "scores"): "scores",
         ("copy_p0", "bank"): "turn_p0", ("copy_p1", "bank"): "turn_p1", ("turn_p1", "probs"): "shift",
         ("pv", "probs_t"): "copy_p0", ("norm", "bank"): "pv", ("copy_o", "bank"): "turn_o",
         ("project", "o"): "turn_o", ("add_o", "bank"): "project", ("add_b", "bank"): "hidden", ("add_f", "bank"): "fc2", ("fc2", "hid"): "hidden",
         ("rank_e", "bank"): "route", ("copy_g", "bank"): "turn_g", ("add_m", "bank"): "mix_bias",
         ("gelu0", "scores"): "expert_in0", ("gelu1", "scores"): "expert_in1",
         ("expert_out", "hidden_e"): "expert_in0", ("mix_in", "bank"): "expert_out"}
ENGINES = ("pe", "dve", "act", "pool")
HOP = 130
SAME = 20
TABLES = {"exp": 0, "exp_e": 0, "tanh": 0, "gelu0": 1, "gelu1": 1}
TABLE_LOAD = 1300
ATTNS = [n for n, b in enumerate(BLOCKS) if b["kind"] == "attn"]
MOE = NB - 1
BIASED = [n for n in ATTNS if not BLOCKS[n].get("nobias")]
BIAS_FREE = next(n for n in ATTNS if BLOCKS[n].get("nobias"))
GROUPS = 2
GT = TILES // GROUPS
EXPERT_RUNS = [(g, e) for g in range(GROUPS) for e in range(EXPERTS)]


def list_steps():
    steps = {}

    def add(step, n, t, *after):
        steps[step, n, t] = [k for k in after if k]

    for t in range(TILES):
        add("ctx_stats", 0, t)
        add("ctx_root", 0, t, ("ctx_stats", 0, t))
        add("ctx_apply", 0, t, ("ctx_root", 0, t))
        add("ctx_turn", 0, t)
        add("ctx_copy", 0, t, ("ctx_turn", 0, t))
        add("hat_turn", 0, t, ("ctx_apply", 0, t))
        add("hat_copy", 0, t, ("hat_turn", 0, t))
        updated, last_attn = None, None
        for n, b in enumerate(BLOCKS):
            if b["ln"]:
                add("stats", n, t, updated)
                add("root", n, t, ("stats", n, t))
                add("apply", n, t, ("root", n, t))
            add("turn_h", n, t, ("apply", n, t) if b["ln"] else updated)
            add("copy_h", n, t, ("turn_h", n, t))
            if b["kind"] == "moe":
                for step, before in (("route", "copy_h"), ("rank_e", "route"), ("exp_e", "rank_e"), ("gates", "exp_e"),
                                     ("turn_g", "gates"), ("copy_g", "turn_g"), ("mix_bias", "copy_g"), ("add_m", "mix_bias")):
                    add(step, n, t, (before, n, t))
                continue
            if b.get("topk"):
                add("score", n, t, updated)
                add("rank_spread", n, t, ("score", n, t))
                add("rank", n, t, ("rank_spread", n, t))
            if n in BIASED and t == 0:
                add("wide_bias", n, 0, ("turn_h", n, 0))
                add("bias_out", n, 0, ("wide_bias", n, 0))
                add("add_bias", n, 0, ("bias_out", n, 0))
            add("xbias", n, t, ("rank", n, t) if b.get("topk") else updated, ("turn_h", n, t),
                n in BIASED and ("add_bias", n, 0))
            if b["kind"] == "mlp":
                add("hidden", n, t, ("copy_h", n, t))
                add("add_b", n, t, ("hidden", n, t))
                if b["act"] == "gelu":
                    add("square", n, t, ("add_b", n, t))
                    add("cubic", n, t, ("square", n, t))
                add("tanh", n, t, ("cubic" if b["act"] == "gelu" else "add_b", n, t))
                add("gate", n, t, ("tanh", n, t))
                add("fc2", n, t, ("gate", n, t))
                add("add_f", n, t, ("fc2", n, t), ("xbias", n, t))
                updated = ("add_f", n, t)
                continue
            kv = {"self": ("copy_h", n, t), "ctx": ("ctx_copy", 0, t)}.get(b["kv"], ("hat_copy", 0, t))
            keys_read = last_attn is not None and ("scores", last_attn, t)
            values_read = last_attn is not None and ("pv", last_attn, t)
            if b.get("rope"):
                add("qk_rope", n, t, ("copy_h", n, t), kv)
                add("copy_rope", n, t, ("qk_rope", n, t), keys_read, ("ctx_apply", 0, t), ("ctx_turn", 0, t))
                add("rope_q", n, t, ("copy_rope", n, t))
                add("rope_k", n, t, ("rope_q", n, t))
            else:
                add("qk", n, t, ("copy_h", n, t), kv)
                add("copy_qk", n, t, ("qk", n, t), keys_read)
            add("keys", n, t, ("rope_k" if b.get("rope") else "copy_qk", n, t))
            add("values", n, t, kv, values_read)
            add("copy_v", n, t, ("values", n, t))
            add("scores", n, t, ("keys", n, t))
            for step, before in (("shift", "scores"), ("exp", "shift"), ("turn_p0", "exp"), ("turn_p1", "turn_p0"), ("copy_p0", "turn_p0")):
                add(step, n, t, (before, n, t))
            add("copy_p1", n, t, ("turn_p1", n, t), ("copy_p0", n, t))
            add("pv", n, t, ("copy_p1", n, t), ("copy_v", n, t))
            add("norm", n, t, ("pv", n, t), ("hat_turn", 0, t))
            for step, before in (("turn_o", "norm"), ("copy_o", "turn_o"), ("project", "copy_o")):
                add(step, n, t, (before, n, t))
            add("add_o", n, t, ("project", n, t), ("xbias", n, t))
            updated, last_attn = ("add_o", n, t), n
    for r, (g, e) in enumerate(EXPERT_RUNS):
        tiles = range(g * GT, (g + 1) * GT)
        add("expert_in0", MOE, r, *[("copy_h", MOE, t) for t in tiles])
        add("gelu0", MOE, r, ("expert_in0", MOE, r))
        add("expert_in1", MOE, r, ("expert_in0", MOE, r))
        add("gelu1", MOE, r, ("expert_in1", MOE, r), ("gelu0", MOE, r))
        add("expert_out", MOE, r, ("gelu1", MOE, r))
        add("mix_in", MOE, r, ("expert_out", MOE, r), *([("mix_in", MOE, r - 1)] if e else [("add_m", MOE, t) for t in tiles]))
    return steps


def urgency(key):
    step, n, t = key
    return (NB if step in ("expert_in0", "expert_in1", "gelu0", "gelu1", "expert_out", "mix_in") else n, t)


def arrange():
    after = list_steps()
    waiting = {e: [k for k in after if STEPS[k[0]][0] == e] for e in ENGINES}
    order = {e: [] for e in ENGINES}
    clock = {e: 0 for e in ENGINES}
    free = {b: [(0, i) for i in range(count)] for b, count in BUFFERS.items()}
    end, index, freed_by, last_freed, table = {}, {}, {}, {}, 0
    while any(waiting.values()):
        choices = []
        for e in ENGINES:
            mine = []
            for k in waiting[e]:
                takes = STEPS[k[0]][2]
                if all(d in end for d in after[k]) and all(free[b] for b in takes):
                    at = max([clock[e]] + [end[d] + (SAME if STEPS[d[0]][0] == e else HOP) for d in after[k]]
                             + [min(free[b])[0] + HOP for b in takes])
                    load = TABLE_LOAD if TABLES.get(k[0], table) != table else 0
                    mine.append((at + load, urgency(k), at, load, k))
            if mine:
                _, _, at, load, k = min(mine)
                choices.append((at, e, load, k))
        at, e, load, k = min(choices)
        _, length, takes, frees = STEPS[k[0]]
        for b in takes:
            use = min(free[b])
            free[b].remove(use)
            index[k, b] = use[1]
            freed_by[k, b] = last_freed.get((b, use[1]))
        end[k] = clock[e] = at + load + length
        if k[0] in TABLES:
            table = TABLES[k[0]]
        for b in frees:
            i = index[(TAKER[k[0], b],) + k[1:], b]
            free[b].append((end[k], i))
            last_freed[b, i] = k
        waiting[e].remove(k)
        order[e].append(k)
    return order, index, freed_by


ORDER, INDEX, FREED_BY = arrange()
NTH = {}
for _e in ENGINES:
    _runs = {}
    for _k in ORDER[_e]:
        _runs[_k[0]] = NTH[_k] = _runs.get(_k[0], 0) + 1


def build(nc, x_in, ctx_in, weights, mlp_w, moe_w1, moe_w2, moe_b2, router_w, cols, rows, consts, out):
    with ExitStack() as ctx:
        def sb(name, shape, dt=F32):
            return ctx.enter_context(nc.sbuf_tensor(name, shape, dt))

        def sem(name):
            return ctx.enter_context(nc.semaphore(name))

        w_sb = sb("w_sb", [P, len(WEIGHTS), D])
        mlp_sb = sb("mlp_sb", [P, 2, 2, FF])
        moe1_sb = sb("moe1_sb", [P, EXPERTS, FF])
        moe2_sb = sb("moe2_sb", [P, EXPERTS, CH, D])
        moe_b2_sb = sb("moe_b2_sb", [EXPERTS, D])
        router_sb = sb("router_sb", [P, EXPERTS])
        cols_sb = sb("cols_sb", [P, len(COLS)])
        rows_sb = sb("rows_sb", [P, ROW_N])
        const_sb = sb("const_sb", [P, CONST_N])
        ident16 = sb("ident16", [P, P], BF16)
        causal16 = sb("causal16", [P, SEQ], BF16)
        bv_wide = sb("bv_wide", [P, BUFFERS["wide"], 2, P])
        out_bias = sb("out_bias", [P, len(ATTNS), D])
        minus_half = sb("minus_half", [P, 1])
        x_sb = sb("x_sb", [P, TILES, D])
        ctx_sb = sb("ctx_sb", [P, TILES, D])
        ctx_hat = sb("ctx_hat", [P, TILES, D])
        feat = {k: sb(f"feat_{k}", [P, TILES, P]) for k in ("self", "ctx", "ctx1", "ctx3")}
        xhat = sb("xhat", [P, TILES, D])
        xbias = xhat
        stats = sb("stats", [P, TILES, 6])
        moments = sb("moments", [P, TILES, 2])
        varp = sb("varp", [P, TILES, 1])
        rstd = sb("rstd", [P, TILES, 1])
        cstats = sb("cstats", [P, TILES, 6])
        cmoments = sb("cmoments", [P, TILES, 2])
        cvarp = sb("cvarp", [P, TILES, 1])
        crstd = sb("crstd", [P, TILES, 1])
        k_feat = ctx_sb
        q_blocks = sb("q_blocks", [P, TILES, 2, 2, SEQ])
        rope_a = sb("rope_a", [P, BUFFERS["rope"], 2, P])
        rope_b = sb("rope_b", [P, BUFFERS["rope"], 2, P])
        key_blocks = sb("key_blocks", [P, TILES, 2, SLOTS, SEQ])
        value_blocks = sb("value_blocks", [P, TILES, 2, 2, SP, 2, VW])
        row_max = sb("row_max", [P, TILES, HEADS])
        probs = sb("probs", [P, BUFFERS["probs"], HEADS, SEQ])
        probs_t = sb("probs_t", [P, BUFFERS["probs_t"], PAIRS, P])
        rden = sb("rden", [P, TILES, HEADS])
        onorm = ctx_hat
        o_blocks = sb("o_blocks", [P, BUFFERS["o"], 2, 2, SEQ])
        score_junk = sb("score_junk", [P, D])
        score = sb("score", [P, TILES, 2])
        score_diag = sb("score_diag", [P, TILES, SEQ])
        rank_junk = sb("rank_junk", [P, 3, SEQ])
        rank = sb("rank", [P, TILES, 4])
        chosen = sb("chosen", [P, TILES, 2])
        chosen_bias = sb("chosen_bias", [P, D])
        hid = sb("hid", [P, BUFFERS["hid"], CH, P])
        hid_act = sb("hid_act", [P, BUFFERS["hid"], CH, P])
        logits = sb("logits", [P, TILES, EXPERTS])
        cmp_gt = sb("cmp_gt", [P, 2, EXPERTS, EXPERTS])
        cmp_eq = sb("cmp_eq", [P, 2, EXPERTS, EXPERTS])
        rank8 = sb("rank8", [P, TILES, EXPERTS])
        top = sb("top", [P, TILES, 1])
        gate_e = sb("gate_e", [P, TILES, EXPERTS])
        gate_s = sb("gate_s", [P, TILES, 2])
        gates = sb("gates", [P, TILES, EXPERTS])
        gates_t = feat["ctx1"][0:EXPERTS]
        hidden_e = sb("hidden_e", [P, BUFFERS["hidden_e"], CH, GT * P])
        mix = feat["ctx"]

        ps_scores = ctx.enter_context(nc.psum_tensor("ps_scores", [P, BUFFERS["scores"], 2, 512], F32))
        ps_bank = ctx.enter_context(nc.psum_tensor("ps_bank", [P, BUFFERS["bank"], 512], F32))

        x_loaded, ctx_loaded = sem("x_loaded"), sem("ctx_loaded")
        consts_loaded, cols_loaded, rows_loaded = sem("consts_loaded"), sem("cols_loaded"), sem("rows_loaded")
        w_loaded = {b["name"]: sem(f"w_loaded_{b['name']}") for b in BLOCKS}
        ones_made, mask_made, zeros_made = sem("ones_made"), sem("mask_made"), sem("zeros_made")
        dve_chain = sem("dve_chain")
        pool_chain = sem("pool_chain")
        finished = {s: sem(f"finished_{s}") for s in STEPS}
        out_done = sem("out_done")

        def weight(n, which):
            return w_sb[:, WEIGHTS.index((BLOCKS[n]["name"], which)), :]

        def col(name, which):
            i = COLS.index((name, which))
            return cols_sb[:, i:i + 1]

        def row(name, which):
            i = ROWS.index((name, which)) * D
            return rows_sb[:, i:i + D]

        def const(name):
            at, width = CONSTS[name]
            return const_sb[:, at:at + width]

        ident = const("ident")

        def done(eng, step, n, t):
            eng.wait_ge(finished[step], NTH[step, n, t])

        def take(eng, buffer, step, n, t):
            freeing = FREED_BY[(step, n, t), buffer]
            if freeing:
                done(eng, *freeing)
            return INDEX[(step, n, t), buffer]

        def held(buffer, step, n, t):
            return INDEX[(step, n, t), buffer]

        def bank(step, n, t):
            return ps_bank[:, held("bank", step, n, t), :]

        def residual(eng, n, t):
            if n == 0:
                eng.wait_ge(x_loaded, 16)
            else:
                done(eng, "add_o" if BLOCKS[n - 1]["kind"] == "attn" else "add_f", n - 1, t)

        block = ctx.enter_context(nc.Block())

        @block.sync
        def _(sp):
            sp.dma_start(const_sb[:, :], consts).then_inc(consts_loaded, 16)
            sp.dma_start(x_sb[:, :, :], x_in.rearrange("(t p) d -> p t d", p=P)).then_inc(x_loaded, 16)
            sp.dma_start(cols_sb[:, :], cols).then_inc(cols_loaded, 16)
            at = 0
            m = 0
            for b in BLOCKS:
                if b["kind"] == "attn":
                    k = sum(w[0] == b["name"] for w in WEIGHTS)
                    sp.dma_start(w_sb[:, at:at + k, :], weights[:, at:at + k, :]).then_inc(w_loaded[b["name"]], 16)
                    at += k
                elif b["kind"] == "mlp":
                    sp.dma_start(mlp_sb[:, m], mlp_w[:, m]).then_inc(w_loaded[b["name"]], 16)
                    m += 1
                if b["name"] == "sa0":
                    sp.dma_start(rows_sb[:, :], rows.broadcast_to([P, ROW_N])).then_inc(rows_loaded, 16)
                    sp.dma_start(ctx_sb[:, :, :], ctx_in.rearrange("(t p) d -> p t d", p=P)).then_inc(ctx_loaded, 16)
            sp.dma_start(router_sb[:, :], router_w).then_inc(w_loaded["moe"], 16)
            sp.dma_start(moe_b2_sb[:, :], moe_b2).then_inc(w_loaded["moe"], 16)
            sp.dma_start(moe1_sb[:, :, :], moe_w1).then_inc(w_loaded["moe"], 16)
            sp.dma_start(moe2_sb[:, :, :, :], moe_w2).then_inc(w_loaded["moe"], 16)
            for g in range(GROUPS):
                done(sp, "mix_in", MOE, g * EXPERTS + EXPERTS - 1)
                part = slice(g * GT * P, (g + 1) * GT * P)
                sp.dma_start(out[part, :].rearrange("(t p) d -> p t d", p=P), mix[:, g * GT:(g + 1) * GT, :]).then_inc(out_done, 16)
            sp.wait_ge(out_done, 16 * GROUPS)

        @block.gpsimd
        def _(pool):
            chain = [0]

            def link(ins):
                chain[0] += 1
                ins.then_inc(pool_chain, 1)
                pool.wait_ge(pool_chain, chain[0])

            link(pool.memset(minus_half[:, :], -0.5))
            for buffer in (q_blocks, o_blocks):
                pool.memset(buffer[:, :, :, :, :].rearrange("p t a b q -> p (t a b q)"), 0.0).then_inc(zeros_made, 1)
            pool.wait_ge(consts_loaded, 16)

            for step, n, t in ORDER["pool"]:
                b = BLOCKS[n]
                if step in ("ctx_root", "root"):
                    if step == "root":
                        done(pool, "stats", n, t)
                        variance, var_eps, inverse_root = moments[:, t, 1:2], varp[:, t, :], rstd[:, t, :]
                    else:
                        done(pool, "ctx_stats", n, t)
                        variance, var_eps, inverse_root = cmoments[:, t, 1:2], cvarp[:, t, :], crstd[:, t, :]
                    link(pool.tensor_scalar(var_eps, variance, LN_EPS, None, ALU.add))
                    pool.tensor_tensor(inverse_root, var_eps, minus_half[:, :], ALU.pow).then_inc(finished[step], 1)
                elif step == "xbias":
                    if b.get("topk"):
                        done(pool, "rank", n, t)
                        done(pool, "turn_h", n, t)
                        done(pool, "add_bias", n, 0)
                        keep = chosen[:, t, 1:2].broadcast_to([P, D])
                        take_bias = chosen[:, t, 0:1].broadcast_to([P, D])
                        link(pool.tensor_tensor(xbias[:, t, :], x_sb[:, t, :], keep, ALU.mult))
                        link(pool.tensor_tensor(chosen_bias[:, :], out_bias[:, ATTNS.index(n), :], take_bias, ALU.mult))
                        pool.tensor_tensor(xbias[:, t, :], xbias[:, t, :], chosen_bias[:, :], ALU.add).then_inc(finished[step], 1)
                    else:
                        residual(pool, n, t)
                        done(pool, "turn_h", n, t)
                        if n in BIASED:
                            done(pool, "add_bias", n, 0)
                            bias = out_bias[:, ATTNS.index(n), :]
                        else:
                            pool.wait_ge(rows_loaded, 16)
                            bias = row(b["name"], "bo")
                        pool.tensor_tensor(xbias[:, t, :], x_sb[:, t, :], bias, ALU.add).then_inc(finished[step], 1)
                elif step == "rope_k":
                    i = held("rope", "qk_rope", n, t)
                    done(pool, "copy_rope", n, t)
                    done(pool, "rope_q", n, t)
                    pool.tensor_tensor(k_feat[:, t, :], rope_a[:, i, 1], rope_b[:, i, 1], ALU.add).then_inc(finished[step], 1)
                elif step == "keys":
                    done(pool, "rope_k" if b.get("rope") else "copy_qk", n, t)
                    spread = k_feat[:, t, :].rearrange("p (b o k) -> p b o k", b=2, o=1).broadcast_to([P, 2, SLOTS, SEQ])
                    mask = const("slot").rearrange("p (b s o) -> p b s o", b=1, o=1).broadcast_to([P, 2, SLOTS, SEQ])
                    pool.tensor_tensor(key_blocks[:, t], spread, mask, ALU.mult).then_inc(finished[step], 1)
                elif step == "cubic":
                    i = held("hid", "hidden", n, t)
                    done(pool, "square", n, t)
                    link(pool.tensor_tensor(hid_act[:, i], hid_act[:, i], hid[:, i], ALU.mult))
                    pool.tensor_tensor(hid_act[:, i], hid_act[:, i], hid[:, i], ALU.add).then_inc(finished[step], 1)

        @block.scalar
        def _(act):
            act.wait_ge(cols_loaded, 16)

            def affine(out, in_, g, b):
                return nc.scalar.activation(out, in_, ACT.Identity, bias=b, scale=g)

            for step, n, t in ORDER["act"]:
                b = BLOCKS[n]
                name = b["name"]
                if step == "ctx_copy":
                    done(act, "ctx_turn", n, t)
                    nc.scalar.copy(feat["ctx"][:, t, :], bank("ctx_turn", n, t)[:, 0:P]).then_inc(finished[step], 1)
                elif step == "hat_copy":
                    done(act, "hat_turn", n, t)
                    ps = bank("hat_turn", n, t)[:, 0:P]
                    affine(feat["ctx1"][:, t, :], ps, col("ctx1", "g"), col("ctx1", "b"))
                    affine(feat["ctx3"][:, t, :], ps, col("ctx3", "g"), col("ctx3", "b")).then_inc(finished[step], 1)
                elif step == "copy_h":
                    done(act, "turn_h", n, t)
                    ps = bank("turn_h", n, t)[:, 0:P]
                    if b["ln"]:
                        affine(feat["self"][:, t, :], ps, col(name, "g"), col(name, "b")).then_inc(finished[step], 1)
                    else:
                        nc.scalar.copy(feat["self"][:, t, :], ps).then_inc(finished[step], 1)
                elif step == "copy_v":
                    done(act, "values", n, t)
                    if n == 0:
                        act.wait_ge(ones_made, 1)
                    ps = bank("values", n, t)
                    for e in range(2):
                        r = slice(e * SEQ, (e + 1) * SEQ)
                        dst = value_blocks[r, t, :, :, :, e, 0:HD].rearrange("p s h j d -> p (s h j) d")
                        last = nc.scalar.copy(dst, ps[r, 0:D].rearrange("p (g d) -> p g d", d=HD))
                    last.then_inc(finished[step], 1)
                elif step == "exp":
                    done(act, "shift", n, t)
                    flat = probs[:, held("probs", "shift", n, t)].rearrange("p h k -> p (h k)")
                    nc.scalar.activation(flat, flat, ACT.Exp).then_inc(finished[step], 1)
                elif step == "copy_p0":
                    done(act, "turn_p0", n, t)
                    i = take(act, "probs_t", step, n, t)
                    nc.scalar.copy(probs_t[:, i, 0:4, :].rearrange("p g q -> p (g q)"), bank("turn_p0", n, t)).then_inc(finished[step], 1)
                elif step == "copy_p1":
                    done(act, "turn_p1", n, t)
                    i = held("probs_t", "copy_p0", n, t)
                    nc.scalar.copy(probs_t[:, i, 4:8, :].rearrange("p g q -> p (g q)"), bank("turn_p1", n, t)).then_inc(finished[step], 1)
                elif step == "copy_o":
                    done(act, "turn_o", n, t)
                    if n == 0:
                        act.wait_ge(zeros_made, 2)
                    ps = bank("turn_o", n, t)
                    i = held("o", "turn_o", n, t)
                    for s in range(2):
                        r = slice(s * SEQ, (s + 1) * SEQ)
                        last = nc.scalar.copy(o_blocks[r, i, :, s, :], ps[r, 0:P].rearrange("p (h q) -> p h q", h=2))
                    last.then_inc(finished[step], 1)
                elif step == "square":
                    done(act, "add_b", n, t)
                    i = held("hid", "hidden", n, t)
                    nc.scalar.activation(hid_act[:, i], hid[:, i], ACT.Square, scale=GELU_A ** 0.5).then_inc(finished[step], 1)
                elif step == "tanh":
                    i = held("hid", "hidden", n, t)
                    if b["act"] == "gelu":
                        done(act, "cubic", n, t)
                        src, scale = hid_act[:, i], GELU_C
                    else:
                        done(act, "add_b", n, t)
                        src, scale = hid[:, i], 0.5
                    nc.scalar.activation(hid_act[:, i], src, ACT.Tanh, scale=scale).then_inc(finished[step], 1)
                elif step == "exp_e":
                    done(act, "rank_e", n, t)
                    nc.scalar.activation(gate_e[:, t, :], gate_e[:, t, :], ACT.Exp).then_inc(finished[step], 1)
                elif step == "copy_g":
                    done(act, "turn_g", n, t)
                    nc.scalar.copy(gates_t[:, t, :], bank("turn_g", n, t)[0:EXPERTS, 0:P]).then_inc(finished[step], 1)
                elif step in ("gelu0", "gelu1"):
                    half = int(step[-1])
                    done(act, f"expert_in{half}", n, t)
                    g, e = EXPERT_RUNS[t]
                    i = held("hidden_e", "expert_in0", n, t)
                    j = held("scores", f"expert_in{half}", n, t)
                    for c in range(2):
                        ins = nc.scalar.activation(hidden_e[:, i, 2 * half + c, :], ps_scores[:, j, c, :], ACT.Gelu,
                                                   bias=col("moe", f"f{e}_{2 * half + c}"))
                    ins.then_inc(finished[step], 1)

        @block.vector
        def _(dve):
            v = nc.vector
            chain = [0]

            def link(ins):
                chain[0] += 1
                ins.then_inc(dve_chain, 1)
                dve.wait_ge(dve_chain, chain[0])

            dve.wait_ge(consts_loaded, 16)
            link(v.tensor_copy(ident16[:, :], ident))
            v.tensor_copy(causal16[:, :], const("causal")).then_inc(mask_made, 1)
            link(v.memset(value_blocks[:, :, :, :, :, :, :].rearrange("p t s h j e v -> p (t s h j e v)"), 0.0))
            for e in range(2):
                r = slice(e * SEQ, (e + 1) * SEQ)
                ones = value_blocks[r, :, :, :, :, e, HD].rearrange("p t s h j -> p (t s h j)")
                if e == 0:
                    link(v.memset(ones, 1.0))
                else:
                    v.memset(ones, 1.0).then_inc(ones_made, 1)
            dve.wait_ge(cols_loaded, 16)

            for step, n, t in ORDER["dve"]:
                b = BLOCKS[n]
                name = b["name"]
                if step == "wide_bias":
                    i = take(dve, "wide", step, n, t)
                    for h in range(2):
                        ins = v.tensor_scalar(bv_wide[0:SEQ, i, h, :], const("same_seq")[0:SEQ], 0.0, col(name, f"bv{h}")[0:SEQ], ALU.mult, ALU.add)
                    ins.then_inc(finished[step], 1)
                elif step == "add_bias":
                    done(dve, "bias_out", n, t)
                    dve.wait_ge(rows_loaded, 16)
                    v.tensor_tensor(out_bias[:, ATTNS.index(n), :], bank("bias_out", n, t)[:, 0:D], row(name, "bo"), ALU.add).then_inc(finished[step], 1)
                elif step == "ctx_stats":
                    dve.wait_ge(ctx_loaded, 16)
                    link(v.bn_stats(cstats[:, t, :], ctx_sb[:, t, :]))
                    v.bn_aggr(cmoments[:, t, :], cstats[:, t, :]).then_inc(finished[step], 1)
                elif step == "ctx_apply":
                    done(dve, "ctx_stats", n, t)
                    done(dve, "ctx_root", n, t)
                    v.tensor_scalar(ctx_hat[:, t, :], ctx_sb[:, t, :], cmoments[:, t, 0:1], crstd[:, t, :],
                                    ALU.subtract, ALU.mult).then_inc(finished[step], 1)
                elif step == "stats":
                    residual(dve, n, t)
                    link(v.bn_stats(stats[:, t, :], x_sb[:, t, :]))
                    v.bn_aggr(moments[:, t, :], stats[:, t, :]).then_inc(finished[step], 1)
                elif step == "apply":
                    done(dve, "stats", n, t)
                    done(dve, "root", n, t)
                    v.tensor_scalar(xhat[:, t, :], x_sb[:, t, :], moments[:, t, 0:1], rstd[:, t, :],
                                    ALU.subtract, ALU.mult).then_inc(finished[step], 1)
                elif step == "score":
                    residual(dve, n, t)
                    dve.wait_ge(rows_loaded, 16)
                    link(v.scalar_tensor_tensor(score_junk[:, :], x_sb[:, t, :], 1.0, row("ca2", "score"), ALU.mult, ALU.mult,
                                                accum_out=score[:, t, 0:1]))
                    link(v.tensor_scalar(score[:, t, 1:2], score[:, t, 0:1], rows_sb[:, ROW_SCORE_B:ROW_SCORE_B + 1], None, ALU.add))
                    v.tensor_scalar(score_diag[:, t], const("fold"), score[:, t, 1:2], None, ALU.mult).then_inc(finished[step], 1)
                elif step == "rank":
                    done(dve, "rank_spread", n, t)
                    ps = bank("rank_spread", n, t)[:, 0:SEQ]
                    own, above, ties, total = (rank[:, t, i:i + 1] for i in range(4))
                    link(v.scalar_tensor_tensor(rank_junk[:, 0], ps, 1.0, const("fold"), ALU.mult, ALU.mult, accum_out=own))
                    link(v.tensor_scalar(rank_junk[:, 1], ps, own, 0.0, ALU.is_gt, ALU.add, accum_out=above))
                    link(v.scalar_tensor_tensor(rank_junk[:, 2], ps, own, const("before"), ALU.is_equal, ALU.mult, accum_out=ties))
                    link(v.tensor_tensor(total, above, ties, ALU.add))
                    link(v.tensor_scalar(chosen[:, t, 0:1], total, TOPK - 0.5, None, ALU.is_lt))
                    v.tensor_scalar(chosen[:, t, 1:2], chosen[:, t, 0:1], -1.0, 1.0, ALU.mult, ALU.add).then_inc(finished[step], 1)
                elif step == "copy_qk":
                    done(dve, "qk", n, t)
                    ps = bank("qk", n, t)
                    for h in range(2):
                        r = slice(h * SEQ, (h + 1) * SEQ)
                        src = ps[r, 0:P].rearrange("p (b s) -> p b s", b=2)
                        if b.get("nobias"):
                            v.tensor_scalar(q_blocks[r, t, :, h, :], src, SCALE, None, ALU.mult)
                        else:
                            v.tensor_scalar(q_blocks[r, t, :, h, :], src, col(name, "bq")[r], SCALE, ALU.add, ALU.mult)
                    if b.get("nobias"):
                        v.tensor_copy(k_feat[:, t, :], ps[:, P:2 * P]).then_inc(finished[step], 1)
                    else:
                        v.tensor_scalar(k_feat[:, t, :], ps[:, P:2 * P], col(name, "bk"), None, ALU.add).then_inc(finished[step], 1)
                elif step == "copy_rope":
                    done(dve, "qk_rope", n, t)
                    if n == 0:
                        done(dve, "ctx_apply", 0, t)
                        done(dve, "ctx_turn", 0, t)
                    i = held("rope", "qk_rope", n, t)
                    v4 = bank("qk_rope", n, t).rearrange("p (k b s) -> p k b s", k=4, b=2)
                    for table, first, dst, suffix in (("cos", 0, rope_a, ""), ("sin", 2, rope_b, "r")):
                        for k in range(2):
                            tab = const(table)[:, k * SEQ:(k + 1) * SEQ].rearrange("p (o s) -> p o s", o=1).broadcast_to([P, 2, SEQ])
                            ins = v.scalar_tensor_tensor(dst[:, i, k].rearrange("p (b s) -> p b s", b=2), v4[:, first + k],
                                                         col(name, "b" + "qk"[k] + suffix), tab, ALU.add, ALU.mult)
                    ins.then_inc(finished[step], 1)
                elif step == "rope_q":
                    done(dve, "copy_rope", n, t)
                    i = held("rope", "qk_rope", n, t)
                    if n == 0:
                        dve.wait_ge(zeros_made, 1)
                    for h in range(2):
                        r = slice(h * SEQ, (h + 1) * SEQ)
                        ins = v.tensor_tensor(q_blocks[r, t, :, h, :], rope_a[r, i, 0].rearrange("p (b s) -> p b s", b=2),
                                              rope_b[r, i, 0].rearrange("p (b s) -> p b s", b=2), ALU.add)
                    ins.then_inc(finished[step], 1)
                elif step == "shift":
                    done(dve, "scores", n, t)
                    s3 = ps_scores[:, held("scores", "scores", n, t)].rearrange("p g (h k) -> p (g h) k", k=SEQ)
                    link(v.tensor_reduce(row_max[:, t], s3, AX_X, ALU.max))
                    i = take(dve, "probs", step, n, t)
                    mx = row_max[:, t].rearrange("p (h o) -> p h o", o=1).broadcast_to([P, HEADS, SEQ])
                    v.tensor_tensor(probs[:, i], s3, mx, ALU.subtract).then_inc(finished[step], 1)
                elif step == "norm":
                    done(dve, "pv", n, t)
                    if n == 0:
                        done(dve, "hat_turn", 0, t)
                    ps = bank("pv", n, t)
                    o5 = ps[:, 0:PAIRS * 4 * VW].rearrange("p (g h e v) -> p g h e v", g=PAIRS, h=2, e=2)
                    for h in range(2):
                        r = slice(h * SEQ, (h + 1) * SEQ)
                        rd = rden[r, t, :].rearrange("p (g e) -> p g e", e=2)
                        v.reciprocal(rd, o5[r, :, h, :, HD]).then_inc(dve_chain, 1)
                        chain[0] += 1
                    dve.wait_ge(dve_chain, chain[0])
                    for h in range(2):
                        r = slice(h * SEQ, (h + 1) * SEQ)
                        rd = rden[r, t, :].rearrange("p (g e o) -> p g e o", e=2, o=1).broadcast_to([SEQ, PAIRS, 2, HD])
                        dst = onorm[r, t, :].rearrange("p (g e d) -> p g e d", e=2, d=HD)
                        ins = v.tensor_tensor(dst, o5[r, :, h, :, 0:HD], rd, ALU.mult)
                    ins.then_inc(finished[step], 1)
                elif step == "add_o":
                    done(dve, "project", n, t)
                    done(dve, "xbias", n, t)
                    ps = bank("project", n, t)[:, 0:D]
                    if b.get("topk"):
                        v.scalar_tensor_tensor(x_sb[:, t, :], ps, chosen[:, t, 0:1], xbias[:, t, :], ALU.mult, ALU.add).then_inc(finished[step], 1)
                    else:
                        v.tensor_tensor(x_sb[:, t, :], ps, xbias[:, t, :], ALU.add).then_inc(finished[step], 1)
                elif step == "add_b":
                    done(dve, "hidden", n, t)
                    c0 = COLS.index((name, "f0"))
                    bias = cols_sb[:, c0:c0 + CH].rearrange("p (c o) -> p c o", o=1).broadcast_to([P, CH, P])
                    v.tensor_tensor(hid[:, held("hid", "hidden", n, t)], bank("hidden", n, t).rearrange("p (c q) -> p c q", c=CH),
                                    bias, ALU.add).then_inc(finished[step], 1)
                elif step == "gate":
                    done(dve, "tanh", n, t)
                    i = held("hid", "hidden", n, t)
                    v.scalar_tensor_tensor(hid_act[:, i], hid_act[:, i], 1.0, hid[:, i], ALU.add, ALU.mult).then_inc(finished[step], 1)
                elif step == "add_f":
                    done(dve, "fc2", n, t)
                    done(dve, "xbias", n, t)
                    v.scalar_tensor_tensor(x_sb[:, t, :], bank("fc2", n, t)[:, 0:D], 0.5, xbias[:, t, :], ALU.mult, ALU.add).then_inc(finished[step], 1)
                elif step == "rank_e":
                    done(dve, "route", n, t)
                    j = t % 2
                    lg = logits[:, t, :]
                    link(v.tensor_tensor(lg, bank("route", n, t)[:, 0:EXPERTS], rows_sb[:, ROW_ROUTER:ROW_ROUTER + EXPERTS], ALU.add))
                    mine = lg.rearrange("p (e o) -> p e o", o=1).broadcast_to([P, EXPERTS, EXPERTS])
                    other = lg.rearrange("p (o f) -> p o f", o=1).broadcast_to([P, EXPERTS, EXPERTS])
                    link(v.tensor_tensor(cmp_eq[:, j], other, mine, ALU.is_equal))
                    link(v.tensor_tensor(cmp_gt[:, j], other, mine, ALU.is_gt))
                    link(v.tensor_tensor(cmp_eq[:, j], cmp_eq[:, j], const("before8").rearrange("p (e f) -> p e f", e=EXPERTS), ALU.mult))
                    link(v.tensor_tensor(cmp_gt[:, j], cmp_gt[:, j], cmp_eq[:, j], ALU.add))
                    link(v.tensor_reduce(rank8[:, t, :], cmp_gt[:, j], AX_X, ALU.add))
                    link(v.tensor_reduce(top[:, t, :], lg, AX_X, ALU.max))
                    v.tensor_scalar(gate_e[:, t, :], lg, top[:, t, :], None, ALU.subtract).then_inc(finished[step], 1)
                elif step == "gates":
                    done(dve, "exp_e", n, t)
                    link(v.scalar_tensor_tensor(gates[:, t, :], rank8[:, t, :], 1.5, gate_e[:, t, :], ALU.is_lt, ALU.mult,
                                                accum_out=gate_s[:, t, 0:1]))
                    link(v.reciprocal(gate_s[:, t, 1:2], gate_s[:, t, 0:1]))
                    v.tensor_scalar(gates[:, t, :], gates[:, t, :], gate_s[:, t, 1:2], None, ALU.mult).then_inc(finished[step], 1)
                elif step == "add_m":
                    done(dve, "mix_bias", n, t)
                    v.tensor_tensor(mix[:, t, :], bank("mix_bias", n, t)[:, 0:D], x_sb[:, t, :], ALU.add).then_inc(finished[step], 1)
                elif step == "mix_in":
                    done(dve, "expert_out", n, t)
                    g, e = EXPERT_RUNS[t]
                    if e:
                        done(dve, "mix_in", n, t - 1)
                    for k in range(GT):
                        u = g * GT + k
                        if e == 0:
                            done(dve, "add_m", n, u)
                        ins = v.scalar_tensor_tensor(mix[:, u, :], bank("expert_out", n, t)[:, k * P:(k + 1) * P], gates[:, u, e:e + 1],
                                                     mix[:, u, :], ALU.mult, ALU.add)
                    ins.then_inc(finished[step], 1)

        @block.tensor
        def _(pe):
            def source(n, t):
                kv = BLOCKS[n]["kv"]
                if kv == "self":
                    done(pe, "copy_h", n, t)
                else:
                    done(pe, "ctx_copy" if kv == "ctx" else "hat_copy", 0, t)
                return feat[kv][:, t, :]

            pe.wait_ge(consts_loaded, 16)
            for step, n, t in ORDER["pe"]:
                b = BLOCKS[n]
                if "bank" in STEPS[step][2]:
                    ps = ps_bank[:, take(pe, "bank", step, n, t), :]
                if step == "bias_out":
                    done(pe, "wide_bias", n, t)
                    pe.wait_ge(w_loaded[b["name"]], 16)
                    i = held("wide", "wide_bias", n, t)
                    for h in range(2):
                        ins = nc.tensor.matmul(ps[:, 0:D], bv_wide[0:SEQ, i, h, :], weight(n, f"o{h}")[0:SEQ], start=(h == 0), stop=(h == 1))
                    ins.then_inc(finished[step], 1)
                elif step == "ctx_turn":
                    pe.wait_ge(ctx_loaded, 16)
                    nc.tensor.transpose(ps[:, 0:P], ctx_sb[:, t, :], ident).then_inc(finished[step], 1)
                elif step == "hat_turn":
                    done(pe, "ctx_apply", n, t)
                    nc.tensor.transpose(ps[:, 0:P], ctx_hat[:, t, :], ident).then_inc(finished[step], 1)
                elif step == "turn_h":
                    if b["ln"]:
                        done(pe, "apply", n, t)
                        src = xhat[:, t, :]
                    else:
                        residual(pe, n, t)
                        src = x_sb[:, t, :]
                    nc.tensor.transpose(ps[:, 0:P], src, ident).then_inc(finished[step], 1)
                elif step == "rank_spread":
                    done(pe, "score", n, t)
                    nc.tensor.matmul(ps[:, 0:SEQ], const("same_seq"), score_diag[:, t], start=True, stop=True).then_inc(finished[step], 1)
                elif step in ("qk", "qk_rope"):
                    done(pe, "copy_h", n, t)
                    src_kv = source(n, t)
                    pe.wait_ge(w_loaded[b["name"]], 16)
                    if step == "qk_rope":
                        take(pe, "rope", step, n, t)
                    for i, w in enumerate(["q", "k", "qr", "kr"] if step == "qk_rope" else ["q", "k"]):
                        src = src_kv if w[0] == "k" else feat["self"][:, t, :]
                        ins = nc.tensor.matmul(ps[:, i * P:(i + 1) * P], weight(n, w), src, start=True, stop=True)
                    ins.then_inc(finished[step], 1)
                elif step == "values":
                    src_kv = source(n, t)
                    pe.wait_ge(w_loaded[b["name"]], 16)
                    for s in range(2):
                        for e in range(2):
                            ins = nc.tensor.matmul(ps[e * SEQ:(e + 1) * SEQ, s * SEQ:(s + 1) * SEQ], src_kv[:, s * SEQ:(s + 1) * SEQ],
                                                   weight(n, "v")[:, e * SEQ:(e + 1) * SEQ], start=True, stop=True)
                    ins.then_inc(finished[step], 1)
                elif step == "scores":
                    done(pe, "keys", n, t)
                    done(pe, "rope_q" if b.get("rope") else "copy_qk", n, t)
                    j = take(pe, "scores", step, n, t)
                    if b.get("causal"):
                        pe.wait_ge(mask_made, 1)
                    for s in range(2):
                        dst = ps_scores[:, j, s, :]
                        if b.get("causal"):
                            mask = causal16[:, :].rearrange("p (o k) -> p o k", o=1).broadcast_to([P, SLOTS, SEQ])
                            nc.tensor.matmul(dst, ident16[:, :], mask, start=True, stop=False)
                        ins = nc.tensor.matmul(dst, q_blocks[:, t, s].rearrange("p h q -> p (h q)"),
                                               key_blocks[:, t, s].rearrange("p h k -> p (h k)"),
                                               start=not b.get("causal"), stop=True)
                    ins.then_inc(finished[step], 1)
                elif step in ("turn_p0", "turn_p1"):
                    half = int(step[-1])
                    done(pe, "exp", n, t)
                    i = held("probs", "shift", n, t)
                    for g in range(4):
                        pair = probs[:, i, 8 * half + 2 * g:8 * half + 2 * g + 2, :].rearrange("p h k -> p (h k)")
                        ins = nc.tensor.transpose(ps[:, g * P:(g + 1) * P], pair, ident)
                    ins.then_inc(finished[step], 1)
                elif step == "pv":
                    done(pe, "copy_v", n, t)
                    done(pe, "copy_p1", n, t)
                    i = held("probs_t", "copy_p0", n, t)
                    for g in range(PAIRS):
                        ins = nc.tensor.matmul(ps[:, g * 4 * VW:(g + 1) * 4 * VW], probs_t[:, i, g, :],
                                               value_blocks[:, t, g // SP, :, g % SP].rearrange("p h e v -> p h (e v)"), start=True, stop=True)
                    ins.then_inc(finished[step], 1)
                elif step == "turn_o":
                    done(pe, "norm", n, t)
                    take(pe, "o", step, n, t)
                    nc.tensor.transpose(ps[:, 0:P], onorm[:, t, :], ident).then_inc(finished[step], 1)
                elif step == "project":
                    done(pe, "copy_o", n, t)
                    i = held("o", "turn_o", n, t)
                    for h in range(2):
                        ins = nc.tensor.matmul(ps[:, 0:D], o_blocks[:, i, h].rearrange("p s q -> p (s q)"), weight(n, f"o{h}"),
                                               start=(h == 0), stop=(h == 1))
                    ins.then_inc(finished[step], 1)
                elif step == "hidden":
                    done(pe, "copy_h", n, t)
                    pe.wait_ge(w_loaded[b["name"]], 16)
                    take(pe, "hid", step, n, t)
                    m = 0 if b["name"] == "ff0" else 1
                    for c in range(CH):
                        ins = nc.tensor.matmul(ps[:, c * P:(c + 1) * P], mlp_sb[:, m, 0, c * P:(c + 1) * P], feat["self"][:, t, :],
                                               start=True, stop=True)
                    ins.then_inc(finished[step], 1)
                elif step == "fc2":
                    done(pe, "gate", n, t)
                    m = 0 if b["name"] == "ff0" else 1
                    for c in range(CH):
                        ins = nc.tensor.matmul(ps[:, 0:D], hid_act[:, held("hid", "hidden", n, t), c, :],
                                               mlp_sb[:, m, 1, c * D:(c + 1) * D], start=(c == 0), stop=(c == CH - 1))
                    ins.then_inc(finished[step], 1)
                elif step == "route":
                    done(pe, "copy_h", n, t)
                    pe.wait_ge(w_loaded["moe"], 64)
                    nc.tensor.matmul(ps[:, 0:EXPERTS], feat["self"][:, t, :], router_sb[:, :], start=True, stop=True).then_inc(finished[step], 1)
                elif step == "turn_g":
                    done(pe, "gates", n, t)
                    nc.tensor.transpose(ps[0:EXPERTS, 0:P], gates[:, t, :], ident).then_inc(finished[step], 1)
                elif step == "mix_bias":
                    done(pe, "copy_g", n, t)
                    nc.tensor.matmul(ps[:, 0:D], gates_t[:, t, :], moe_b2_sb[:, :], start=True, stop=True).then_inc(finished[step], 1)
                elif step in ("expert_in0", "expert_in1"):
                    half = int(step[-1])
                    g, e = EXPERT_RUNS[t]
                    pe.wait_ge(w_loaded["moe"], 64)
                    for u in range(g * GT, (g + 1) * GT):
                        done(pe, "copy_h", MOE, u)
                    if half == 0:
                        take(pe, "hidden_e", step, n, t)
                    j = take(pe, "scores", step, n, t)
                    for c in range(2):
                        at = (2 * half + c) * P
                        ins = nc.tensor.matmul(ps_scores[:, j, c, :], moe1_sb[:, e, at:at + P],
                                               feat["self"][:, g * GT:(g + 1) * GT, :], start=True, stop=True)
                    ins.then_inc(finished[step], 1)
                elif step == "expert_out":
                    done(pe, "gelu0", n, t)
                    done(pe, "gelu1", n, t)
                    g, e = EXPERT_RUNS[t]
                    i = held("hidden_e", "expert_in0", n, t)
                    for k in range(GT):
                        for c in range(CH):
                            ins = nc.tensor.matmul(ps[:, k * P:(k + 1) * P], hidden_e[:, i, c, k * P:(k + 1) * P],
                                                   moe2_sb[:, e, c, :], start=(c == 0), stop=(c == CH - 1))
                    ins.then_inc(finished[step], 1)


def shape_constants():
    import numpy as np

    c = np.zeros((P, CONST_N), np.float32)

    def put(name, a):
        at, width = CONSTS[name]
        c[:, at:at + width] = a

    p = np.arange(P)
    put("ident", np.eye(P))
    put("same_seq", (p[:, None] // SEQ) == (p[None, :] // SEQ))
    k = np.arange(SEQ)
    put("fold", (p[:, None] % SEQ) == k)
    put("before", k < (p[:, None] % SEQ))
    put("slot", (p[:, None] // HD % SLOTS) == np.arange(SLOTS))
    put("causal", np.where(k > (p[:, None] % SEQ), -1e30, 0.0))
    half = HD // 2
    inv = (1.0 / 10000.0 ** (np.arange(0, HD, 2, dtype=np.float32) / HD)).astype(np.float32)
    angle = np.outer(inv[p % half], np.arange(SEQ, dtype=np.float32)).astype(np.float32)
    cos, sin = np.cos(angle), np.sin(angle) * np.where(p % HD < half, -1.0, 1.0)[:, None]
    put("cos", np.concatenate([cos * SCALE, cos], 1))
    put("sin", np.concatenate([sin * SCALE, sin], 1))
    e = np.arange(EXPERTS)
    put("before8", np.broadcast_to((e[None, :] < e[:, None]).reshape(-1), (P, EXPERTS * EXPERTS)))
    return c


def kernel(**inputs):
    import numpy as np
    import concourse.bacc as bacc
    from concourse.bass_utils import run_bass_kernel_spmd

    a = {k: np.asarray(v) for k, v in inputs.items()}
    p = np.arange(D)
    partner = p // HD * HD + (p % HD + HD // 2) % HD

    by_parity = p.reshape(PAIRS, 2, HD).transpose(1, 0, 2).reshape(-1)

    def split3(w):
        return w[0:D], w[D:2 * D], w[2 * D:3 * D]

    w, c, r = {}, {}, {}
    for name, pre in (("sa0", "L0_xattn_sa_"), ("ca0", "L0_xattn_ca_")):
        for x in "qkvo":
            w[name, x] = a[pre + "w" + x]
            if x in "qk":
                w[name, x + "r"] = a[pre + "w" + x][:, partner]
                c[name, "b" + x], c[name, "b" + x + "r"] = a[pre + "b" + x], a[pre + "b" + x][partner]
        c[name, "bv"], r[name, "bo"] = a[pre + "bv"], a[pre + "bo"]
    kv1 = a["L1_xattn_Wkv"]
    w["ca1", "q"], w["ca1", "k"], w["ca1", "v"], w["ca1", "o"] = (
        a["L1_xattn_Wq"].T, kv1[0:D].T, kv1[D:2 * D].T, a["L1_xattn_Wo"].T)
    r["ca1", "bo"] = a["L1_xattn_bo"]
    for name, win, bin_, wout, bout in (("ca2", "L2_xattn_in_proj_w", "L2_xattn_in_proj_b", "L2_xattn_out_w", "L2_xattn_out_b"),
                                        ("sa3", "L3_xattn_sa_in_w", "L3_xattn_sa_in_b", "L3_xattn_sa_out_w", "L3_xattn_sa_out_b"),
                                        ("ca3", "L3_xattn_ca_in_w", "L3_xattn_ca_in_b", "L3_xattn_ca_out_w", "L3_xattn_ca_out_b")):
        for x, part, bias in zip("qkv", split3(a[win]), split3(a[bin_])):
            w[name, x], c[name, "b" + x] = part.T, bias
        w[name, "o"], r[name, "bo"] = a[wout].T, a[bout]
    for name, pre in (("sa0", "L0_xattn_ln1_"), ("ca0", "L0_xattn_ln2_"), ("ff0", "L0_xattn_ln3_"), ("ca1", "L1_xattn_ln_q_"),
                      ("ctx1", "L1_xattn_ln_kv_"), ("sa3", "L3_xattn_sa_ln_"), ("ca3", "L3_xattn_ca_q_ln_"),
                      ("ctx3", "L3_xattn_ca_kv_ln_"), ("moe", "L3_xattn_moe_ln_")):
        c[name, "g"], c[name, "b"] = a[pre + "g"], a[pre + "b"]
    for name, b1, b2 in (("ff0", "L0_xattn_fc1_b", "L0_xattn_fc2_b"), ("ff1", "L1_xattn_b1", "L1_xattn_b2")):
        for i in range(CH):
            c[name, f"f{i}"] = a[b1][i * P:(i + 1) * P]
        r[name, "bo"] = a[b2]
    for e in range(EXPERTS):
        for i in range(CH):
            c["moe", f"f{e}_{i}"] = a["L3_xattn_e_fc1_b"][e, i * P:(i + 1) * P]
    r["ca2", "score"] = a["L2_xattn_score_w"][0]

    for name in {k[0] for k in w}:
        wo = w.pop((name, "o"))
        for h in range(2):
            half = slice(h * D // 2, (h + 1) * D // 2)
            w[name, f"o{h}"] = np.concatenate([wo[half], wo[half]], 0)
            if (name, "bv") in c:
                c[name, f"bv{h}"] = np.concatenate([c[name, "bv"][half]] * 2)

    def hidden_major(w2):
        return w2.reshape(CH, P, D).transpose(1, 0, 2).reshape(P, CH * D)

    mlp = np.stack([np.stack([a["L0_xattn_fc1_w"], hidden_major(a["L0_xattn_fc2_w"])], 1),
                    np.stack([a["L1_xattn_W1"].T, hidden_major(a["L1_xattn_W2"].T)], 1)], 1)
    arrays = {
        "x": a["x"].reshape(SEQS * SEQ, D),
        "ctx": a["ctx_1024"].reshape(SEQS * SEQ, D),
        "weights": np.stack([w[k][:, by_parity] if k[1] == "v" else w[k] for k in WEIGHTS], 1),
        "mlp_w": mlp,
        "moe_w1": a["L3_xattn_e_fc1_w"].transpose(2, 0, 1),
        "moe_w2": a["L3_xattn_e_fc2_w"].transpose(2, 0, 1).reshape(CH, P, EXPERTS, D).transpose(1, 2, 0, 3),
        "moe_b2": a["L3_xattn_e_fc2_b"],
        "router_w": a["L3_xattn_router_w"].T,
        "cols": np.stack([c[k] for k in COLS], 1),
        "rows": np.concatenate([r[k] for k in ROWS] + [a["L3_xattn_router_b"], a["L2_xattn_score_b"]])[None, :],
        "consts": shape_constants(),
    }
    nc = bacc.Bacc("TRN2", target_bir_lowering=False, num_devices=1)
    args = []
    feed = {}
    for name, array in arrays.items():
        feed[f"in_{name}"] = np.ascontiguousarray(array)
        args.append(nc.dram_tensor(f"in_{name}", array.shape, F32, kind="ExternalInput").ap())
    args.append(nc.dram_tensor("out", [SEQS * SEQ, D], F32, kind="ExternalOutput").ap())
    build(nc, *args)
    got = run_bass_kernel_spmd(nc, [feed], core_ids=[0])
    return got.results[0]["out"].reshape(SEQS, SEQ, D)
```

```python
from contextlib import ExitStack

import concourse.bass as bass
from concourse import mybir

ALU = mybir.AluOpType
ACT = mybir.ActivationFunctionType
AX_X = mybir.AxisListType.X
F32 = mybir.dt.float32
BF16 = mybir.dt.bfloat16
F32R = mybir.dt.float32r

P = 128
D = 128
SEQS, SEQ = 16, 64
TILES = SEQS * SEQ // P
HEADS, HD = 16, 8
PAIRS = HEADS // 2
SLOTS = HEADS // 2
SP = SLOTS // 2
VB = 4 * HD
FF = 512
CH = FF // P
EXPERTS = 8
TOPK = 10
LN_EPS = 1e-5
SCALE = HD ** -0.5
GELU_C = 0.7978845608028654
GELU_A = 0.044715

BLOCKS = [
    dict(name="sa0", kind="attn", ln=True, rope=True, kv="self", causal=True),
    dict(name="ca0", kind="attn", ln=True, rope=True, kv="ctx"),
    dict(name="ff0", kind="mlp", ln=True, act="gelu"),
    dict(name="ca1", kind="attn", ln=True, kv="ctx1", nobias=True),
    dict(name="ff1", kind="mlp", ln=False, act="silu"),
    dict(name="ca2", kind="attn", ln=False, kv="ctx", topk=True),
    dict(name="sa3", kind="attn", ln=True, kv="self"),
    dict(name="ca3", kind="attn", ln=True, kv="ctx3"),
    dict(name="moe", kind="moe", ln=True),
]
NB = len(BLOCKS)

WEIGHTS = []
for _b in BLOCKS:
    if _b["kind"] == "attn":
        WEIGHTS += [(_b["name"], w) for w in (("q", "qr", "k", "kr", "v", "o") if _b.get("rope") else ("q", "k", "v", "o"))]
COLS = []
for _b in BLOCKS:
    if _b["ln"]:
        COLS += [(_b["name"], "g"), (_b["name"], "b")]
    if _b["kind"] == "attn" and not _b.get("nobias"):
        COLS += [(_b["name"], c) for c in (("bq", "bqr", "bk", "bkr", "bv") if _b.get("rope") else ("bq", "bk", "bv"))]
    if _b["kind"] == "mlp":
        COLS += [(_b["name"], f"f{c}") for c in range(CH)]
COLS += [("ctx1", "g"), ("ctx1", "b"), ("ctx3", "g"), ("ctx3", "b")]
COLS += [("moe", f"f{e}_{c}") for e in range(EXPERTS) for c in range(CH)]
ROWS = [(b["name"], "bo") for b in BLOCKS if b["kind"] != "moe"] + [("ca2", "score")]
ROW_ROUTER = len(ROWS) * D
ROW_SCORE_B = ROW_ROUTER + EXPERTS
ROW_N = ROW_SCORE_B + 1
CONSTS, _at = {}, 0
for _n, _w in (("ident", P), ("same_seq", P), ("fold", SEQ), ("before", SEQ), ("causal", SEQ), ("slot", SLOTS),
               ("cos", SEQ), ("sin", SEQ), ("half", 2), ("before8", EXPERTS * EXPERTS)):
    CONSTS[_n] = (_at, _w)
    _at += _w
CONST_N = _at

ACT_HEADS = 4

STEPS = {
    "ctx_stats": ("dve", 404, (), ()),
    "ctx_root": ("pool", 620, (), ()),
    "ctx_apply": ("dve", 256, (), ()),
    "ctx_turn": ("pe", 213, ("bank",), ()),
    "ctx_copy": ("act", 350, (), ("bank",)),
    "hat_turn": ("pe", 150, ("bank",), ()),
    "hat_copy": ("act", 600, (), ("bank",)),
    "wide_bias": ("dve", 200, ("wide",), ()),
    "wo_halves": ("pool", 800, (), ()),
    "bias_out": ("pe", 250, ("bank",), ("wide",)),
    "add_bias": ("dve", 220, (), ("bank",)),
    "stats": ("dve", 404, (), ()),
    "root": ("pool", 620, (), ()),
    "apply": ("dve", 256, (), ()),
    "turn_h": ("pe", 130, ("bank",), ()),
    "copy_h": ("act", 350, (), ("bank",)),
    "xbias": ("pool", 420, (), ()),
    "score": ("dve", 748, (), ()),
    "rank_spread": ("pe", 160, ("bank",), ()),
    "rank": ("dve", 1365, (), ("bank",)),
    "qk": ("pe", 440, ("bank",), ()),
    "copy_qk": ("act", 760, (), ("bank",)),
    "qk_rope": ("pe", 880, ("bank", "rope"), ()),
    "copy_rope": ("dve", 1050, (), ("bank",)),
    "rope_q": ("dve", 420, (), ()),
    "rope_k": ("pool", 420, (), ("rope",)),
    "keys": ("pool", 1855, (), ()),
    "values": ("pe", 320, ("bank",), ()),
    "copy_v": ("act", 320, (), ("bank",)),
    "scores": ("pe", 1720, ("scores",), ()),
    "shift": ("dve", 2450 - 67 * ACT_HEADS, ("probs",), ()),
    "exp": ("act", 950 + 232 * ACT_HEADS, (), ("scores",)),
    "total": ("dve", 1431 - 67 * ACT_HEADS, (), ()),
    "spread": ("pool", 600, ("spread",), ()),
    "turn_r": ("pe", 260, ("bank",), ("spread",)),
    "turn_p0": ("pe", 450, ("bank", "probs_t"), ()),
    "turn_p1": ("pe", 450, ("bank",), ("probs",)),
    "copy_p0": ("act", 480, (), ("bank",)),
    "copy_p1": ("act", 480, (), ("bank",)),
    "pv": ("pe", 620, ("bank", "o"), ("probs_t",)),
    "copy_o": ("act", 350, (), ("bank",)),
    "norm": ("dve", 340, (), ("bank",)),
    "project": ("pe", 440, ("bank",), ("o",)),
    "add_o": ("dve", 220, (), ("bank",)),
    "hidden": ("pe", 880, ("bank", "hid"), ()),
    "add_b": ("dve", 600, (), ("bank",)),
    "square": ("act", 520, (), ()),
    "cubic": ("pool", 2552, (), ()),
    "tanh": ("act", 520, (), ()),
    "gate": ("dve", 600, (), ()),
    "fc2": ("pe", 880, ("bank",), ("hid",)),
    "add_f": ("dve", 220, (), ("bank",)),
    "route": ("pe", 220, ("bank",), ()),
    "rank_e": ("dve", 1851, (), ("bank",)),
    "exp_e": ("act", 120, (), ()),
    "gates": ("dve", 539, (), ()),
    "turn_g": ("pe", 150, ("bank",), ()),
    "copy_g": ("act", 160, (), ("bank",)),
    "mix_bias": ("pe", 220, ("bank",), ()),
    "add_m": ("dve", 220, (), ("bank",)),
    "split_w": ("dve", 1010, (), ()),
    "split_h": ("dve", 420, (), ()),
    "expert_in0": ("pe", 1300, ("scores", "hidden_e"), ()),
    "expert_in1": ("pe", 1300, ("scores",), ()),
    "gelu0": ("act", 1140, (), ("scores",)),
    "gelu1": ("act", 1140, (), ("scores",)),
    "expert_out": ("pe", 3450, ("bank",), ("hidden_e",)),
    "mix_in": ("dve", 1052, (), ("bank",)),
}
BUFFERS = {"spread": 2, "wide": 1, "bank": 4, "scores": 2, "probs": 3, "probs_t": 2, "hid": 2, "rope": 2, "o": 3, "hidden_e": 2}
TAKER = {("bias_out", "wide"): "wide_bias", ("add_bias", "bank"): "bias_out",
         ("ctx_copy", "bank"): "ctx_turn", ("hat_copy", "bank"): "hat_turn", ("copy_h", "bank"): "turn_h",
         ("rank", "bank"): "rank_spread", ("copy_qk", "bank"): "qk", ("copy_rope", "bank"): "qk_rope",
         ("rope_k", "rope"): "qk_rope", ("copy_v", "bank"): "values", ("exp", "scores"): "scores",
         ("copy_p0", "bank"): "turn_p0", ("copy_p1", "bank"): "turn_p1", ("turn_p1", "probs"): "shift",
         ("pv", "probs_t"): "turn_p0", ("copy_o", "bank"): "pv", ("norm", "bank"): "turn_r", ("turn_r", "spread"): "spread",
         ("project", "o"): "pv", ("add_o", "bank"): "project", ("add_b", "bank"): "hidden", ("add_f", "bank"): "fc2", ("fc2", "hid"): "hidden",
         ("rank_e", "bank"): "route", ("copy_g", "bank"): "turn_g", ("add_m", "bank"): "mix_bias",
         ("gelu0", "scores"): "expert_in0", ("gelu1", "scores"): "expert_in1",
         ("expert_out", "hidden_e"): "expert_in0", ("mix_in", "bank"): "expert_out"}
ARRIVAL = {"stats": (4300, 4300, 6200, 6200, 6200, 6200, 6200, 6200), "ctx_stats": (10000,) * TILES, "ctx_turn": (10000,) * TILES}
ENGINES = ("pe", "dve", "act", "pool")
HOP = 130
SAME = 20
TABLES = {"exp": 0, "exp_e": 0, "tanh": 0, "gelu0": 1, "gelu1": 1}
TABLE_LOAD = 1300
TILE_STAGGER = 8300
TILE_LAG = 4000
HEAD_START = {
    "add_b": -2900, "add_bias": 15700, "add_f": 8300, "add_m": 23200, "add_o": 41600, "apply": -3600,
    "bias_out": 6300, "copy_g": -10100, "copy_h": -3100, "copy_o": 10600, "copy_p0": -12100, "copy_p1": -15000,
    "copy_qk": -1100, "copy_rope": -13700, "copy_v": -2400, "ctx_apply": 35100, "ctx_copy": 11300,
    "ctx_root": 19700, "ctx_stats": 2200, "ctx_turn": 20100, "cubic": -11000, "exp": -23100, "exp_e": 12900,
    "fc2": 74400, "gate": -1100, "gates": -19700, "hat_copy": 48600, "hat_turn": -32100, "hidden": 2700,
    "keys": -29800, "mix_bias": -20700, "norm": 22000, "project": -300, "pv": 2900, "qk": 30300, "qk_rope": -1200,
    "rank": -9600, "rank_e": -6700, "rank_spread": 6000, "root": -9600, "rope_k": -12600, "rope_q": -7000,
    "route": -36000, "score": 48100, "scores": -15300, "shift": -15100, "split_h": 2000, "split_w": -13000,
    "spread": -11800, "square": -34600, "stats": 3000, "tanh": -5700, "total": -12400, "turn_g": -66300,
    "turn_h": 12300, "turn_p0": 17400, "turn_p1": 2200, "turn_r": 1300, "values": 2300, "wide_bias": 7700,
    "wo_halves": -53800, "xbias": -1700,
}
EXPERT_RANK = 1
EXPERT_STEPS = ("expert_in0", "expert_in1", "gelu0", "gelu1", "expert_out", "mix_in")
ATTNS = [n for n, b in enumerate(BLOCKS) if b["kind"] == "attn"]
MOE = NB - 1
BIASED = [n for n in ATTNS if not BLOCKS[n].get("nobias")]
GROUPS = [range(0, 4), range(4, 8)]
GT = max(len(g) for g in GROUPS)
EXPERT_RUNS = [(g, e) for g in GROUPS for e in range(EXPERTS)]


def list_steps():
    steps = {}

    def add(step, n, t, *after):
        steps[step, n, t] = list(dict.fromkeys(k for k in after if k))

    for t in range(TILES):
        add("ctx_stats", 0, t)
        add("ctx_root", 0, t, ("ctx_stats", 0, t))
        add("ctx_apply", 0, t, ("ctx_root", 0, t))
        add("ctx_turn", 0, t)
        add("ctx_copy", 0, t, ("ctx_turn", 0, t))
        add("hat_turn", 0, t, ("ctx_apply", 0, t))
        add("hat_copy", 0, t, ("hat_turn", 0, t))
        updated, last_attn = None, None
        for n, b in enumerate(BLOCKS):
            if b["ln"]:
                add("stats", n, t, updated)
                add("root", n, t, ("stats", n, t))
                add("apply", n, t, ("root", n, t))
            add("turn_h", n, t, ("apply", n, t) if b["ln"] else updated)
            add("copy_h", n, t, ("turn_h", n, t))
            if b["kind"] == "moe":
                add("split_h", n, t, ("copy_h", n, t))
                for step, before in (("route", "copy_h"), ("rank_e", "route"), ("exp_e", "rank_e"), ("gates", "exp_e"),
                                     ("turn_g", "gates"), ("copy_g", "turn_g"), ("mix_bias", "copy_g"), ("add_m", "mix_bias")):
                    add(step, n, t, (before, n, t))
                continue
            if b.get("topk"):
                add("score", n, t, updated)
                add("rank_spread", n, t, ("score", n, t))
                add("rank", n, t, ("rank_spread", n, t))
            if n in BIASED and t == 0:
                add("wide_bias", n, 0, ("turn_h", n, 0))
                add("bias_out", n, 0, ("wide_bias", n, 0))
                add("add_bias", n, 0, ("bias_out", n, 0))
            add("xbias", n, t, ("rank", n, t) if b.get("topk") else updated, ("turn_h", n, t),
                n in BIASED and ("add_bias", n, 0))
            if b["kind"] == "mlp":
                add("hidden", n, t, ("copy_h", n, t))
                add("add_b", n, t, ("hidden", n, t))
                if b["act"] == "gelu":
                    add("square", n, t, ("add_b", n, t))
                    add("cubic", n, t, ("square", n, t))
                add("tanh", n, t, ("cubic" if b["act"] == "gelu" else "add_b", n, t))
                add("gate", n, t, ("tanh", n, t))
                add("fc2", n, t, ("gate", n, t))
                add("add_f", n, t, ("fc2", n, t), ("xbias", n, t))
                updated = ("add_f", n, t)
                continue
            kv = {"self": ("copy_h", n, t), "ctx": ("ctx_copy", 0, t)}.get(b["kv"], ("hat_copy", 0, t))
            keys_read = last_attn is not None and ("scores", last_attn, t)
            values_read = last_attn is not None and ("pv", last_attn, t)
            if b.get("rope"):
                add("qk_rope", n, t, ("copy_h", n, t), kv)
                add("copy_rope", n, t, ("qk_rope", n, t), keys_read, ("ctx_apply", 0, t), ("ctx_turn", 0, t))
                add("rope_q", n, t, ("copy_rope", n, t))
                add("rope_k", n, t, ("rope_q", n, t))
            else:
                add("qk", n, t, ("copy_h", n, t), kv)
                add("copy_qk", n, t, ("qk", n, t), keys_read)
            add("keys", n, t, ("rope_k" if b.get("rope") else "copy_qk", n, t))
            add("values", n, t, kv, values_read)
            add("copy_v", n, t, ("values", n, t))
            add("scores", n, t, ("keys", n, t))
            for step, before in (("shift", "scores"), ("exp", "shift"), ("total", "exp"), ("spread", "total"), ("turn_r", "spread"), ("turn_p0", "exp"), ("copy_p0", "turn_p0")):
                add(step, n, t, (before, n, t))
            add("turn_p1", n, t, ("turn_p0", n, t), ("total", n, t))
            add("copy_p1", n, t, ("turn_p1", n, t), ("copy_p0", n, t))
            add("pv", n, t, ("copy_p1", n, t), ("copy_v", n, t))
            add("copy_o", n, t, ("pv", n, t))
            add("norm", n, t, ("copy_o", n, t), ("turn_r", n, t))
            if t == 0:
                add("wo_halves", n, 0, ("turn_h", n, 0), n in BIASED and ("bias_out", n, 0))
            add("project", n, t, ("norm", n, t), ("wo_halves", n, 0))
            add("add_o", n, t, ("project", n, t), ("xbias", n, t))
            updated, last_attn = ("add_o", n, t), n
    for e in range(EXPERTS):
        add("split_w", MOE, e, ("scores", ATTNS[-1], e))
    for r, (g, e) in enumerate(EXPERT_RUNS):
        add("expert_in0", MOE, r, ("split_w", MOE, e), *[("split_h", MOE, t) for t in g])
        add("gelu0", MOE, r, ("expert_in0", MOE, r))
        add("expert_in1", MOE, r, ("expert_in0", MOE, r))
        add("gelu1", MOE, r, ("expert_in1", MOE, r), ("gelu0", MOE, r))
        add("expert_out", MOE, r, ("gelu1", MOE, r), *([("expert_out", MOE, r - 1)] if e else [("add_m", MOE, t) for t in g]))
        add("mix_in", MOE, r, ("expert_out", MOE, r), e and ("mix_in", MOE, r - 1))
    return steps


def arrange():
    after = list_steps()
    opens = {k: [] for k in after}
    for k, before in after.items():
        for d in before:
            opens[d].append(k)
    ahead = {}
    for k in reversed(list(after)):
        ahead[k] = STEPS[k[0]][1] + max((ahead[o] + HOP for o in opens[k]), default=0)
    rank = {}
    for k in after:
        lag = k[2] * TILE_LAG + (k[2] >= TILES // 2) * TILE_STAGGER
        rank[k] = EXPERT_RANK if k[0] in EXPERT_STEPS else lag - ahead[k] - HEAD_START.get(k[0], 0)
    blocked = {k: len(before) for k, before in after.items()}
    ready = {e: {} for e in ENGINES}
    for k in after:
        if not blocked[k]:
            ready[STEPS[k[0]][0]][k] = ARRIVAL[k[0]][k[2]]
    order = {e: [] for e in ENGINES}
    clock = {e: 0 for e in ENGINES}
    free = {b: [(0, i) for i in range(count)] for b, count in BUFFERS.items()}
    end, index, freed_by, last_freed, table = {}, {}, {}, {}, 0
    while any(ready.values()):
        choices = []
        for e in ENGINES:
            mine = []
            for k, at in ready[e].items():
                at = max(at, clock[e])
                for b in STEPS[k[0]][2]:
                    at = max(at, min(free[b])[0] + HOP) if free[b] else None
                    if at is None:
                        break
                if at is not None:
                    load = TABLE_LOAD if TABLES.get(k[0], table) != table else 0
                    mine.append((at + load, rank[k], at, load, k))
            if mine:
                _, _, at, load, k = min(mine)
                choices.append((at, e, load, k))
        at, e, load, k = min(choices)
        _, length, takes, frees = STEPS[k[0]]
        if k[0] in EXPERT_STEPS:
            length = length * len(EXPERT_RUNS[k[2]][0]) // GT
        for b in takes:
            use = min(free[b])
            free[b].remove(use)
            index[k, b] = use[1]
            freed_by[k, b] = last_freed.get((b, use[1]))
        end[k] = clock[e] = at + load + length
        if k[0] in TABLES:
            table = TABLES[k[0]]
        for b in frees:
            i = index[(TAKER[k[0], b],) + k[1:], b]
            free[b].append((end[k], i))
            last_freed[b, i] = k
        for o in opens[k]:
            blocked[o] -= 1
            if not blocked[o]:
                other = STEPS[o[0]][0]
                ready[other][o] = max(end[d] + (SAME if STEPS[d[0]][0] == other else HOP) for d in after[o])
        del ready[e][k]
        order[e].append(k)
    return order, index, freed_by


ORDER, INDEX, FREED_BY = arrange()
NTH = {}
for _e in ENGINES:
    _runs = {}
    for _k in ORDER[_e]:
        _runs[_k[0]] = NTH[_k] = _runs.get(_k[0], 0) + 1


def build(nc, x_in, ctx_in, weights, mlp_w, moe_w1, moe_w2, moe_b2, router_w, cols, rows, consts, out):
    with ExitStack() as ctx:
        def sb(name, shape, dt=F32):
            return ctx.enter_context(nc.sbuf_tensor(name, shape, dt))

        def sem(name):
            return ctx.enter_context(nc.semaphore(name))

        w_sb = sb("w_sb", [P, len(WEIGHTS), D])
        mlp_sb = sb("mlp_sb", [P, 2, 2, FF])
        moe1_sb = sb("moe1_sb", [P, EXPERTS, FF])
        moe2_sb = sb("moe2_sb", [P, EXPERTS, CH, D])
        moe_b2_sb = sb("moe_b2_sb", [EXPERTS, D])
        router_sb = sb("router_sb", [P, EXPERTS])
        cols_sb = sb("cols_sb", [P, len(COLS)])
        rows_sb = sb("rows_sb", [P, ROW_N])
        const_sb = sb("const_sb", [P, CONST_N])
        ident16 = sb("ident16", [P, P], BF16)
        causal16 = sb("causal16", [P, SEQ], BF16)
        bv_wide = sb("bv_wide", [P, BUFFERS["wide"], P])
        wo_second = sb("wo_second", [P, len(ATTNS), D])
        out_bias = sb("out_bias", [P, len(ATTNS), D])
        minus_half = sb("minus_half", [P, 1])
        x_sb = sb("x_sb", [P, TILES, D])
        ctx_sb = sb("ctx_sb", [P, TILES, D])
        ctx_hat = sb("ctx_hat", [P, TILES, D])
        feat = {k: sb(f"feat_{k}", [P, TILES, P]) for k in ("self", "ctx", "ctx1", "ctx3")}
        xhat = sb("xhat", [P, TILES, D])
        xbias = xhat
        stats = sb("stats", [P, TILES, 6])
        moments = sb("moments", [P, TILES, 2])
        varp = sb("varp", [P, TILES, 1])
        rstd = sb("rstd", [P, TILES, 1])
        cstats = sb("cstats", [P, TILES, 6])
        cmoments = sb("cmoments", [P, TILES, 2])
        cvarp = sb("cvarp", [P, TILES, 1])
        crstd = sb("crstd", [P, TILES, 1])
        k_feat = ctx_sb
        rope_a = sb("rope_a", [P, BUFFERS["rope"], 2, P])
        rope_b = sb("rope_b", [P, BUFFERS["rope"], 2, P])
        value_blocks = sb("value_blocks", [P, TILES, 2, SP, 2, 2, HD])
        row_max = sb("row_max", [P, TILES, HEADS])
        probs = sb("probs", [P, BUFFERS["probs"], HEADS, SEQ])
        probs_t = sb("probs_t", [P, BUFFERS["probs_t"], PAIRS, P])
        minus_max = sb("minus_max", [P, TILES, ACT_HEADS])
        den = sb("den", [P, TILES, HEADS])
        rden = sb("rden", [P, TILES, HEADS])
        rden_wide = sb("rden_wide", [P, BUFFERS["spread"], 2 * P])
        o_feat = sb("o_feat", [P, BUFFERS["o"], 2, 2, SEQ])
        score_junk = sb("score_junk", [P, D])
        score = sb("score", [P, TILES, 2])
        score_diag = ctx_hat[:, :, 0:SEQ]
        rank_junk = ctx_hat[:, :, SEQ:2 * SEQ]
        rank = sb("rank", [P, TILES, 4])
        chosen = sb("chosen", [P, TILES, 2])
        chosen_bias = sb("chosen_bias", [P, D])
        hid = sb("hid", [P, BUFFERS["hid"], CH, P])
        hid_act = sb("hid_act", [P, BUFFERS["hid"], CH, P])
        logits = sb("logits", [P, TILES, EXPERTS])
        cmp_gt = sb("cmp_gt", [P, EXPERTS, EXPERTS])
        cmp_eq = sb("cmp_eq", [P, EXPERTS, EXPERTS])
        rank8 = sb("rank8", [P, TILES, EXPERTS])
        top = sb("top", [P, TILES, 1])
        gate_e = sb("gate_e", [P, TILES, EXPERTS])
        gate_s = sb("gate_s", [P, TILES, 2])
        gates = sb("gates", [P, TILES, EXPERTS])
        gates_t = feat["ctx1"][0:EXPERTS]
        hidden_e = sb("hidden_e", [P, BUFFERS["hidden_e"], CH, GT * P])
        mix = feat["ctx"]

        with ExitStack() as attention_only:
            key_blocks = attention_only.enter_context(nc.sbuf_tensor("key_blocks", [P, TILES, 2, SLOTS, SEQ], F32))
            q_blocks = attention_only.enter_context(nc.sbuf_tensor("q_blocks", [P, TILES, 2, 2, SEQ], F32))
        w1_parts = sb("w1_parts", [P, EXPERTS, 2, FF], F32R)
        input_parts = sb("input_parts", [P, TILES, 2, P], F32R)

        ps_scores = ctx.enter_context(nc.psum_tensor("ps_scores", [P, BUFFERS["scores"], 2, 512], F32))
        ps_bank = ctx.enter_context(nc.psum_tensor("ps_bank", [P, BUFFERS["bank"], 512], F32))

        x_loaded = [sem("x_loaded_tiles01"), sem("x_loaded_others")]
        ctx_loaded = sem("ctx_loaded")
        consts_loaded, cols_loaded, rows_loaded = sem("consts_loaded"), sem("cols_loaded"), sem("rows_loaded")
        w_loaded = {b["name"]: sem(f"w_loaded_{b['name']}") for b in BLOCKS}
        mask_made, zeros_made = sem("mask_made"), sem("zeros_made")
        dve_chain = sem("dve_chain")
        pool_chain = sem("pool_chain")
        finished = {s: sem(f"finished_{s}") for s in STEPS}
        out_done = sem("out_done")

        def weight(n, which):
            return w_sb[:, WEIGHTS.index((BLOCKS[n]["name"], which)), :]

        def col(name, which):
            i = COLS.index((name, which))
            return cols_sb[:, i:i + 1]

        def row(name, which):
            i = ROWS.index((name, which)) * D
            return rows_sb[:, i:i + D]

        def const(name):
            at, width = CONSTS[name]
            return const_sb[:, at:at + width]

        ident = const("ident")

        def done(eng, step, n, t):
            eng.wait_ge(finished[step], NTH[step, n, t])

        def take(eng, buffer, step, n, t):
            freeing = FREED_BY[(step, n, t), buffer]
            if freeing:
                done(eng, *freeing)
            return INDEX[(step, n, t), buffer]

        def held(buffer, step, n, t):
            return INDEX[(step, n, t), buffer]

        def bank(step, n, t):
            return ps_bank[:, held("bank", step, n, t), :]

        def residual(eng, n, t):
            if n == 0:
                eng.wait_ge(x_loaded[t >= 2], 16)
            else:
                done(eng, "add_o" if BLOCKS[n - 1]["kind"] == "attn" else "add_f", n - 1, t)

        block = ctx.enter_context(nc.Block())

        @block.sync
        def _(sp):
            x_tiles = x_in.rearrange("(t p) d -> p t d", p=P)
            sp.dma_start(x_sb[:, 0:2, :], x_tiles[:, 0:2, :]).then_inc(x_loaded[0], 16)
            sp.dma_start(const_sb[:, :], consts).then_inc(consts_loaded, 16)
            sp.dma_start(cols_sb[:, :], cols).then_inc(cols_loaded, 16)
            sp.dma_start(x_sb[:, 2:, :], x_tiles[:, 2:, :]).then_inc(x_loaded[1], 16)
            at = 0
            m = 0
            for b in BLOCKS:
                if b["kind"] == "attn":
                    k = sum(w[0] == b["name"] for w in WEIGHTS)
                    sp.dma_start(w_sb[:, at:at + k, :], weights[:, at:at + k, :]).then_inc(w_loaded[b["name"]], 16)
                    at += k
                elif b["kind"] == "mlp":
                    sp.dma_start(mlp_sb[:, m], mlp_w[:, m]).then_inc(w_loaded[b["name"]], 16)
                    m += 1
                if b["name"] == "sa0":
                    sp.dma_start(rows_sb[:, :], rows.broadcast_to([P, ROW_N])).then_inc(rows_loaded, 16)
                    sp.dma_start(ctx_sb[:, :, :], ctx_in.rearrange("(t p) d -> p t d", p=P)).then_inc(ctx_loaded, 16)
            sp.dma_start(router_sb[:, :], router_w).then_inc(w_loaded["moe"], 16)
            sp.dma_start(moe_b2_sb[:, :], moe_b2).then_inc(w_loaded["moe"], 16)
            sp.dma_start(moe1_sb[:, :, :], moe_w1).then_inc(w_loaded["moe"], 16)
            sp.dma_start(moe2_sb[:, :, :, :], moe_w2).then_inc(w_loaded["moe"], 16)
            for i, g in enumerate(GROUPS):
                done(sp, "mix_in", MOE, i * EXPERTS + EXPERTS - 1)
                part = slice(g.start * P, g.stop * P)
                sp.dma_start(out[part, :].rearrange("(t p) d -> p t d", p=P), mix[:, g.start:g.stop, :]).then_inc(out_done, 16)
            sp.wait_ge(out_done, 16 * len(GROUPS))

        @block.gpsimd
        def _(pool):
            chain = [0]

            def link(ins):
                chain[0] += 1
                ins.then_inc(pool_chain, 1)
                pool.wait_ge(pool_chain, chain[0])

            link(pool.memset(minus_half[:, :], -0.5))
            pool.memset(q_blocks[:, :, :, :, :].rearrange("p t a b q -> p (t a b q)"), 0.0).then_inc(zeros_made, 1)
            pool.wait_ge(consts_loaded, 16)

            for step, n, t in ORDER["pool"]:
                b = BLOCKS[n]
                if step in ("ctx_root", "root"):
                    if step == "root":
                        done(pool, "stats", n, t)
                        variance, var_eps, inverse_root = moments[:, t, 1:2], varp[:, t, :], rstd[:, t, :]
                    else:
                        done(pool, "ctx_stats", n, t)
                        variance, var_eps, inverse_root = cmoments[:, t, 1:2], cvarp[:, t, :], crstd[:, t, :]
                    link(pool.tensor_scalar(var_eps, variance, LN_EPS, None, ALU.add))
                    pool.tensor_tensor(inverse_root, var_eps, minus_half[:, :], ALU.pow).then_inc(finished[step], 1)
                elif step == "xbias":
                    if b.get("topk"):
                        done(pool, "rank", n, t)
                        done(pool, "turn_h", n, t)
                        done(pool, "add_bias", n, 0)
                        keep = chosen[:, t, 1:2].broadcast_to([P, D])
                        take_bias = chosen[:, t, 0:1].broadcast_to([P, D])
                        link(pool.tensor_tensor(xbias[:, t, :], x_sb[:, t, :], keep, ALU.mult))
                        link(pool.tensor_tensor(chosen_bias[:, :], out_bias[:, ATTNS.index(n), :], take_bias, ALU.mult))
                        pool.tensor_tensor(xbias[:, t, :], xbias[:, t, :], chosen_bias[:, :], ALU.add).then_inc(finished[step], 1)
                    else:
                        residual(pool, n, t)
                        done(pool, "turn_h", n, t)
                        if n in BIASED:
                            done(pool, "add_bias", n, 0)
                            bias = out_bias[:, ATTNS.index(n), :]
                        else:
                            pool.wait_ge(rows_loaded, 16)
                            bias = row(b["name"], "bo")
                        pool.tensor_tensor(xbias[:, t, :], x_sb[:, t, :], bias, ALU.add).then_inc(finished[step], 1)
                elif step == "wo_halves":
                    pool.wait_ge(w_loaded[b["name"]], 16)
                    if n in BIASED:
                        done(pool, "bias_out", n, 0)
                    second, first = (const("half")[:, h:h + 1].broadcast_to([P, D]) for h in (1, 0))
                    link(pool.tensor_tensor(wo_second[:, ATTNS.index(n), :], weight(n, "o"), second, ALU.mult))
                    pool.tensor_tensor(weight(n, "o"), weight(n, "o"), first, ALU.mult).then_inc(finished[step], 1)
                elif step == "spread":
                    done(pool, "total", n, t)
                    i = take(pool, "spread", step, n, t)
                    factor = rden[:, t, :].rearrange("p (h o) -> p h o", o=1).broadcast_to([P, HEADS, 2 * HD])
                    pool.tensor_copy(rden_wide[:, i].rearrange("p (h x) -> p h x", x=2 * HD), factor).then_inc(finished[step], 1)
                elif step == "wo_halves":
                    pool.wait_ge(w_loaded[b["name"]], 16)
                    if n in BIASED:
                        done(pool, "bias_out", n, 0)
                    second, first = (const("half")[:, h:h + 1].broadcast_to([P, D]) for h in (1, 0))
                    link(pool.tensor_tensor(wo_second[:, ATTNS.index(n), :], weight(n, "o"), second, ALU.mult))
                    pool.tensor_tensor(weight(n, "o"), weight(n, "o"), first, ALU.mult).then_inc(finished[step], 1)
                elif step in ("norm0", "norm1"):
                    s = int(step[-1])
                    done(pool, "total", n, t)
                    heads = slice(s * SLOTS, (s + 1) * SLOTS)
                    part = probs[:, held("probs", "shift", n, t), heads, :]
                    factor = rden[:, t, heads].rearrange("p (h o) -> p h o", o=1).broadcast_to([P, SLOTS, SEQ])
                    pool.tensor_tensor(part, part, factor, ALU.mult).then_inc(finished[step], 1)
                elif step == "rope_k":
                    i = held("rope", "qk_rope", n, t)
                    done(pool, "copy_rope", n, t)
                    done(pool, "rope_q", n, t)
                    pool.tensor_tensor(k_feat[:, t, :], rope_a[:, i, 1], rope_b[:, i, 1], ALU.add).then_inc(finished[step], 1)
                elif step == "keys":
                    done(pool, "rope_k" if b.get("rope") else "copy_qk", n, t)
                    spread = k_feat[:, t, :].rearrange("p (b o k) -> p b o k", b=2, o=1).broadcast_to([P, 2, SLOTS, SEQ])
                    mask = const("slot").rearrange("p (b s o) -> p b s o", b=1, o=1).broadcast_to([P, 2, SLOTS, SEQ])
                    pool.tensor_tensor(key_blocks[:, t], spread, mask, ALU.mult).then_inc(finished[step], 1)
                elif step == "cubic":
                    i = held("hid", "hidden", n, t)
                    done(pool, "square", n, t)
                    link(pool.tensor_tensor(hid_act[:, i], hid_act[:, i], hid[:, i], ALU.mult))
                    pool.tensor_tensor(hid_act[:, i], hid_act[:, i], hid[:, i], ALU.add).then_inc(finished[step], 1)

        @block.scalar
        def _(act):
            act.wait_ge(cols_loaded, 16)

            def affine(out, in_, g, b):
                return nc.scalar.activation(out, in_, ACT.Identity, bias=b, scale=g)

            for step, n, t in ORDER["act"]:
                b = BLOCKS[n]
                name = b["name"]
                if step == "ctx_copy":
                    done(act, "ctx_turn", n, t)
                    nc.scalar.copy(feat["ctx"][:, t, :], bank("ctx_turn", n, t)[:, 0:P]).then_inc(finished[step], 1)
                elif step == "hat_copy":
                    done(act, "hat_turn", n, t)
                    ps = bank("hat_turn", n, t)[:, 0:P]
                    affine(feat["ctx1"][:, t, :], ps, col("ctx1", "g"), col("ctx1", "b"))
                    affine(feat["ctx3"][:, t, :], ps, col("ctx3", "g"), col("ctx3", "b")).then_inc(finished[step], 1)
                elif step == "copy_h":
                    done(act, "turn_h", n, t)
                    ps = bank("turn_h", n, t)[:, 0:P]
                    if b["ln"]:
                        affine(feat["self"][:, t, :], ps, col(name, "g"), col(name, "b")).then_inc(finished[step], 1)
                    else:
                        nc.scalar.copy(feat["self"][:, t, :], ps).then_inc(finished[step], 1)
                elif step == "copy_v":
                    done(act, "values", n, t)
                    if n == 0:
                        act.wait_ge(zeros_made, 2)
                    ps = bank("values", n, t)
                    for e in range(2):
                        r = slice(e * SEQ, (e + 1) * SEQ)
                        dst = value_blocks[r, t, :, :, e, :, :].rearrange("p s j h d -> p (s j) (h d)")
                        last = nc.scalar.copy(dst, ps[r, 0:D].rearrange("p (g x) -> p g x", x=2 * HD))
                    last.then_inc(finished[step], 1)
                elif step == "copy_qk":
                    done(act, "qk", n, t)
                    ps = bank("qk", n, t)
                    for h in range(2):
                        r = slice(h * SEQ, (h + 1) * SEQ)
                        src = ps[r, 0:P].rearrange("p (b s) -> p b s", b=2)
                        if b.get("nobias"):
                            nc.scalar.copy(q_blocks[r, t, :, h, :], src)
                        else:
                            nc.scalar.activation(q_blocks[r, t, :, h, :], src, ACT.Identity, bias=col(name, "bq")[r])
                    if b.get("nobias"):
                        nc.scalar.copy(k_feat[:, t, :], ps[:, P:2 * P]).then_inc(finished[step], 1)
                    else:
                        nc.scalar.activation(k_feat[:, t, :], ps[:, P:2 * P], ACT.Identity, bias=col(name, "bk")).then_inc(finished[step], 1)
                elif step == "exp":
                    done(act, "shift", n, t)
                    i = held("probs", "shift", n, t)
                    j = held("scores", "scores", n, t)
                    for h in range(ACT_HEADS):
                        nc.scalar.activation(probs[:, i, h, :], ps_scores[:, j, h // SLOTS, h % SLOTS * SEQ:(h % SLOTS + 1) * SEQ], ACT.Exp,
                                             bias=minus_max[:, t, h:h + 1], scale=SCALE, accum_out=den[:, t, h:h + 1])
                    rest = probs[:, i, ACT_HEADS:].rearrange("p h k -> p (h k)")
                    nc.scalar.activation(rest, rest, ACT.Exp, scale=SCALE).then_inc(finished[step], 1)
                elif step == "copy_p0":
                    done(act, "turn_p0", n, t)
                    i = held("probs_t", "turn_p0", n, t)
                    nc.scalar.copy(probs_t[:, i, 0:4, :].rearrange("p g q -> p (g q)"), bank("turn_p0", n, t)).then_inc(finished[step], 1)
                elif step == "copy_p1":
                    done(act, "turn_p1", n, t)
                    i = held("probs_t", "turn_p0", n, t)
                    nc.scalar.copy(probs_t[:, i, 4:8, :].rearrange("p g q -> p (g q)"), bank("turn_p1", n, t)).then_inc(finished[step], 1)
                elif step == "copy_o":
                    done(act, "pv", n, t)
                    dst = o_feat[:, held("o", "pv", n, t)].rearrange("p h s q -> p s h q")
                    nc.scalar.copy(dst, bank("pv", n, t)[:, 0:2 * P].rearrange("p (s h q) -> p s h q", s=2, h=2)).then_inc(finished[step], 1)
                elif step == "square":
                    done(act, "add_b", n, t)
                    i = held("hid", "hidden", n, t)
                    nc.scalar.activation(hid_act[:, i], hid[:, i], ACT.Square, scale=GELU_A ** 0.5).then_inc(finished[step], 1)
                elif step == "tanh":
                    i = held("hid", "hidden", n, t)
                    if b["act"] == "gelu":
                        done(act, "cubic", n, t)
                        src, scale = hid_act[:, i], GELU_C
                    else:
                        done(act, "add_b", n, t)
                        src, scale = hid[:, i], 0.5
                    nc.scalar.activation(hid_act[:, i], src, ACT.Tanh, scale=scale).then_inc(finished[step], 1)
                elif step == "exp_e":
                    done(act, "rank_e", n, t)
                    nc.scalar.activation(gate_e[:, t, :], gate_e[:, t, :], ACT.Exp).then_inc(finished[step], 1)
                elif step == "copy_g":
                    done(act, "turn_g", n, t)
                    nc.scalar.copy(gates_t[:, t, :], bank("turn_g", n, t)[0:EXPERTS, 0:P]).then_inc(finished[step], 1)
                elif step in ("gelu0", "gelu1"):
                    half = int(step[-1])
                    done(act, f"expert_in{half}", n, t)
                    g, e = EXPERT_RUNS[t]
                    i = held("hidden_e", "expert_in0", n, t)
                    j = held("scores", f"expert_in{half}", n, t)
                    for c in range(2):
                        ins = nc.scalar.activation(hidden_e[:, i, 2 * half + c, 0:len(g) * P], ps_scores[:, j, c, 0:len(g) * P], ACT.Gelu,
                                                   bias=col("moe", f"f{e}_{2 * half + c}"))
                    ins.then_inc(finished[step], 1)

        @block.vector
        def _(dve):
            v = nc.vector
            chain = [0]

            def link(ins):
                chain[0] += 1
                ins.then_inc(dve_chain, 1)
                dve.wait_ge(dve_chain, chain[0])

            v.memset(value_blocks[:, :, :, :, :, :, :].rearrange("p t s j e h d -> p (t s j e h d)"), 0.0).then_inc(zeros_made, 1)
            def split(value, high, low):
                link(v.tensor_copy(high, value))
                return v.tensor_tensor(low, value, high, ALU.subtract)

            dve.wait_ge(consts_loaded, 16)
            link(v.tensor_copy(ident16[:, :], ident))
            v.tensor_copy(causal16[:, :], const("causal")).then_inc(mask_made, 1)
            dve.wait_ge(cols_loaded, 16)

            for step, n, t in ORDER["dve"]:
                b = BLOCKS[n]
                name = b["name"]
                if step == "wide_bias":
                    i = take(dve, "wide", step, n, t)
                    ins = v.tensor_scalar(bv_wide[:, i, :], ident, 0.0, col(name, "bv"), ALU.mult, ALU.add)
                    ins.then_inc(finished[step], 1)
                elif step == "add_bias":
                    done(dve, "bias_out", n, t)
                    dve.wait_ge(rows_loaded, 16)
                    v.tensor_tensor(out_bias[:, ATTNS.index(n), :], bank("bias_out", n, t)[:, 0:D], row(name, "bo"), ALU.add).then_inc(finished[step], 1)
                elif step == "ctx_stats":
                    dve.wait_ge(ctx_loaded, 16)
                    link(v.bn_stats(cstats[:, t, :], ctx_sb[:, t, :]))
                    v.bn_aggr(cmoments[:, t, :], cstats[:, t, :]).then_inc(finished[step], 1)
                elif step == "ctx_apply":
                    done(dve, "ctx_stats", n, t)
                    done(dve, "ctx_root", n, t)
                    v.tensor_scalar(ctx_hat[:, t, :], ctx_sb[:, t, :], cmoments[:, t, 0:1], crstd[:, t, :],
                                    ALU.subtract, ALU.mult).then_inc(finished[step], 1)
                elif step == "stats":
                    residual(dve, n, t)
                    link(v.bn_stats(stats[:, t, :], x_sb[:, t, :]))
                    v.bn_aggr(moments[:, t, :], stats[:, t, :]).then_inc(finished[step], 1)
                elif step == "apply":
                    done(dve, "stats", n, t)
                    done(dve, "root", n, t)
                    v.tensor_scalar(xhat[:, t, :], x_sb[:, t, :], moments[:, t, 0:1], rstd[:, t, :],
                                    ALU.subtract, ALU.mult).then_inc(finished[step], 1)
                elif step == "score":
                    residual(dve, n, t)
                    dve.wait_ge(rows_loaded, 16)
                    link(v.scalar_tensor_tensor(score_junk[:, :], x_sb[:, t, :], 1.0, row("ca2", "score"), ALU.mult, ALU.mult,
                                                accum_out=score[:, t, 0:1]))
                    link(v.tensor_scalar(score[:, t, 1:2], score[:, t, 0:1], rows_sb[:, ROW_SCORE_B:ROW_SCORE_B + 1], None, ALU.add))
                    v.tensor_scalar(score_diag[:, t], const("fold"), score[:, t, 1:2], None, ALU.mult).then_inc(finished[step], 1)
                elif step == "rank":
                    done(dve, "rank_spread", n, t)
                    ps = bank("rank_spread", n, t)[:, 0:SEQ]
                    own, above, ties, total = (rank[:, t, i:i + 1] for i in range(4))
                    link(v.scalar_tensor_tensor(rank_junk[:, t], ps, 1.0, const("fold"), ALU.mult, ALU.mult, accum_out=own))
                    link(v.tensor_scalar(rank_junk[:, t], ps, own, 0.0, ALU.is_gt, ALU.add, accum_out=above))
                    link(v.scalar_tensor_tensor(rank_junk[:, t], ps, own, const("before"), ALU.is_equal, ALU.mult, accum_out=ties))
                    link(v.tensor_tensor(total, above, ties, ALU.add))
                    link(v.tensor_scalar(chosen[:, t, 0:1], total, TOPK - 0.5, None, ALU.is_lt))
                    v.tensor_scalar(chosen[:, t, 1:2], chosen[:, t, 0:1], -1.0, 1.0, ALU.mult, ALU.add).then_inc(finished[step], 1)
                elif step == "copy_rope":
                    done(dve, "qk_rope", n, t)
                    if n == 0:
                        done(dve, "ctx_apply", 0, t)
                        done(dve, "ctx_turn", 0, t)
                    i = held("rope", "qk_rope", n, t)
                    v4 = bank("qk_rope", n, t).rearrange("p (k b s) -> p k b s", k=4, b=2)
                    for table, first, dst, suffix in (("cos", 0, rope_a, ""), ("sin", 2, rope_b, "r")):
                        for k in range(2):
                            tab = const(table).rearrange("p (o s) -> p o s", o=1).broadcast_to([P, 2, SEQ])
                            ins = v.scalar_tensor_tensor(dst[:, i, k].rearrange("p (b s) -> p b s", b=2), v4[:, first + k],
                                                         col(name, "b" + "qk"[k] + suffix), tab, ALU.add, ALU.mult)
                    ins.then_inc(finished[step], 1)
                elif step == "rope_q":
                    done(dve, "copy_rope", n, t)
                    i = held("rope", "qk_rope", n, t)
                    if n == 0:
                        dve.wait_ge(zeros_made, 2)
                    for h in range(2):
                        r = slice(h * SEQ, (h + 1) * SEQ)
                        ins = v.tensor_tensor(q_blocks[r, t, :, h, :], rope_a[r, i, 0].rearrange("p (b s) -> p b s", b=2),
                                              rope_b[r, i, 0].rearrange("p (b s) -> p b s", b=2), ALU.add)
                    ins.then_inc(finished[step], 1)
                elif step == "shift":
                    done(dve, "scores", n, t)
                    s3 = ps_scores[:, held("scores", "scores", n, t)].rearrange("p g (h k) -> p (g h) k", k=SEQ)
                    link(v.tensor_reduce(row_max[:, t], s3, AX_X, ALU.max))
                    i = take(dve, "probs", step, n, t)
                    v.tensor_scalar(minus_max[:, t], row_max[:, t, 0:ACT_HEADS], -SCALE, None, ALU.mult)
                    others = HEADS - ACT_HEADS
                    mx = row_max[:, t, ACT_HEADS:].rearrange("p (h o) -> p h o", o=1).broadcast_to([P, others, SEQ])
                    v.tensor_tensor(probs[:, i, ACT_HEADS:], s3[:, ACT_HEADS:], mx, ALU.subtract).then_inc(finished[step], 1)
                elif step == "total":
                    done(dve, "exp", n, t)
                    link(v.tensor_reduce(den[:, t, ACT_HEADS:], probs[:, held("probs", "shift", n, t), ACT_HEADS:], AX_X, ALU.add))
                    v.reciprocal(rden[:, t], den[:, t]).then_inc(finished[step], 1)
                elif step == "norm":
                    done(dve, "copy_o", n, t)
                    done(dve, "turn_r", n, t)
                    factor = bank("turn_r", n, t)[:, 0:2 * P].rearrange("p (s h q) -> p s h q", s=2, h=2)
                    dst = o_feat[:, held("o", "pv", n, t)].rearrange("p h s q -> p s h q")
                    v.tensor_tensor(dst, dst, factor, ALU.mult).then_inc(finished[step], 1)
                elif step == "add_o":
                    done(dve, "project", n, t)
                    done(dve, "xbias", n, t)
                    ps = bank("project", n, t)[:, 0:D]
                    if b.get("topk"):
                        v.scalar_tensor_tensor(x_sb[:, t, :], ps, chosen[:, t, 0:1], xbias[:, t, :], ALU.mult, ALU.add).then_inc(finished[step], 1)
                    else:
                        v.tensor_tensor(x_sb[:, t, :], ps, xbias[:, t, :], ALU.add).then_inc(finished[step], 1)
                elif step == "add_b":
                    done(dve, "hidden", n, t)
                    c0 = COLS.index((name, "f0"))
                    bias = cols_sb[:, c0:c0 + CH].rearrange("p (c o) -> p c o", o=1).broadcast_to([P, CH, P])
                    v.tensor_tensor(hid[:, held("hid", "hidden", n, t)], bank("hidden", n, t).rearrange("p (c q) -> p c q", c=CH),
                                    bias, ALU.add).then_inc(finished[step], 1)
                elif step == "gate":
                    done(dve, "tanh", n, t)
                    i = held("hid", "hidden", n, t)
                    v.scalar_tensor_tensor(hid_act[:, i], hid_act[:, i], 1.0, hid[:, i], ALU.add, ALU.mult).then_inc(finished[step], 1)
                elif step == "add_f":
                    done(dve, "fc2", n, t)
                    done(dve, "xbias", n, t)
                    v.scalar_tensor_tensor(x_sb[:, t, :], bank("fc2", n, t)[:, 0:D], 0.5, xbias[:, t, :], ALU.mult, ALU.add).then_inc(finished[step], 1)
                elif step == "rank_e":
                    done(dve, "route", n, t)
                    lg = logits[:, t, :]
                    link(v.tensor_tensor(lg, bank("route", n, t)[:, 0:EXPERTS], rows_sb[:, ROW_ROUTER:ROW_ROUTER + EXPERTS], ALU.add))
                    mine = lg.rearrange("p (e o) -> p e o", o=1).broadcast_to([P, EXPERTS, EXPERTS])
                    other = lg.rearrange("p (o f) -> p o f", o=1).broadcast_to([P, EXPERTS, EXPERTS])
                    link(v.tensor_tensor(cmp_eq[:, :, :], other, mine, ALU.is_equal))
                    link(v.tensor_tensor(cmp_gt[:, :, :], other, mine, ALU.is_gt))
                    link(v.tensor_tensor(cmp_eq[:, :, :], cmp_eq[:, :, :], const("before8").rearrange("p (e f) -> p e f", e=EXPERTS), ALU.mult))
                    link(v.tensor_tensor(cmp_gt[:, :, :], cmp_gt[:, :, :], cmp_eq[:, :, :], ALU.add))
                    link(v.tensor_reduce(rank8[:, t, :], cmp_gt[:, :, :], AX_X, ALU.add))
                    link(v.tensor_reduce(top[:, t, :], lg, AX_X, ALU.max))
                    v.tensor_scalar(gate_e[:, t, :], lg, top[:, t, :], None, ALU.subtract).then_inc(finished[step], 1)
                elif step == "gates":
                    done(dve, "exp_e", n, t)
                    link(v.scalar_tensor_tensor(gates[:, t, :], rank8[:, t, :], 1.5, gate_e[:, t, :], ALU.is_lt, ALU.mult,
                                                accum_out=gate_s[:, t, 0:1]))
                    link(v.reciprocal(gate_s[:, t, 1:2], gate_s[:, t, 0:1]))
                    v.tensor_scalar(gates[:, t, :], gates[:, t, :], gate_s[:, t, 1:2], None, ALU.mult).then_inc(finished[step], 1)
                elif step == "add_m":
                    done(dve, "mix_bias", n, t)
                    v.tensor_tensor(mix[:, t, :], bank("mix_bias", n, t)[:, 0:D], x_sb[:, t, :], ALU.add).then_inc(finished[step], 1)
                elif step == "split_w":
                    dve.wait_ge(w_loaded["moe"], 64)
                    done(dve, "scores", ATTNS[-1], t)
                    split(moe1_sb[:, t, :], w1_parts[:, t, 0, :], w1_parts[:, t, 1, :]).then_inc(finished[step], 1)
                elif step == "split_h":
                    done(dve, "copy_h", n, t)
                    done(dve, "scores", ATTNS[-1], t)
                    split(feat["self"][:, t, :], input_parts[:, t, 0, :], input_parts[:, t, 1, :]).then_inc(finished[step], 1)
                elif step == "mix_in":
                    done(dve, "expert_out", n, t)
                    g, e = EXPERT_RUNS[t]
                    if e:
                        done(dve, "mix_in", n, t - 1)
                    for k, u in enumerate(g):
                        if e == 0:
                            done(dve, "add_m", n, u)
                        ins = v.scalar_tensor_tensor(mix[:, u, :], bank("expert_out", n, t)[:, k * P:(k + 1) * P], gates[:, u, e:e + 1],
                                                     mix[:, u, :], ALU.mult, ALU.add)
                    ins.then_inc(finished[step], 1)

        @block.tensor
        def _(pe):
            def source(n, t):
                kv = BLOCKS[n]["kv"]
                if kv == "self":
                    done(pe, "copy_h", n, t)
                else:
                    done(pe, "ctx_copy" if kv == "ctx" else "hat_copy", 0, t)
                return feat[kv][:, t, :]

            pe.wait_ge(consts_loaded, 16)
            for step, n, t in ORDER["pe"]:
                b = BLOCKS[n]
                if "bank" in STEPS[step][2]:
                    ps = ps_bank[:, take(pe, "bank", step, n, t), :]
                if step == "bias_out":
                    done(pe, "wide_bias", n, t)
                    pe.wait_ge(w_loaded[b["name"]], 16)
                    i = held("wide", "wide_bias", n, t)
                    nc.tensor.matmul(ps[:, 0:D], bv_wide[:, i, :], weight(n, "o"), start=True, stop=True).then_inc(finished[step], 1)
                elif step == "ctx_turn":
                    pe.wait_ge(ctx_loaded, 16)
                    nc.tensor.transpose(ps[:, 0:P], ctx_sb[:, t, :], ident).then_inc(finished[step], 1)
                elif step == "hat_turn":
                    done(pe, "ctx_apply", n, t)
                    nc.tensor.transpose(ps[:, 0:P], ctx_hat[:, t, :], ident).then_inc(finished[step], 1)
                elif step == "turn_h":
                    if b["ln"]:
                        done(pe, "apply", n, t)
                        src = xhat[:, t, :]
                    else:
                        residual(pe, n, t)
                        src = x_sb[:, t, :]
                    nc.tensor.transpose(ps[:, 0:P], src, ident).then_inc(finished[step], 1)
                elif step == "rank_spread":
                    done(pe, "score", n, t)
                    nc.tensor.matmul(ps[:, 0:SEQ], const("same_seq"), score_diag[:, t], start=True, stop=True).then_inc(finished[step], 1)
                elif step in ("qk", "qk_rope"):
                    done(pe, "copy_h", n, t)
                    src_kv = source(n, t)
                    pe.wait_ge(w_loaded[b["name"]], 16)
                    if step == "qk_rope":
                        take(pe, "rope", step, n, t)
                    for i, w in enumerate(["q", "k", "qr", "kr"] if step == "qk_rope" else ["q", "k"]):
                        src = src_kv if w[0] == "k" else feat["self"][:, t, :]
                        ins = nc.tensor.matmul(ps[:, i * P:(i + 1) * P], weight(n, w), src, start=True, stop=True)
                    ins.then_inc(finished[step], 1)
                elif step == "values":
                    src_kv = source(n, t)
                    pe.wait_ge(w_loaded[b["name"]], 16)
                    for s in range(2):
                        for e in range(2):
                            ins = nc.tensor.matmul(ps[e * SEQ:(e + 1) * SEQ, s * SEQ:(s + 1) * SEQ], src_kv[:, s * SEQ:(s + 1) * SEQ],
                                                   weight(n, "v")[:, e * SEQ:(e + 1) * SEQ], start=True, stop=True)
                    ins.then_inc(finished[step], 1)
                elif step == "scores":
                    done(pe, "keys", n, t)
                    done(pe, "rope_q" if b.get("rope") else "copy_qk", n, t)
                    j = take(pe, "scores", step, n, t)
                    if b.get("causal"):
                        pe.wait_ge(mask_made, 1)
                    for s in range(2):
                        dst = ps_scores[:, j, s, :]
                        if b.get("causal"):
                            mask = causal16[:, :].rearrange("p (o k) -> p o k", o=1).broadcast_to([P, SLOTS, SEQ])
                            nc.tensor.matmul(dst, ident16[:, :], mask, start=True, stop=False)
                        ins = nc.tensor.matmul(dst, q_blocks[:, t, s].rearrange("p h q -> p (h q)"),
                                               key_blocks[:, t, s].rearrange("p h k -> p (h k)"),
                                               start=not b.get("causal"), stop=True)
                    ins.then_inc(finished[step], 1)
                elif step in ("turn_p0", "turn_p1"):
                    half = int(step[-1])
                    done(pe, "exp", n, t)
                    if half:
                        done(pe, "total", n, t)
                    if half == 0:
                        take(pe, "probs_t", step, n, t)
                    i = held("probs", "shift", n, t)
                    for g in range(4):
                        pair = probs[:, i, 8 * half + 2 * g:8 * half + 2 * g + 2, :].rearrange("p h k -> p (h k)")
                        ins = nc.tensor.transpose(ps[:, g * P:(g + 1) * P], pair, ident)
                    ins.then_inc(finished[step], 1)
                elif step == "turn_r":
                    done(pe, "spread", n, t)
                    for s in range(2):
                        ins = nc.tensor.transpose(ps[:, s * P:(s + 1) * P], rden_wide[:, held("spread", "spread", n, t), s * P:(s + 1) * P], ident)
                    ins.then_inc(finished[step], 1)
                elif step == "pv":
                    done(pe, "copy_v", n, t)
                    done(pe, "copy_p1", n, t)
                    i = held("probs_t", "turn_p0", n, t)
                    take(pe, "o", step, n, t)
                    for s in range(2):
                        for j in range(SP):
                            ins = nc.tensor.matmul(ps[j * VB:(j + 1) * VB, s * P:(s + 1) * P], value_blocks[:, t, s, j].rearrange("p e h d -> p (e h d)"),
                                                   probs_t[:, i, s * SP + j, :], start=True, stop=True)
                    ins.then_inc(finished[step], 1)
                elif step == "project":
                    done(pe, "norm", n, t)
                    done(pe, "wo_halves", n, 0)
                    i = held("o", "pv", n, t)
                    for h in range(2):
                        ins = nc.tensor.matmul(ps[:, 0:D], o_feat[:, i, h].rearrange("p s q -> p (s q)"), (wo_second[:, ATTNS.index(n), :] if h else weight(n, "o")),
                                               start=(h == 0), stop=(h == 1))
                    ins.then_inc(finished[step], 1)
                elif step == "hidden":
                    done(pe, "copy_h", n, t)
                    pe.wait_ge(w_loaded[b["name"]], 16)
                    take(pe, "hid", step, n, t)
                    m = 0 if b["name"] == "ff0" else 1
                    for c in range(CH):
                        ins = nc.tensor.matmul(ps[:, c * P:(c + 1) * P], mlp_sb[:, m, 0, c * P:(c + 1) * P], feat["self"][:, t, :],
                                               start=True, stop=True)
                    ins.then_inc(finished[step], 1)
                elif step == "fc2":
                    done(pe, "gate", n, t)
                    m = 0 if b["name"] == "ff0" else 1
                    for c in range(CH):
                        ins = nc.tensor.matmul(ps[:, 0:D], hid_act[:, held("hid", "hidden", n, t), c, :],
                                               mlp_sb[:, m, 1, c * D:(c + 1) * D], start=(c == 0), stop=(c == CH - 1))
                    ins.then_inc(finished[step], 1)
                elif step == "route":
                    done(pe, "copy_h", n, t)
                    pe.wait_ge(w_loaded["moe"], 64)
                    nc.tensor.matmul(ps[:, 0:EXPERTS], feat["self"][:, t, :], router_sb[:, :], start=True, stop=True).then_inc(finished[step], 1)
                elif step == "turn_g":
                    done(pe, "gates", n, t)
                    nc.tensor.transpose(ps[0:EXPERTS, 0:P], gates[:, t, :], ident).then_inc(finished[step], 1)
                elif step == "mix_bias":
                    done(pe, "copy_g", n, t)
                    nc.tensor.matmul(ps[:, 0:D], gates_t[:, t, :], moe_b2_sb[:, :], start=True, stop=True).then_inc(finished[step], 1)
                elif step in ("expert_in0", "expert_in1"):
                    half = int(step[-1])
                    g, e = EXPERT_RUNS[t]
                    pe.wait_ge(w_loaded["moe"], 64)
                    for u in g:
                        done(pe, "split_h", MOE, u)
                    done(pe, "split_w", MOE, e)
                    if half == 0:
                        take(pe, "hidden_e", step, n, t)
                    j = take(pe, "scores", step, n, t)
                    for c in range(2):
                        at = (2 * half + c) * P
                        for k, (w, h) in enumerate(((0, 0), (0, 1), (1, 0))):
                            ins = nc.tensor.matmul(ps_scores[:, j, c, 0:len(g) * P], w1_parts[:, e, w, at:at + P],
                                                   input_parts[:, g.start:g.stop, h, :], start=(k == 0), stop=(k == 2))
                    ins.then_inc(finished[step], 1)
                elif step == "expert_out":
                    done(pe, "gelu0", n, t)
                    done(pe, "gelu1", n, t)
                    g, e = EXPERT_RUNS[t]
                    i = held("hidden_e", "expert_in0", n, t)
                    for k in range(len(g)):
                        for c in range(CH):
                            ins = nc.tensor.matmul(ps[:, k * P:(k + 1) * P], hidden_e[:, i, c, k * P:(k + 1) * P],
                                                   moe2_sb[:, e, c, :], start=(c == 0), stop=(c == CH - 1))
                    ins.then_inc(finished[step], 1)


def shape_constants():
    import numpy as np

    c = np.zeros((P, CONST_N), np.float32)

    def put(name, a):
        at, width = CONSTS[name]
        c[:, at:at + width] = a

    p = np.arange(P)
    put("ident", np.eye(P))
    put("same_seq", (p[:, None] // SEQ) == (p[None, :] // SEQ))
    k = np.arange(SEQ)
    put("fold", (p[:, None] % SEQ) == k)
    put("before", k < (p[:, None] % SEQ))
    put("slot", (p[:, None] // HD % SLOTS) == np.arange(SLOTS))
    put("causal", np.where(k > (p[:, None] % SEQ), -1e30, 0.0))
    half = HD // 2
    inv = (1.0 / 10000.0 ** (np.arange(0, HD, 2, dtype=np.float32) / HD)).astype(np.float32)
    angle = np.outer(inv[p % half], np.arange(SEQ, dtype=np.float32)).astype(np.float32)
    cos, sin = np.cos(angle), np.sin(angle) * np.where(p % HD < half, -1.0, 1.0)[:, None]
    put("cos", cos)
    put("sin", sin)
    put("half", (p[:, None] // HD % 2) == np.arange(2))
    e = np.arange(EXPERTS)
    put("before8", np.broadcast_to((e[None, :] < e[:, None]).reshape(-1), (P, EXPERTS * EXPERTS)))
    return c


def kernel(**inputs):
    import numpy as np
    import concourse.bacc as bacc
    from concourse.bass_utils import run_bass_kernel_spmd

    a = {k: np.asarray(v) for k, v in inputs.items()}
    p = np.arange(D)
    partner = p // HD * HD + (p % HD + HD // 2) % HD

    features = p.reshape(2, SP, 2, HD)
    by_parity = features.transpose(2, 1, 0, 3).reshape(-1)
    by_slot_pair = features.transpose(1, 2, 0, 3).reshape(-1)

    def split3(w):
        return w[0:D], w[D:2 * D], w[2 * D:3 * D]

    w, c, r = {}, {}, {}
    for name, pre in (("sa0", "L0_xattn_sa_"), ("ca0", "L0_xattn_ca_")):
        for x in "qkvo":
            w[name, x] = a[pre + "w" + x]
            if x in "qk":
                w[name, x + "r"] = a[pre + "w" + x][:, partner]
                c[name, "b" + x], c[name, "b" + x + "r"] = a[pre + "b" + x], a[pre + "b" + x][partner]
        c[name, "bv"], r[name, "bo"] = a[pre + "bv"], a[pre + "bo"]
    kv1 = a["L1_xattn_Wkv"]
    w["ca1", "q"], w["ca1", "k"], w["ca1", "v"], w["ca1", "o"] = (
        a["L1_xattn_Wq"].T, kv1[0:D].T, kv1[D:2 * D].T, a["L1_xattn_Wo"].T)
    r["ca1", "bo"] = a["L1_xattn_bo"]
    for name, win, bin_, wout, bout in (("ca2", "L2_xattn_in_proj_w", "L2_xattn_in_proj_b", "L2_xattn_out_w", "L2_xattn_out_b"),
                                        ("sa3", "L3_xattn_sa_in_w", "L3_xattn_sa_in_b", "L3_xattn_sa_out_w", "L3_xattn_sa_out_b"),
                                        ("ca3", "L3_xattn_ca_in_w", "L3_xattn_ca_in_b", "L3_xattn_ca_out_w", "L3_xattn_ca_out_b")):
        for x, part, bias in zip("qkv", split3(a[win]), split3(a[bin_])):
            w[name, x], c[name, "b" + x] = part.T, bias
        w[name, "o"], r[name, "bo"] = a[wout].T, a[bout]
    for name, pre in (("sa0", "L0_xattn_ln1_"), ("ca0", "L0_xattn_ln2_"), ("ff0", "L0_xattn_ln3_"), ("ca1", "L1_xattn_ln_q_"),
                      ("ctx1", "L1_xattn_ln_kv_"), ("sa3", "L3_xattn_sa_ln_"), ("ca3", "L3_xattn_ca_q_ln_"),
                      ("ctx3", "L3_xattn_ca_kv_ln_"), ("moe", "L3_xattn_moe_ln_")):
        c[name, "g"], c[name, "b"] = a[pre + "g"], a[pre + "b"]
    for name, b1, b2 in (("ff0", "L0_xattn_fc1_b", "L0_xattn_fc2_b"), ("ff1", "L1_xattn_b1", "L1_xattn_b2")):
        for i in range(CH):
            c[name, f"f{i}"] = a[b1][i * P:(i + 1) * P]
        r[name, "bo"] = a[b2]
    for e in range(EXPERTS):
        for i in range(CH):
            c["moe", f"f{e}_{i}"] = a["L3_xattn_e_fc1_b"][e, i * P:(i + 1) * P]
    r["ca2", "score"] = a["L2_xattn_score_w"][0]

    for name in {k[0] for k in w}:
        w[name, "o"] = w[name, "o"][by_slot_pair]
        if (name, "bv") in c:
            c[name, "bv"] = c[name, "bv"][by_slot_pair]

    def hidden_major(w2):
        return w2.reshape(CH, P, D).transpose(1, 0, 2).reshape(P, CH * D)

    mlp = np.stack([np.stack([a["L0_xattn_fc1_w"], hidden_major(a["L0_xattn_fc2_w"])], 1),
                    np.stack([a["L1_xattn_W1"].T, hidden_major(a["L1_xattn_W2"].T)], 1)], 1)
    arrays = {
        "x": a["x"].reshape(SEQS * SEQ, D),
        "ctx": a["ctx_1024"].reshape(SEQS * SEQ, D),
        "weights": np.stack([w[k][:, by_parity] if k[1] == "v" else w[k] for k in WEIGHTS], 1),
        "mlp_w": mlp,
        "moe_w1": a["L3_xattn_e_fc1_w"].transpose(2, 0, 1),
        "moe_w2": a["L3_xattn_e_fc2_w"].transpose(2, 0, 1).reshape(CH, P, EXPERTS, D).transpose(1, 2, 0, 3),
        "moe_b2": a["L3_xattn_e_fc2_b"],
        "router_w": a["L3_xattn_router_w"].T,
        "cols": np.stack([c[k] for k in COLS], 1),
        "rows": np.concatenate([r[k] for k in ROWS] + [a["L3_xattn_router_b"], a["L2_xattn_score_b"]])[None, :],
        "consts": shape_constants(),
    }
    nc = bacc.Bacc("TRN2", target_bir_lowering=False, num_devices=1)
    args = []
    feed = {}
    for name, array in arrays.items():
        feed[f"in_{name}"] = np.ascontiguousarray(array)
        args.append(nc.dram_tensor(f"in_{name}", array.shape, F32, kind="ExternalInput").ap())
    args.append(nc.dram_tensor("out", [SEQS * SEQ, D], F32, kind="ExternalOutput").ap())
    build(nc, *args)
    got = run_bass_kernel_spmd(nc, [feed], core_ids=[0])
    return got.results[0]["out"].reshape(SEQS, SEQ, D)
```
